# Optimizing a Trainium2 kernel written in Bass

```python
import numpy as np
import jax
import jax.numpy as jnp

def _softmax(x, axis=-1):
    return jax.nn.softmax(x, axis=axis)

def _gelu(x):
    return jax.nn.gelu(x, approximate=True)

def _silu(x):
    return jax.nn.silu(x)

def _sigmoid(x):
    return jax.nn.sigmoid(x)

def _layernorm(x, axis=-1, eps=1e-05):
    m = jnp.mean(x, axis=axis, keepdims=True)
    v = jnp.var(x, axis=axis, keepdims=True)
    return (x - m) / jnp.sqrt(v + eps)

def _scatter_add(tgt, idx, src, axis=0):
    return tgt.at[idx].add(src)

def _segment_sum(src, seg, n):
    return jax.ops.segment_sum(src, seg, n)
kernel_name = 'mk_audio_tower_d1_tok_audfeat768_r4_ad7947'

def setup_inputs(seed: int=0):
    np.random.seed(seed)
    _w = jnp.asarray

    def _rec_inputs():
        import jax
        import jax.numpy as jnp
        _rk = jax.random.key(seed)
        x = -0.000183583 + 0.999963 * jax.random.normal(jax.random.fold_in(_rk, 1), (32, 375, 192), jnp.float32)
        return x
    x = _rec_inputs()

    def _L0_tok_setup():
        import jax, jax.numpy as jnp
        import numpy as np
        KEEP_RATIO = 0.7
        LN_EPS = 1e-05
        key = jax.random.key(seed)
        k1, k2 = jax.random.split(key)
        B, N, D = (16, 2048, 192)
        x = jax.random.normal(k1, (B, N, D), dtype=jnp.float32)
        gamma = jnp.ones((D,), dtype=jnp.float32)
        beta = jnp.zeros((D,), dtype=jnp.float32)
        w = jax.random.normal(k2, (D,), dtype=jnp.float32) * (1.0 / np.sqrt(D))
        b = jnp.zeros((1,), dtype=jnp.float32)
        return {'x': x, 'gamma': gamma, 'beta': beta, 'w': w, 'b': b}
    _L0_tok_all = _L0_tok_setup()
    _L0_tok_in = {k: v for k, v in _L0_tok_all.items() if k in ('gamma', 'beta', 'w', 'b')}
    del _L0_tok_all

    def _L0_attn_setup():
        import jax, jax.numpy as jnp
        import numpy as np
        B, N, C, H = (8, 256, 192, 12)
        D = C // H
        SCALE = D ** (-0.5)
        key = jax.random.key(seed)
        ks = jax.random.split(key, 5)
        s = lambda k, sh, fan: jax.random.normal(k, sh, jnp.float32) * fan ** (-0.5)
        return {'x': jax.random.normal(ks[0], (B, N, C), jnp.float32), 'w_qkv': s(ks[1], (C, 3 * C), C), 'b_qkv': jnp.zeros((3 * C,), jnp.float32), 'w_l': s(ks[2], (H, H), H), 'b_l': jnp.zeros((H,), jnp.float32), 'w_w': s(ks[3], (H, H), H), 'b_w': jnp.zeros((H,), jnp.float32), 'w_proj': s(ks[4], (C, C), C), 'b_proj': jnp.zeros((C,), jnp.float32)}
    _L0_attn_all = _L0_attn_setup()
    _L0_attn_in = {k: v for k, v in _L0_attn_all.items() if k in ('w_qkv', 'b_qkv', 'w_l', 'b_l', 'w_w', 'b_w', 'w_proj', 'b_proj')}
    del _L0_attn_all

    def _L0_ffn_setup():
        import jax, jax.numpy as jnp
        import numpy as np
        B, T, D, E, K = (4, 512, 192, 8, 2)
        H = 4 * D
        key = jax.random.key(seed)
        k0, k1, k2, k3, k4 = jax.random.split(key, 5)
        s = 0.02
        return {'x': jax.random.normal(k0, (B, T, D), jnp.float32), 'router_w': jax.random.uniform(k1, (E, D), jnp.float32, -s * 0.1, s * 0.1), 'Wg': jax.random.uniform(k2, (E, H, D), jnp.float32, -s * 0.4, s * 0.4), 'Wu': jax.random.uniform(k3, (E, H, D), jnp.float32, -s * 0.4, s * 0.4), 'Wd': jax.random.normal(k4, (E, D, H), jnp.float32) * 0.01}
    _L0_ffn_all = _L0_ffn_setup()
    _L0_ffn_in = {k: v for k, v in _L0_ffn_all.items() if k in ('router_w', 'Wg', 'Wu', 'Wd')}
    del _L0_ffn_all
    return {'x': x, 'L0_tok_gamma': _L0_tok_in['gamma'], 'L0_tok_beta': _L0_tok_in['beta'], 'L0_tok_w': _L0_tok_in['w'], 'L0_tok_b': _L0_tok_in['b'], 'L0_attn_w_qkv': _L0_attn_in['w_qkv'], 'L0_attn_b_qkv': _L0_attn_in['b_qkv'], 'L0_attn_w_l': _L0_attn_in['w_l'], 'L0_attn_b_l': _L0_attn_in['b_l'], 'L0_attn_w_w': _L0_attn_in['w_w'], 'L0_attn_b_w': _L0_attn_in['b_w'], 'L0_attn_w_proj': _L0_attn_in['w_proj'], 'L0_attn_b_proj': _L0_attn_in['b_proj'], 'L0_ffn_router_w': _L0_ffn_in['router_w'], 'L0_ffn_Wg': _L0_ffn_in['Wg'], 'L0_ffn_Wu': _L0_ffn_in['Wu'], 'L0_ffn_Wd': _L0_ffn_in['Wd']}

def reference(x, L0_tok_gamma, L0_tok_beta, L0_tok_w, L0_tok_b, L0_attn_w_qkv, L0_attn_b_qkv, L0_attn_w_l, L0_attn_b_l, L0_attn_w_w, L0_attn_b_w, L0_attn_w_proj, L0_attn_b_proj, L0_ffn_router_w, L0_ffn_Wg, L0_ffn_Wu, L0_ffn_Wd):
    import jax
    import jax.numpy as jnp

    def _L0_tok_ref(x, gamma, beta, w, b):
        import jax, jax.numpy as jnp
        import numpy as np
        KEEP_RATIO = 0.7
        LN_EPS = 1e-05
        B, N, D = x.shape
        mu = jnp.mean(x, axis=-1, keepdims=True)
        var = jnp.mean(jnp.square(x - mu), axis=-1, keepdims=True)
        xn = (x - mu) * jax.lax.rsqrt(var + LN_EPS) * gamma + beta
        scores = jnp.einsum('bnd,d->bn', xn, w) + b[0]
        k = int(N * KEEP_RATIO)
        _, idx = jax.lax.top_k(scores, k)
        x_kept = jnp.take_along_axis(x, idx[..., None], axis=1)
        return x_kept

    def _L0_attn_ref(x, w_qkv, b_qkv, w_l, b_l, w_w, b_w, w_proj, b_proj):
        import jax, jax.numpy as jnp
        import numpy as np
        B, N, C, H = (8, 256, 192, 12)
        D = C // H
        SCALE = D ** (-0.5)
        Bq, Nq, Cq = x.shape
        qkv = (x @ w_qkv + b_qkv).reshape(Bq, Nq, 3, H, D).transpose(2, 0, 3, 1, 4)
        q, k, v = (qkv[0] * SCALE, qkv[1], qkv[2])
        attn = jnp.einsum('bhnd,bhmd->bhnm', q, k)
        attn = jnp.einsum('bhnm,hg->bgnm', attn, w_l) + b_l[None, :, None, None]
        attn = jax.nn.softmax(attn, axis=-1)
        attn = jnp.einsum('bhnm,hg->bgnm', attn, w_w) + b_w[None, :, None, None]
        out = jnp.einsum('bhnm,bhmd->bnhd', attn, v).reshape(Bq, Nq, Cq)
        return out @ w_proj + b_proj

    def _L0_ffn_ref(x, router_w, Wg, Wu, Wd):
        import jax, jax.numpy as jnp
        import numpy as np
        B, T, D, E, K = (4, 512, 192, 8, 2)
        H = 4 * D
        Bv, Tv, Dv = x.shape
        N = Bv * Tv
        xf = x.reshape(N, Dv)
        logits = (xf @ router_w.T).astype(jnp.float32)
        top_logits, top_idx = jax.lax.top_k(logits, K)
        top_w = jax.nn.softmax(top_logits, axis=-1).astype(x.dtype)
        out = jnp.zeros_like(xf)
        for e in range(E):
            w_e = jnp.sum(top_w * (top_idx == e), axis=-1)
            h = jax.nn.silu(xf @ Wg[e].T) * (xf @ Wu[e].T)
            out = out + h @ Wd[e].T * w_e[:, None]
        return out.reshape(Bv, Tv, Dv)
    h = _L0_tok_ref(x, L0_tok_gamma, L0_tok_beta, L0_tok_w, L0_tok_b)
    h = h + _L0_attn_ref(_layernorm(h, axis=-1), L0_attn_w_qkv, L0_attn_b_qkv, L0_attn_w_l, L0_attn_b_l, L0_attn_w_w, L0_attn_b_w, L0_attn_w_proj, L0_attn_b_proj)
    h = h + _L0_ffn_ref(_layernorm(h, axis=-1), L0_ffn_router_w, L0_ffn_Wg, L0_ffn_Wu, L0_ffn_Wd)
    return h

_drawn_inputs = setup_inputs


def setup_inputs(seed=0):
    import zlib

    import numpy as np

    out = dict(_drawn_inputs(seed))
    spreads = {'L0_tok_gamma': (1.0, 0.2),
     'L0_tok_beta': (0.0, 0.1),
     'L0_attn_b_qkv': (0.0, 0.1),
     'L0_attn_b_l': (0.0, 0.8),
     'L0_attn_b_w': (0.0, 0.1),
     'L0_attn_b_proj': (0.0, 0.1)}
    factors = {'L0_ffn_router_w': 8.0, 'L0_ffn_Wg': 8.0, 'L0_ffn_Wu': 8.0, 'L0_ffn_Wd': 8.0}
    for name, (base, spread) in spreads.items():
        noise = np.random.default_rng([zlib.crc32(name.encode()), seed]).standard_normal(out[name].shape)
        drawn = base * np.exp(spread * noise) if base else spread * noise
        out[name] = jnp.asarray(drawn.astype(out[name].dtype))
    for name, factor in factors.items():
        out[name] = (out[name] * factor).astype(out[name].dtype)
    return out
```

```python
import concourse.bass as bass
from concourse import mybir
from contextlib import ExitStack

F32 = mybir.dt.float32
U32 = mybir.dt.uint32
I32 = mybir.dt.int32
ALU = mybir.AluOpType
ACT = mybir.ActivationFunctionType
AX = mybir.AxisListType

B, N, C = 32, 375, 192
KEEP = int(N * 0.7)
H, D = 12, 16
E, F = 8, 768
EPS = 1e-5
SCALE = D ** -0.5

TPP = 3
NP = N // TPP
XW = C + 2
GROUPS = 4
BG = B // GROUPS

TILE = 88
SIZES = [TILE, TILE, KEEP - 2 * TILE]
CH = C // 2

ROWS = H * KEEP
RT = -(-ROWS // 128)
P_RING = 4
LAG = 3


def rows_of(r):
    return min(128, ROWS - 128 * r)


def last_tile(h):
    return (KEEP * (h + 1) - 1) // 128


def last_head(r):
    return (128 * r + rows_of(r) - 1) // KEEP


def before(r, ring):
    if r >= ring:
        return r - ring + 1
    return max(q for q in range(RT) if q % ring == r % ring) + 1 - RT


BL_PARTS = [(g, r, max(g * KEEP - 128 * r, 0), min((g + 1) * KEEP - 128 * r, 128))
            for g in range(H) for r in range(g * KEEP // 128, last_tile(g) + 1)]

T = B * KEEP
REGION = -(-T // 128) * 128
TILES = (2 * T + E * 127) // 128
TILES += TILES % 2
SLOTS = E * REGION + (TILES + 2) * 128
HF = F // 2
COLS = B * 3


def build(nc, x, gamma, beta, tok_w, tok_b, w_qkv, b_qkv, w_l, b_l, w_w, b_w, w_proj, b_proj,
          router_wT, WgT, WuT, WdT, out, xs, ids, h_rows, n_rows, y_rows):
    outer = ExitStack()
    with outer:
        outer.enter_context(nc.allow_non_contiguous_dma(reason="biases and slot numbers"))

        def sem(name):
            return outer.enter_context(nc.semaphore(name))

        def alloc(ctx, name, shape, dt=F32):
            return ctx.enter_context(nc.sbuf_tensor(name, shape, dt))

        def sb(name, shape, dt=F32):
            return alloc(outer, name, shape, dt)

        bank = [outer.enter_context(nc.psum_tensor(f"bank{i}", [128, 512], F32)) for i in range(8)]

        ident = sb("ident", [128, 128])
        ones = sb("ones", [128, 128])
        upper = sb("upper", [TILE, TILE])
        iota8 = sb("iota8", [TILE, 3, E])
        valid = sb("valid", [TILE, 3, E])
        w1_all = sb("w1_all", [TILE, COLS])
        w2_all = sb("w2_all", [TILE, COLS])
        slot_all = sb("slot_all", [TILE, COLS, 2])
        run = sb("run", [TILE, E])
        tile_e = sb("tile_e", [1, TILES + 2], I32)
        tile_at = sb("tile_at", [1, TILES + 2], I32)

        sel = ExitStack()
        xe = alloc(sel, "xe", [NP, B * TPP * XW])
        xe4 = xe[:].rearrange("p (b t w) -> p b t w", b=B, t=TPP)
        gw = alloc(sel, "gw", [NP, C])
        gtmp = alloc(sel, "gtmp", [NP, 2, C])
        c0 = alloc(sel, "c0", [NP, 1])
        c1 = alloc(sel, "c1", [NP, 1])
        tb = alloc(sel, "tb", [NP, 1])
        stats = alloc(sel, "stats", [NP, TPP, 6])
        mv = alloc(sel, "mv", [NP, TPP, 2])
        junk = alloc(sel, "junk", [NP, 2 * TPP, N])
        dots = alloc(sel, "dots", [NP, TPP])
        score = alloc(sel, "score", [NP, B * TPP])
        var = alloc(sel, "var", [NP, B * TPP])
        r0 = alloc(sel, "r0", [NP, B * TPP])
        rr = alloc(sel, "rr", [NP, B * TPP])
        earlier = alloc(sel, "earlier", [NP, TPP, N])
        row0 = alloc(sel, "row0", [NP, B])
        sc_cur = alloc(sel, "sc_cur", [NP, 2, TPP])
        sc_wide = alloc(sel, "sc_wide", [NP, 2, TPP, NP])
        x_out = alloc(sel, "x_out", [NP, 2, TPP, XW])
        above = alloc(sel, "above", [NP, 2, TPP])
        equal = alloc(sel, "equal", [NP, 2, TPP])
        place = alloc(sel, "place", [NP, 2, TPP], U32)
        sel.close()

        att = ExitStack()
        wq = alloc(att, "wq", [CH, 2, 3 * C])
        bqk = alloc(att, "bqk", [CH, 4])
        bv = alloc(att, "bv", [TILE, C])
        wl = alloc(att, "wl", [CH, 2, H])
        bl = alloc(att, "bl", [128, RT])
        ww = alloc(att, "ww", [TILE, H, H, D])
        wwt = alloc(att, "wwt", [TILE, H * H])
        bw = alloc(att, "bw", [CH, 2])
        wp = alloc(att, "wp", [CH, 2, C])
        bp = alloc(att, "bp", [TILE, C])
        rw = alloc(att, "rw", [CH, 2, E])
        half = alloc(att, "half", [TILE, 3])
        x_in = alloc(att, "x_in", [TILE, 3, XW])
        hn = alloc(att, "hn", [TILE, 3, C])
        hnT = alloc(att, "hnT", [CH, 2, KEEP])
        qs = alloc(att, "qs", [CH, 2, KEEP])
        kT = alloc(att, "kT", [CH, 2, KEEP])
        v = alloc(att, "v", [TILE, 3, C])
        vb_next = alloc(att, "vb_next", [CH, 2])
        vb = alloc(att, "vb", [CH, 2])
        qh = alloc(att, "qh", [CH, 2, ROWS])
        vh = alloc(att, "vh", [TILE, H, 3, C])
        nmax = alloc(att, "nmax", [128, RT])
        nbias = alloc(att, "nbias", [128, RT])
        zsum = alloc(att, "zsum", [128, RT])
        rz = alloc(att, "rz", [128, RT])
        prob = alloc(att, "prob", [128, P_RING, KEEP])
        pT = alloc(att, "pT", [TILE, 3, ROWS])
        oT = alloc(att, "oT", [CH, 2, KEEP])
        x_res = alloc(att, "x_res", [TILE, 3, C])
        hres = alloc(att, "hres", [TILE, 3, C])
        n2 = alloc(att, "n2", [TILE, 3, C])
        n2T = alloc(att, "n2T", [CH, 2, KEEP])
        st2 = alloc(att, "st2", [TILE, 3, 6])
        mv2 = alloc(att, "mv2", [TILE, 3, 2])
        ve = alloc(att, "ve", [TILE, 3])
        ra = alloc(att, "ra", [TILE, 3])
        rb = alloc(att, "rb", [TILE, 3])
        lg = alloc(att, "lg", [TILE, 3, E])
        mx = alloc(att, "mx", [TILE, 3, 8])
        ix = alloc(att, "ix", [TILE, 3, 8], U32)
        ixf = alloc(att, "ixf", [TILE, 3, 2])
        oh = alloc(att, "oh", [TILE, 2, 3, E])
        ohs = alloc(att, "ohs", [TILE, 3, E])
        dl = alloc(att, "dl", [TILE, 3])
        ed = alloc(att, "ed", [TILE, 3])
        ed1 = alloc(att, "ed1", [TILE, 3])
        wa = alloc(att, "wa", [TILE, 3])
        pos = alloc(att, "pos", [TILE, 3, E])
        posm = alloc(att, "posm", [TILE, 2, 3, E])
        slots = alloc(att, "slots", [TILE, 3, 2])
        slot_u = alloc(att, "slot_u", [TILE, 2, 3], U32)
        idc = alloc(att, "idc", [TILE, 3])
        id_u = alloc(att, "id_u", [TILE, 3], U32)
        zero_ids = alloc(att, "zero_ids", [128, SLOTS // 128], U32)
        att.close()

        ffn = ExitStack()
        wg = alloc(ffn, "wg", [CH, 2 * E * F])
        wu = alloc(ffn, "wu", [CH, 2 * E * F])
        wd = alloc(ffn, "wd", [128, E * (F // 128) * C])
        id_in = alloc(ffn, "id_in", [128, 2], U32)
        xg = alloc(ffn, "xg", [128, 2, C])
        xgT = alloc(ffn, "xgT", [CH, 2, 2, 128])
        sg = alloc(ffn, "sg", [128, F])
        hh = alloc(ffn, "hh", [128, 2, F])
        hT = alloc(ffn, "hT", [128, F // 128, 128])
        yo = alloc(ffn, "yo", [128, 2, C])
        cnt = alloc(ffn, "cnt", [TILE, E])
        cnti = alloc(ffn, "cnti", [TILE, E], I32)
        slot_ge = alloc(ffn, "slot_ge", [TILE, E - 1, 2 * COLS])
        cntf = alloc(ffn, "cntf", [TILE, E])
        jump = alloc(ffn, "jump", [TILE, E])
        upto = alloc(ffn, "upto", [TILE, E])
        tix = alloc(ffn, "tix", [1, TILES + 2])
        ge = alloc(ffn, "ge", [1, E, TILES + 2])
        te = alloc(ffn, "te", [1, TILES + 2])
        ta = alloc(ffn, "ta", [1, TILES + 2])
        base8 = alloc(ffn, "base8", [TILE, E])
        sl_cur = alloc(ffn, "sl_cur", [TILE, 2, 3], U32)
        y1 = alloc(ffn, "y1", [TILE, 3, C])
        y2 = alloc(ffn, "y2", [TILE, 3, C])
        hc = alloc(ffn, "hc", [TILE, 3, C])
        oa = alloc(ffn, "oa", [TILE, 3, C])
        oc = alloc(ffn, "oc", [TILE, 3, C])
        ffn.close()

        dve_passed, pool_passed = sem("dve_passed"), sem("pool_passed")
        pool_c = sem("pool_c")
        consts_ready = sem("consts_ready")
        x_loaded = [sem(f"x_loaded{g}") for g in range(GROUPS)]
        tokp_loaded = sem("tokp_loaded")
        dve_prep = sem("dve_prep")
        dve_stat = sem("dve_stat")
        var_ready, sqrt_ready, score_ready = sem("var_ready"), sem("sqrt_ready"), sem("score_ready")
        wide_ready, rows_ready, rows_used = sem("wide_ready"), sem("rows_ready"), sem("rows_used")
        xout_ready, place_ready = sem("xout_ready"), sem("place_ready")
        scattered = [sem(f"scattered{i}") for i in range(2)]
        dve_rank = sem("dve_rank")
        w_loaded, ww_loaded = sem("w_loaded"), sem("ww_loaded")
        bl_loaded = sem("bl_loaded")
        prep_ready = sem("prep_ready")
        x_in_loaded, x_in_used = sem("x_in_loaded"), sem("x_in_used")
        x_res_loaded, x_res_ready = sem("x_res_loaded"), sem("x_res_ready")
        hn_ready, hnT_psum, hnT_ready = sem("hn_ready"), sem("hnT_psum"), sem("hnT_ready")
        q_psum, qs_ready, k_psum, kT_ready = sem("q_psum"), sem("qs_ready"), sem("k_psum"), sem("kT_ready")
        v_psum, v_ready, vb_psum, vb_ready = sem("v_psum"), sem("v_ready"), sem("vb_psum"), sem("vb_ready")
        vb_kept = sem("vb_kept")
        qh_ready, vh_ready = sem("qh_ready"), sem("vh_ready")
        s_psum, max_done, bias_ready = sem("s_psum"), sem("max_done"), sem("bias_ready")
        exp_done, rz_done, prob_ready = sem("exp_done"), sem("rz_done"), sem("prob_ready")
        t_psum, pT_ready, av_done, oT_ready = sem("t_psum"), sem("pT_ready"), sem("av_done"), sem("oT_ready")
        proj_psum, hres_ready, n2_ready = sem("proj_psum"), sem("hres_ready"), sem("n2_ready")
        ve_ready, pow_ready = sem("ve_ready"), sem("pow_ready")
        n2T_psum, n2T_ready, router_psum, lg_ready = sem("n2T_psum"), sem("n2T_ready"), sem("router_psum"), sem("lg_ready")
        oh_ready, pos_psum, pos_used = sem("oh_ready"), sem("pos_psum"), sem("pos_used")
        dl_ready, ed_ready = sem("dl_ready"), sem("ed_ready")
        slots_ready, ids_sent = sem("slots_ready"), sem("ids_sent")
        ids_zeroed, ids_free = sem("ids_zeroed"), sem("ids_free")
        dve_post, dve_route, dve_slot = sem("dve_post"), sem("dve_route"), sem("dve_slot")
        h_stored, n_stored = sem("h_stored"), sem("n_stored")
        att_over = sem("att_over")
        fw_loaded = sem("fw_loaded")
        tab_ready = sem("tab_ready")
        dve_tab = sem("dve_tab")
        id_loaded = [sem(f"id_loaded{i}") for i in range(2)]
        xg_loaded = [sem(f"xg_loaded{i}") for i in range(2)]
        xgT_psum, xgT_ready = sem("xgT_psum"), sem("xgT_ready")
        gu_psum, silu_done, hh_ready = sem("gu_psum"), sem("silu_done"), sem("hh_ready")
        hT_psum, hT_ready, y_psum, y_ready = sem("hT_psum"), sem("hT_ready"), sem("y_psum"), sem("y_ready")
        y_stored = [sem(f"y_stored{i}") for i in range(2)]
        slc_ready = sem("slc_ready")
        y_gathered = [sem(f"y_gathered{i}") for i in range(3)]
        hc_loaded, comb_step, comb_done, out_stored = sem("hc_loaded"), sem("comb_step"), sem("comb_done"), sem("out_stored")

        block = outer.enter_context(nc.Block())

        class Chain:

            def __init__(self, eng, signal, per):
                self.eng, self.sem, self.per, self.n, self.base = eng, signal, per, 0, 0

            def start(self, n):
                self.base, self.n = n * self.per, 0

            def mark(self, ins):
                self.n += 1
                ins.then_inc(self.sem, 1)

            def sync(self, apart=None):
                if apart is not None:
                    wait_apart(self.eng, self.sem, self.base + self.n, apart)
                else:
                    self.eng.wait_ge(self.sem, self.base + self.n)

            def link(self, ins):
                self.mark(ins)
                self.sync()

            def end(self):
                assert self.n == self.per, (self.n, self.per)

        def wait_apart(eng, signal, value, passed):
            eng.wait_ge(signal, value)
            eng.sem_inc(passed, 1)

        def wait(eng, signal, value):
            if not isinstance(value, int) or value > 0:
                eng.wait_ge(signal, value)

        def batches(eng, body, edge):
            body(0, False, True)
            with eng.Fori(1, B - 1) as b:
                body(b, True, True)
            body(B - 1, True, False)
            edge()

        def tok_rows(b, t):
            return bass.ds(b * KEEP + TILE * t, SIZES[t])

        PROJ, N2T, ROUTE, POS, HNT, QQ, VV, VB = 2, 7, 10, 13, 15, 17, 18, 20

        @block.sync
        def _(sp):
            sp.sem_inc(h_stored, 32)
            sp.sem_inc(n_stored, 32)
            for s in range(2):
                sp.sem_inc(y_stored[s], 16)
            xv = x.rearrange("b (p t) c -> p b t c", t=TPP)
            for g in range(GROUPS):
                for b in range(g * BG, g * BG + BG):
                    sp.dma_start(xe4[:, b, :, 0:C], xv[:, b]).then_inc(x_loaded[g], 16)
            for s in range(2):
                sp.wait_ge(scattered[s], 16 * TPP * (B // 2))
            for dst, src in ((wq[:], w_qkv.rearrange("(j p) n -> p j n", p=CH)),
                             (wp[:], w_proj.rearrange("(j p) n -> p j n", p=CH)),
                             (rw[:], router_wT.rearrange("(j p) n -> p j n", p=CH)),
                             (bqk[:], b_qkv[0:2 * C].rearrange("(j p) -> p j", p=CH)),
                             (bv[:], b_qkv[2 * C:3 * C].partition_broadcast(TILE)),
                             (bp[:], b_proj.partition_broadcast(TILE)),
                             (wwt[:], w_w.rearrange("a b -> (a b)").partition_broadcast(TILE)),
                             ):
                sp.dma_start(dst, src).then_inc(w_loaded, 16)
            heads = CH // D
            for j in range(2):
                for g in range(heads):
                    hd = j * heads + g
                    sp.dma_start(wl[g * D:(g + 1) * D, j, :], w_l[hd].partition_broadcast(D)).then_inc(w_loaded, 16)
                    sp.dma_start(bw[g * D:(g + 1) * D, j:j + 1], b_w[hd:hd + 1].partition_broadcast(D)).then_inc(w_loaded, 16)
            for g, r, lo, hi in BL_PARTS:
                sp.dma_start(bl[lo:hi, r:r + 1], b_l[g:g + 1].partition_broadcast(hi - lo)).then_inc(bl_loaded, 16)
            wait(sp, prep_ready, 1)
            sp.dma_start(ids.rearrange("(p n) o -> p (n o)", p=128), zero_ids[:]).then_inc(ids_zeroed, 16)

            def load_x(b):
                sp.dma_start(x_in[:, 0:2, :], xs[bass.ds(b * N, 2 * TILE), :].rearrange("(t p) w -> p t w", p=TILE)).then_inc(x_in_loaded, 16)
                sp.dma_start(x_in[0:SIZES[2], 2, :], xs[bass.ds(b * N + 2 * TILE, SIZES[2]), :]).then_inc(x_in_loaded, 16)

            def load_res(b):
                sp.dma_start(x_res[:, 0:2, :], xs[bass.ds(b * N, 2 * TILE), 0:C].rearrange("(t p) w -> p t w", p=TILE)).then_inc(x_res_loaded, 16)
                sp.dma_start(x_res[0:SIZES[2], 2, :], xs[bass.ds(b * N + 2 * TILE, SIZES[2]), 0:C]).then_inc(x_res_loaded, 16)

            def store(b):
                sp.wait_ge(hres_ready, b + 1)
                sp.dma_start(h_rows[bass.ds(b * KEEP, 2 * TILE), :].rearrange("(t p) w -> p t w", p=TILE), hres[:, 0:2, :]).then_inc(h_stored, 16)
                sp.dma_start(h_rows[tok_rows(b, 2), :], hres[0:SIZES[2], 2, :]).then_inc(h_stored, 16)
                sp.wait_ge(n2_ready, b + 1)
                sp.dma_start(n_rows[bass.ds(b * KEEP, 2 * TILE), :].rearrange("(t p) w -> p t w", p=TILE), n2[:, 0:2, :]).then_inc(n_stored, 16)
                sp.dma_start(n_rows[tok_rows(b, 2), :], n2[0:SIZES[2], 2, :]).then_inc(n_stored, 16)

            load_x(0)

            def body(b, post, pre):
                if pre:
                    sp.wait_ge(x_in_used, b + 1)
                    load_x(b + 1)
                if post:
                    store(b - 1)
                load_res(b)

            batches(sp, body, lambda: store(B - 1))

            sp.wait_ge(att_over, 4)
            sp.wait_ge(n_stored, 32 * B + 32)
            sp.wait_ge(h_stored, 32 * B + 32)
            sp.dma_start(wg[:], WgT.rearrange("p k n -> p (k n)")).then_inc(fw_loaded, 16)
            sp.dma_start(wu[:], WuT.rearrange("p k n -> p (k n)")).then_inc(fw_loaded, 16)
            sp.dma_start(wd[:], WdT).then_inc(fw_loaded, 16)
            sp.wait_ge(tab_ready, 1)
            sp.wait_ge(ids_sent, 16 * 6 * B)

            def load_ids(i, s):
                at = sp.value_load(tile_at[0:1, bass.ds(i, 1)], min_val=0, max_val=SLOTS - 128)
                sp.dma_start(id_in[:, s:s + 1], ids[bass.ds(at, 128), :]).then_inc(id_loaded[s], 16)

            def store_y(i, s, n):
                sp.wait_ge(y_ready, i + 1)
                sp.dma_start(y_rows[bass.ds(i * 128, 128), :], yo[:, s, :]).then_inc(y_stored[s], 16)

            load_ids(0, 0)
            load_ids(1, 1)
            for s in range(2):
                sp.wait_ge(xg_loaded[s], 16)
                load_ids(2 + s, s)
            with sp.Fori(1, TILES // 2) as n:
                for s in range(2):
                    store_y(2 * n + s - 2, s, n)
                    if True:
                        sp.wait_ge(xg_loaded[s], 16 * n + 16)
                        load_ids_at = 2 * n + s + 2
                        load_ids(load_ids_at, s)
            for s in range(2):
                store_y(TILES - 2 + s, s, TILES // 2)

            for s in range(2):
                sp.wait_ge(y_stored[s], 16 * (TILES // 2) + 16)

            def comb(b, first):
                if not first:
                    sp.wait_ge(comb_done, 3 * b)
                for t in range(3):
                    sp.dma_start(hc[0:SIZES[t], t, :], h_rows[tok_rows(b, t), :]).then_inc(hc_loaded, 16)
                sp.wait_ge(comb_done, 3 * b + 3)
                for t in range(3):
                    sp.dma_start(out[tok_rows(b, t), :], oc[0:SIZES[t], t, :]).then_inc(out_stored, 16)

            comb(0, True)
            with sp.Fori(1, B) as b:
                comb(b, False)
            sp.wait_ge(out_stored, 16 * COLS)

        @block.gpsimd
        def _(pool):
            ch = Chain(pool, pool_c, 0)
            ch.link(pool.memset(ident[:], 0.0))
            ch.link(pool.affine_select(out=ident[:], in_=ident[:], compare_op=ALU.not_equal, fill=1.0, base=0,
                                       pattern=[[-1, 128]], channel_multiplier=1))
            ch.link(pool.memset(ones[:], 1.0))
            ch.link(pool.affine_select(out=upper[:], in_=ones[0:TILE, 0:TILE], compare_op=ALU.is_gt, fill=0.0,
                                       base=0, pattern=[[1, TILE]], channel_multiplier=-1))
            ch.link(pool.iota(iota8[:], pattern=[[0, 3], [1, E]], base=0, channel_multiplier=0,
                              allow_small_or_imprecise_dtypes=True))
            ch.link(pool.memset(valid[:], 1.0))
            ch.link(pool.affine_select(out=valid[:], in_=valid[:], compare_op=ALU.is_gt, fill=0.0, base=KEEP,
                                       pattern=[[-TILE, 3], [0, E]], channel_multiplier=-1))
            ch.link(pool.iota(run[:], pattern=[[REGION, E]], base=0, channel_multiplier=0,
                              allow_small_or_imprecise_dtypes=True))
            ch.link(pool.memset(earlier[:], 1.0))
            for t in range(TPP):
                ch.link(pool.affine_select(out=earlier[:, t, :].rearrange("p (a q) -> p a q", a=TPP),
                                           in_=earlier[:, t, :].rearrange("p (a q) -> p a q", a=TPP),
                                           compare_op=ALU.is_gt, fill=0.0, base=t,
                                           pattern=[[-1, TPP], [-TPP, NP]], channel_multiplier=TPP))
            ch.link(pool.iota(row0[:], pattern=[[N, B]], base=0, channel_multiplier=0,
                              allow_small_or_imprecise_dtypes=True))
            pool.sem_inc(consts_ready, 1)
            for dst, src in ((gtmp[:, 0], gamma), (gtmp[:, 1], beta), (gw[:], tok_w), (tb[:], tok_b)):
                pool.dma_start(dst, src.partition_broadcast(NP)).then_inc(tokp_loaded, 16)

            with pool.Fori(0, B // 2) as i:
                for s in range(2):
                    pool.wait_ge(place_ready, 2 * i + s + 1)
                    wait_apart(pool, xout_ready, 2 * i + s + 1, pool_passed)
                    for t in range(TPP):
                        pool.indirect_dma_start(out=xs, out_offset=bass.IndirectOffsetOnAxis(ap=place[:, s, t:t + 1], axis=0),
                                                in_=x_out[:, s, t, :], in_offset=None).then_inc(scattered[s], 16)
            for s in range(2):
                pool.wait_ge(scattered[s], 16 * TPP * (B // 2))
            ch.link(pool.memset(half[:], -0.5))
            ch.link(pool.memset(zero_ids[:], 0))
            ch.link(pool.memset(hres[:], 0.0))
            ch.link(pool.memset(n2[:], 0.0))
            ch.link(pool.memset(lg[:], 0.0))
            ch.link(pool.iota(idc[:], pattern=[[TILE, 3]], base=0, channel_multiplier=1,
                              allow_small_or_imprecise_dtypes=True))
            pool.sem_inc(prep_ready, 1)

            def v_heads(b, done_before):
                pool.wait_ge(v_ready, b + 1)
                for h in range(H):
                    if done_before:
                        pool.wait_ge(av_done, (b - 1) * H + h + 1)
                    for t in range(3):
                        n = SIZES[t]
                        ins = pool.tensor_tensor(vh[0:n, h, t, :], v[0:n, t, :],
                                                 ww[0:n, h].rearrange("p g d -> p (g d)"), ALU.mult)
                    ins.then_inc(vh_ready, 1)

            def residual(b):
                pool.wait_ge(x_res_loaded, 32 * b + 32)
                for t in range(3):
                    n = SIZES[t]
                    ins = pool.tensor_tensor(x_res[0:n, t, :], x_res[0:n, t, :], bp[0:n, :], ALU.add)
                ins.then_inc(x_res_ready, 1)

            def inv_std(b):
                pool.wait_ge(ve_ready, b + 1)
                pool.tensor_tensor(ra[:], ve[:], half[:], ALU.pow).then_inc(pow_ready, 1)

            def send_ids(b):
                wait_apart(pool, slots_ready, b + 1, pool_passed)
                for t in range(3):
                    n = SIZES[t]
                    for k in range(2):
                        pool.indirect_dma_start(out=ids, out_offset=bass.IndirectOffsetOnAxis(ap=slot_u[0:n, k, t:t + 1], axis=0),
                                                in_=id_u[0:n, t:t + 1], in_offset=None).then_inc(ids_sent, 16)

            def body(b, post, pre):
                if post:
                    inv_std(b - 1)
                    send_ids(b - 1)
                if b is not None:
                    residual(b)
                if post:
                    pool.wait_ge(ids_sent, 16 * 6 * b)
                    pool.sem_inc(ids_free, 1)
                if pre:
                    v_heads(b + 1, True)

            wait(pool, prep_ready, 2)
            pool.wait_ge(ids_zeroed, 16)
            pool.sem_inc(ids_free, 1)
            v_heads(0, False)

            def edge():
                inv_std(B - 1)
                send_ids(B - 1)

            batches(pool, body, edge)
            pool.wait_ge(ids_sent, 16 * 6 * B)
            pool.sem_inc(att_over, 1)
            pool.wait_ge(att_over, 4)

            ch.link(pool.iota(tix[:], pattern=[[1, TILES + 2]], base=0, channel_multiplier=0,
                              allow_small_or_imprecise_dtypes=True))
            ch.link(pool.iota(base8[:], pattern=[[REGION, E]], base=0, channel_multiplier=0,
                              allow_small_or_imprecise_dtypes=True))
            pool.sem_inc(tab_ready, 1) if False else None
            pool.sem_inc(prep_ready, 1)

            def gather(i, s, n):
                pool.wait_ge(id_loaded[s], 16 * n + 16)
                if not isinstance(i, int):
                    wait_apart(pool, xgT_psum, i - 1, pool_passed)
                pool.indirect_dma_start(out=xg[:, s, :], out_offset=None, in_=n_rows,
                                        in_offset=bass.IndirectOffsetOnAxis(ap=id_in[:, s:s + 1], axis=0)).then_inc(xg_loaded[s], 16)

            pool.wait_ge(n_stored, 32 * B + 32)
            for s in range(2):
                gather(s, s, 0)
            with pool.Fori(1, TILES // 2 + 1) as n:
                for s in range(2):
                    gather(2 * n + s, s, n)

            def comb(b):
                wait_apart(pool, slc_ready, b + 1, pool_passed)
                for t in range(3):
                    n = SIZES[t]
                    for k, y in enumerate((y1, y2)):
                        pool.indirect_dma_start(out=y[0:n, t, :], out_offset=None, in_=y_rows,
                                                in_offset=bass.IndirectOffsetOnAxis(ap=sl_cur[0:n, k, t:t + 1], axis=0)).then_inc(y_gathered[t], 16)

            for s in range(2):
                pool.wait_ge(y_stored[s], 16 * (TILES // 2) + 16)
            with pool.Fori(0, B) as b:
                comb(b)

        @block.scalar
        def _(act):
            act.wait_ge(var_ready, 1)
            nc.scalar.activation(r0[:], var[:], ACT.Sqrt).then_inc(sqrt_ready, 1)
            act.wait_ge(score_ready, 1)

            def spread(i, first=False):
                for s in range(2):
                    b = 2 * i + s
                    act.wait_ge(rows_ready, b + 1)
                    src = score[:, bass.ds(b * TPP, TPP)].unsqueeze(2).to_broadcast([NP, TPP, NP])
                    nc.scalar.activation(sc_wide[:, s], src, ACT.Copy).then_inc(wide_ready, 1)
                    if not first:
                        act.wait_ge(scattered[s], 16 * TPP * i)
                    nc.scalar.activation(x_out[:, s].rearrange("p t w -> p (t w)"), xe[:, bass.ds(b * TPP * XW, TPP * XW)],
                                         ACT.Copy).then_inc(xout_ready, 1)

            spread(0, True)
            with act.Fori(1, B // 2) as i:
                spread(i)
            wait(act, prep_ready, 2)

            def hnT_out(b):
                act.wait_ge(hnT_psum, b + 1)
                for j in range(2):
                    ins = nc.scalar.activation(hnT[:, j, :], bank[6 + j][0:CH, 0:KEEP], ACT.Copy)
                ins.then_inc(hnT_ready, 1)

            def n2T_out(b):
                act.wait_ge(n2T_psum, b + 1)
                for j in range(2):
                    ins = nc.scalar.activation(n2T[:, j, :], bank[6 + j][0:CH, 0:KEEP], ACT.Copy)
                ins.then_inc(n2T_ready, 1)

            def q_head(b, g):
                for j in range(2):
                    ins = nc.scalar.activation(qh[:, j, g * KEEP:(g + 1) * KEEP], qs[:, j, :], ACT.Copy,
                                               scale=wl[:, j, g:g + 1])
                ins.then_inc(qh_ready, 1)

            def exp_out(b, r):
                n = rows_of(r)
                act.wait_ge(bias_ready, b * RT + r + 1)
                wait(act, t_psum, b * RT + before(r, P_RING))
                nc.scalar.activation(prob[0:n, r % P_RING, :], bank[r % 2][0:n, 0:KEEP], ACT.Exp,
                                     bias=nbias[0:n, r:r + 1], accum_out=zsum[0:n, r:r + 1]).then_inc(exp_done, 1)

            def soft2(b):
                act.wait_ge(dl_ready, b + 1)
                nc.scalar.activation(ed[:], dl[:], ACT.Exp).then_inc(ed_ready, 1)

            def body(b, post, pre):
                for r in range(RT):
                    exp_out(b, r)
                    if post and r == N2T + 1:
                        n2T_out(b - 1)
                    if post and r == ROUTE + 1:
                        soft2(b - 1)
                    if pre and r == HNT + 1:
                        hnT_out(b + 1)
                    if pre and r == QQ + 2:
                        act.wait_ge(qs_ready, b + 2)
                    if pre and r >= QQ + 2:
                        for g in (2 * (r - QQ - 2), 2 * (r - QQ - 2) + 1):
                            if g < H and last_tile(g) <= r - 1:
                                act.wait_ge(s_psum, b * RT + last_tile(g) + 1)
                                q_head(b + 1, g)
                                sent[0] = g + 1
                if pre:
                    for g in range(sent[0], H):
                        act.wait_ge(s_psum, b * RT + last_tile(g) + 1)
                        q_head(b + 1, g)

            sent = [0]
            hnT_out(0)
            act.wait_ge(qs_ready, 1)
            for g in range(H):
                q_head(0, g)

            def edge():
                n2T_out(B - 1)
                soft2(B - 1)

            batches(act, body, edge)
            act.wait_ge(n2T_ready, B)
            act.sem_inc(att_over, 1)
            act.wait_ge(att_over, 4)

            def gate(i, s):
                for k in range(2):
                    act.wait_ge(gu_psum, 2 * i + k + 1)
                    wait(act, hh_ready, 2 * i + k - 1)
                    nc.scalar.activation(sg[:, k * HF:(k + 1) * HF], bank[2 * k][:, 0:HF], ACT.Silu).then_inc(silu_done, 1)

            def hT_out(i):
                act.wait_ge(hT_psum, i + 1)
                wait(act, y_psum, i)
                for k in range(2):
                    ins = nc.scalar.activation(hT[:, 3 * k:3 * k + 3, :], bank[4 + k][:, 0:384].rearrange("p (a q) -> p a q", a=3),
                                               ACT.Copy)
                ins.then_inc(hT_ready, 1)

            def pair(n, first):
                for s in range(2):
                    i = 2 * n + s
                    if not (first and s == 0):
                        hT_out(i - 1)
                    gate(i, s)

            pair(0, True)
            with act.Fori(1, TILES // 2) as n:
                pair(n, False)
            hT_out(TILES - 1)

        @block.tensor
        def _(pe):
            pe.sem_inc(rows_ready, 2)
            pe.wait_ge(consts_ready, 1)
            with pe.Fori(0, B // 2) as i:
                for s in range(2):
                    b = 2 * i + s
                    pe.wait_ge(wide_ready, b + 1)
                    pe.wait_ge(rows_used, b + 1)
                    for t in range(TPP):
                        ins = pe.transpose(bank[s][0:NP, t * NP:(t + 1) * NP], sc_wide[:, s, t, :], ident[0:NP, 0:NP])
                    ins.then_inc(rows_ready, 1)

            def hnT_in(b):
                pe.wait_ge(hn_ready, b + 1)
                for j in range(2):
                    for t in range(3):
                        n = SIZES[t]
                        ins = pe.transpose(bank[6 + j][0:CH, TILE * t:TILE * t + n], hn[0:n, t, j * CH:(j + 1) * CH], ident[0:n, 0:n])
                ins.then_inc(hnT_psum, 1)

            def qk_in(b, which, signal):
                for c in range(2):
                    for k in range(2):
                        ins = pe.matmul(bank[6 + c][0:CH, 0:KEEP], wq[:, k, which * C + c * CH:which * C + (c + 1) * CH], hnT[:, k, :],
                                        start=(k == 0), stop=(k == 1))
                ins.then_inc(signal, 1)

            def v_in(b):
                for t in range(3):
                    n = SIZES[t]
                    dst = bank[6 + t // 2][0:n, (t % 2) * C:(t % 2) * C + C]
                    for k in range(2):
                        ins = pe.matmul(dst, hnT[:, k, TILE * t:TILE * t + n], wq[:, k, 2 * C:3 * C], start=(k == 0), stop=(k == 1))
                ins.then_inc(v_psum, 1)

            def vb_in(b):
                pe.wait_ge(v_ready, b + 1)
                for j in range(2):
                    for t in range(3):
                        n = SIZES[t]
                        ins = pe.matmul(bank[6][0:CH, j:j + 1], v[0:n, t, j * CH:(j + 1) * CH], ones[0:n, 0:1],
                                        start=(t == 0), stop=(t == 2))
                ins.then_inc(vb_psum, 1)

            def scores(b, r):
                n = rows_of(r)
                if r == 0:
                    pe.wait_ge(kT_ready, b + 1)
                pe.wait_ge(qh_ready, b * H + last_head(r) + 1)
                wait(pe, exp_done, b * RT + before(r, 2))
                for k in range(2):
                    ins = pe.matmul(bank[r % 2][0:n, 0:KEEP], qh[:, k, 128 * r:128 * r + n], kT[:, k, :], start=(k == 0), stop=(k == 1))
                ins.then_inc(s_psum, 1)

            def turn(b, r):
                n = rows_of(r)
                pe.wait_ge(prob_ready, b * RT + r + 1)
                wait(pe, pT_ready, b * RT + before(r, 2))
                for t in range(3):
                    m = SIZES[t]
                    ins = pe.transpose(bank[2 + r % 2][0:m, 128 * t:128 * t + n], prob[0:n, r % P_RING, TILE * t:TILE * t + m], ident[0:n, 0:n])
                ins.then_inc(t_psum, 1)

            def av(b, h):
                pe.wait_ge(pT_ready, b * RT + last_tile(h) + 1)
                pe.wait_ge(vh_ready, b * H + h + 1)
                if h == 0:
                    wait(pe, oT_ready, b)
                for j in range(2):
                    for t in range(3):
                        m = SIZES[t]
                        ins = pe.matmul(bank[4 + j][0:CH, 0:KEEP], vh[0:m, h, t, j * CH:(j + 1) * CH], pT[0:m, t, h * KEEP:(h + 1) * KEEP],
                                        start=(h == 0 and t == 0), stop=(h == H - 1 and t == 2))
                ins.then_inc(av_done, 1)

            def proj(b):
                pe.wait_ge(oT_ready, b + 1)
                for t in range(3):
                    n = SIZES[t]
                    dst = bank[6 + t // 2][0:n, (t % 2) * C:(t % 2) * C + C]
                    for k in range(2):
                        ins = pe.matmul(dst, oT[:, k, TILE * t:TILE * t + n], wp[:, k, :], start=(k == 0), stop=(k == 1))
                ins.then_inc(proj_psum, 1)

            def n2T_in(b):
                pe.wait_ge(n2_ready, b + 1)
                for j in range(2):
                    for t in range(3):
                        n = SIZES[t]
                        ins = pe.transpose(bank[6 + j][0:CH, TILE * t:TILE * t + n], n2[0:n, t, j * CH:(j + 1) * CH], ident[0:n, 0:n])
                ins.then_inc(n2T_psum, 1)

            def route_in(b):
                pe.wait_ge(n2T_ready, b + 1)
                for t in range(3):
                    n = SIZES[t]
                    for k in range(2):
                        ins = pe.matmul(bank[6][0:n, E * t:E * t + E], n2T[:, k, TILE * t:TILE * t + n], rw[:, k, :], start=(k == 0), stop=(k == 1))
                ins.then_inc(router_psum, 1)

            def pos_in(b):
                pe.wait_ge(oh_ready, b + 1)
                pe.matmul(bank[7][0:TILE, 0:3 * E], upper[:], ohs[:].rearrange("p t e -> p (t e)"), start=True, stop=True)
                pe.matmul(bank[7][0:TILE, 3 * E:6 * E], ones[0:TILE, 0:TILE], ohs[:].rearrange("p t e -> p (t e)"), start=True, stop=True).then_inc(pos_psum, 1)

            def body(b, post, pre):
                av_next = 0
                for r in range(RT + LAG + 1):
                    if r < RT:
                        scores(b, r)
                    if 0 <= r - LAG < RT:
                        turn(b, r - LAG)
                    if post and r == PROJ:
                        proj(b - 1)
                    if post and r == N2T:
                        n2T_in(b - 1)
                    if post and r == ROUTE:
                        route_in(b - 1)
                    if post and r == POS:
                        pos_in(b - 1)
                    if pre and r == HNT:
                        if post:
                            pe.wait_ge(pos_used, b)
                        hnT_in(b + 1)
                    if pre and r == QQ:
                        pe.wait_ge(hnT_ready, b + 2)
                        qk_in(b + 1, 0, q_psum)
                    if pre and r == VV:
                        pe.wait_ge(qs_ready, b + 2)
                        v_in(b + 1)
                    if pre and r == VB:
                        vb_in(b + 1)
                    if pre and r == RT:
                        pe.wait_ge(vb_ready, b + 2)
                        qk_in(b + 1, 1, k_psum)
                    while av_next < H and last_tile(av_next) + LAG + 1 <= r:
                        av(b, av_next)
                        av_next += 1
                for h in range(av_next, H):
                    av(b, h)

            wait(pe, prep_ready, 2)
            hnT_in(0)
            pe.wait_ge(hnT_ready, 1)
            qk_in(0, 0, q_psum)
            pe.wait_ge(qs_ready, 1)
            v_in(0)
            vb_in(0)
            pe.wait_ge(vb_ready, 1)
            qk_in(0, 1, k_psum)

            def edge():
                proj(B - 1)
                n2T_in(B - 1)
                route_in(B - 1)
                pos_in(B - 1)

            batches(pe, body, edge)
            pe.wait_ge(pos_psum, B)
            pe.sem_inc(att_over, 1)
            pe.wait_ge(att_over, 4)
            pe.wait_ge(tab_ready, 1)
            pe.wait_ge(fw_loaded, 48)

            def x_turn(i, s, n):
                pe.wait_ge(xg_loaded[s], 16 * n + 16)
                wait(pe, xgT_ready, i)
                for j in range(2):
                    ins = pe.transpose(bank[6][0:CH, 128 * j:128 * j + 128], xg[:, s, j * CH:(j + 1) * CH], ident[:])
                ins.then_inc(xgT_psum, 1)

            def gate_up(i, s, k, at):
                pe.wait_ge(xgT_ready, i + 1)
                wait(pe, hh_ready, 2 * i + k - 1)
                for c, w in enumerate((wg, wu)):
                    for kk in range(2):
                        ins = pe.matmul(bank[2 * k + c][:, 0:HF], xgT[:, s, kk, :],
                                        w[:, bass.ds(at * F + kk * E * F + k * HF, HF)], start=(kk == 0), stop=(kk == 1))
                ins.then_inc(gu_psum, 1)

            def h_turn(i, s):
                pe.wait_ge(hh_ready, 2 * i + 2)
                wait(pe, hT_ready, i)
                for c in range(F // 128):
                    ins = pe.transpose(bank[4 + c // 3][:, 128 * (c % 3):128 * (c % 3) + 128], hh[:, s, 128 * c:128 * c + 128], ident[:])
                ins.then_inc(hT_psum, 1)

            def down(i, at):
                pe.wait_ge(hT_ready, i + 1)
                wait(pe, y_ready, i)
                for c in range(F // 128):
                    ins = pe.matmul(bank[7][:, 0:C], hT[:, c, :], wd[:, bass.ds(at * (F // 128 * C) + c * C, C)],
                                    start=(c == 0), stop=(c == F // 128 - 1))
                ins.then_inc(y_psum, 1)

            def expert(i):
                return pe.value_load(tile_e[0:1, bass.ds(i, 1)], min_val=0, max_val=E - 1)

            def pair(n, first):
                for s in range(2):
                    i = 2 * n + s
                    x_turn(i + 1, 1 - s, n + s)
                    gate_up(i, s, 0, expert(i))
                    if not (first and s == 0):
                        h_turn(i - 1, 1 - s)
                    gate_up(i, s, 1, expert(i))
                    if not (first and s == 0):
                        down(i - 1, expert(i - 1))

            x_turn(0, 0, 0)
            pair(0, True)
            with pe.Fori(1, TILES // 2) as n:
                pair(n, False)
            h_turn(TILES - 1, 1)
            down(TILES - 1, expert(TILES - 1))

        @block.vector
        def _(dve):
            dve.sem_inc(rows_used, 2)
            ch = Chain(dve, dve_prep, 0)
            dve.wait_ge(tokp_loaded, 64)
            ch.link(dve.scalar_tensor_tensor(out=junk[:, 0, 0:C], in0=gtmp[:, 1], scalar=1.0, in1=gw[:], op0=ALU.mult, op1=ALU.mult, accum_out=c1[:]))
            ch.link(dve.tensor_tensor(c0[:], c1[:], tb[:], ALU.add))
            ch.link(dve.tensor_tensor(gw[:], gtmp[:, 0], gw[:], ALU.mult))
            st = Chain(dve, dve_stat, 4 * TPP + 1)

            def stat(b, g):
                st.start(b)
                for t in range(TPP):
                    st.mark(dve.bn_stats(stats[:, t, :], xe[:, bass.ds((b * TPP + t) * XW, C)]))
                st.sync(dve_passed)
                for t in range(TPP):
                    st.mark(dve.bn_aggr(mv[:, t, :], stats[:, t, :]))
                st.sync()
                for t in range(TPP):
                    st.mark(dve.scalar_tensor_tensor(out=junk[:, t, 0:C], in0=xe[:, bass.ds((b * TPP + t) * XW, C)], scalar=mv[:, t, 0:1],
                                                     in1=gw[:], op0=ALU.subtract, op1=ALU.mult, accum_out=dots[:, t:t + 1]))
                for t in range(TPP):
                    st.mark(dve.tensor_copy(xe[:, bass.ds((b * TPP + t) * XW + C, 2)], mv[:, t, :]))
                st.sync()
                st.link(dve.tensor_copy(score[:, bass.ds(b * TPP, TPP)], dots[:]))
                st.end()

            for g in range(GROUPS):
                dve.wait_ge(x_loaded[g], 16 * BG)
                with dve.Fori(g * BG, g * BG + BG) as b:
                    stat(b, g)
            rstd = xe4[:, :, :, C + 1:C + 2].rearrange("p b t o -> p (b t o)")
            ch.link(dve.tensor_scalar(var[:], rstd, EPS, None, ALU.add))
            dve.sem_inc(var_ready, 1)
            dve.wait_ge(sqrt_ready, 1)
            ch.link(dve.reciprocal(rr[:], r0[:]))
            ch.link(dve.tensor_tensor(r0[:], rr[:], rr[:], ALU.mult))
            ch.link(dve.tensor_tensor(r0[:], r0[:], var[:], ALU.mult))
            ch.link(dve.tensor_scalar(r0[:], r0[:], -0.5, 0.5, ALU.mult, ALU.add))
            ch.link(dve.tensor_tensor(r0[:], r0[:], rr[:], ALU.mult))
            ch.link(dve.tensor_tensor(rr[:], r0[:], rr[:], ALU.add))
            ch.link(dve.tensor_copy(rstd, rr[:]))
            ch.link(dve.tensor_tensor(score[:], score[:], rr[:], ALU.mult))
            ch.link(dve.tensor_scalar(score[:], score[:], c0[:, 0:1], None, ALU.add))
            dve.sem_inc(score_ready, 1)
            dve.wait_ge(consts_ready, 1)

            rk = Chain(dve, dve_rank, 2 + 2 * TPP)
            with dve.Fori(0, B // 2) as i:
                for s in range(2):
                    b = 2 * i + s
                    rk.start(b)
                    rk.link(dve.tensor_copy(sc_cur[:, s], score[:, bass.ds(b * TPP, TPP)]))
                    dve.wait_ge(rows_ready, b + 3)
                    for t in range(TPP):
                        rk.mark(dve.tensor_scalar(junk[:, t, :], bank[s][0:NP, 0:N], sc_cur[:, s, t:t + 1], 0.0, ALU.is_gt, ALU.add,
                                                  accum_out=above[:, s, t:t + 1]))
                        rk.link(dve.scalar_tensor_tensor(out=junk[:, TPP + t, :], in0=bank[s][0:NP, 0:N], scalar=sc_cur[:, s, t:t + 1],
                                                         in1=earlier[:, t, :], op0=ALU.is_equal, op1=ALU.mult,
                                                         accum_out=equal[:, s, t:t + 1]))
                    dve.sem_inc(rows_used, 1)
                    dve.wait_ge(xout_ready, b + 1)
                    rk.link(dve.scalar_tensor_tensor(out=place[:, s], in0=above[:, s], scalar=row0[:, bass.ds(b, 1)], in1=equal[:, s],
                                                     op0=ALU.add, op1=ALU.add))
                    dve.sem_inc(place_ready, 1)
                    rk.end()

            dve.wait_ge(prep_ready, 1)
            dve.wait_ge(w_loaded, 16 * (7 + 2 * H))
            ch.link(dve.tensor_copy(ww[:].rearrange("p h g d -> p (h g) d"), wwt[:].unsqueeze(2).to_broadcast([TILE, H * H, D])))
            dve.sem_inc(prep_ready, 1)

            def hn_make(b):
                dve.wait_ge(x_in_loaded, 32 * b + 32)
                wait(dve, hnT_psum, b)
                for t in range(3):
                    n = SIZES[t]
                    ins = dve.tensor_scalar(hn[0:n, t, :], x_in[0:n, t, 0:C], x_in[0:n, t, C:C + 1], x_in[0:n, t, C + 1:C + 2],
                                            ALU.subtract, ALU.mult)
                ins.then_inc(hn_ready, 1)
                dve.wait_ge(hn_ready, b + 1)
                dve.sem_inc(x_in_used, 1)

            def q_out(b):
                dve.wait_ge(q_psum, b + 1)
                wait(dve, qh_ready, b * H)
                for c in range(2):
                    ins = dve.tensor_scalar(qs[:, c, :], bank[6 + c][0:CH, 0:KEEP], bqk[:, c:c + 1], SCALE, ALU.add, ALU.mult)
                ins.then_inc(qs_ready, 1)

            def k_out(b):
                dve.wait_ge(k_psum, b + 1)
                for c in range(2):
                    ins = dve.tensor_scalar(kT[:, c, :], bank[6 + c][0:CH, 0:KEEP], bqk[:, 2 + c:3 + c], None, ALU.add)
                ins.then_inc(kT_ready, 1)

            def v_out(b):
                dve.wait_ge(v_psum, b + 1)
                wait(dve, vh_ready, b * H)
                for t in range(3):
                    n = SIZES[t]
                    ins = dve.tensor_tensor(v[0:n, t, :], bank[6 + t // 2][0:n, (t % 2) * C:(t % 2) * C + C], bv[0:n, :], ALU.add)
                ins.then_inc(v_ready, 1)

            def vb_out(b):
                dve.wait_ge(vb_psum, b + 1)
                wait(dve, vb_kept, b)
                dve.tensor_tensor(vb_next[:], bank[6][0:CH, 0:2], bw[:], ALU.mult).then_inc(vb_ready, 1)

            def vb_keep(b):
                dve.wait_ge(vb_ready, b + 1)
                dve.tensor_copy(vb[:], vb_next[:]).then_inc(vb_kept, 1)

            def row_max(b, r):
                n = rows_of(r)
                dve.wait_ge(s_psum, b * RT + r + 1)
                dve.tensor_reduce(nmax[0:n, r:r + 1], bank[r % 2][0:n, 0:KEEP], AX.X, ALU.max, negate=True).then_inc(max_done, 1)

            def row_bias(b, r):
                n = rows_of(r)
                dve.wait_ge(max_done, b * RT + r + 1)
                dve.tensor_scalar(nbias[0:n, r:r + 1], nmax[0:n, r:r + 1], bl[0:n, r:r + 1], bl[0:n, r:r + 1],
                                  ALU.subtract, ALU.add).then_inc(bias_ready, 1)

            def row_recip(b, r):
                n = rows_of(r)
                dve.wait_ge(exp_done, b * RT + r + 1)
                dve.reciprocal(rz[0:n, r:r + 1], zsum[0:n, r:r + 1]).then_inc(rz_done, 1)

            def row_scale(b, r):
                n = rows_of(r)
                dve.wait_ge(rz_done, b * RT + r + 1)
                dve.tensor_scalar(prob[0:n, r % P_RING, :], prob[0:n, r % P_RING, :], rz[0:n, r:r + 1], None, ALU.mult).then_inc(prob_ready, 1)

            def pT_out(b, r):
                n = rows_of(r)
                dve.wait_ge(t_psum, b * RT + r + 1)
                src = bank[2 + r % 2][0:TILE, 0:384].rearrange("p (t q) -> p t q", t=3)
                dve.tensor_copy(pT[:, 0:2, 128 * r:128 * r + n], src[:, 0:2, 0:n])
                dve.tensor_copy(pT[0:SIZES[2], 2, 128 * r:128 * r + n], src[0:SIZES[2], 2, 0:n]).then_inc(pT_ready, 1)

            def oT_out(b):
                dve.wait_ge(av_done, b * H + H)
                dve.wait_ge(vb_kept, b + 1)
                for j in range(2):
                    ins = dve.tensor_scalar(oT[:, j, :], bank[4 + j][0:CH, 0:KEEP], vb[:, j:j + 1], None, ALU.add)
                ins.then_inc(oT_ready, 1)

            post_c = Chain(dve, dve_post, 14)
            route_c = Chain(dve, dve_route, 17)
            slot_c = Chain(dve, dve_slot, 9)

            def hres_out(b):
                c = post_c
                c.start(b)
                dve.wait_ge(proj_psum, b + 1)
                dve.wait_ge(x_res_ready, b + 1)
                dve.wait_ge(h_stored, 32 * b + 32)
                for t in range(3):
                    n = SIZES[t]
                    ins = dve.tensor_tensor(hres[0:n, t, :], bank[6 + t // 2][0:n, (t % 2) * C:(t % 2) * C + C], x_res[0:n, t, :], ALU.add)
                ins.then_inc(hres_ready, 1)
                dve.wait_ge(hres_ready, b + 1)
                for t in range(3):
                    c.mark(dve.bn_stats(st2[:, t, :], hres[:, t, :]))
                c.sync(dve_passed)
                for t in range(3):
                    c.mark(dve.bn_aggr(mv2[:, t, :], st2[:, t, :]))
                c.sync()
                c.link(dve.tensor_scalar(ve[:], mv2[:, :, 1], EPS, None, ALU.add))
                dve.sem_inc(ve_ready, 1)

            def n2_out(b):
                c = post_c
                dve.wait_ge(pow_ready, b + 1)
                c.link(dve.tensor_tensor(rb[:], ra[:], ra[:], ALU.mult))
                c.link(dve.tensor_tensor(rb[:], rb[:], ve[:], ALU.mult))
                c.link(dve.tensor_scalar(rb[:], rb[:], -0.5, 0.5, ALU.mult, ALU.add))
                c.link(dve.tensor_tensor(rb[:], rb[:], ra[:], ALU.mult))
                c.link(dve.tensor_tensor(rb[:], rb[:], ra[:], ALU.add))
                dve.wait_ge(n_stored, 32 * b + 32)
                for t in range(2):
                    c.mark(dve.tensor_scalar(n2[:, t, :], hres[:, t, :], mv2[:, t, 0:1], rb[:, t:t + 1], ALU.subtract, ALU.mult))
                dve.tensor_scalar(n2[:, 2, :], hres[:, 2, :], mv2[:, 2, 0:1], rb[:, 2:3], ALU.subtract, ALU.mult).then_inc(n2_ready, 1)
                c.end()

            def route_out(b):
                c = route_c
                c.start(b)
                dve.wait_ge(router_psum, b + 1)
                dve.tensor_copy(lg[:, 0:2, :], bank[6][0:TILE, 0:2 * E].rearrange("p (t e) -> p t e", t=2))
                c.mark(dve.tensor_copy(lg[0:SIZES[2], 2, :], bank[6][0:SIZES[2], 2 * E:3 * E]))
                c.sync(dve_passed)
                for t in range(3):
                    c.mark(dve.max(mx[:, t, :], lg[:, t, :]))
                c.sync(dve_passed)
                for t in range(3):
                    c.mark(dve.max_index(ix[:, t, :], mx[:, t, :], lg[:, t, :]))
                c.link(dve.tensor_tensor(dl[:], mx[:, :, 1], mx[:, :, 0], ALU.subtract))
                dve.sem_inc(dl_ready, 1)
                c.link(dve.tensor_copy(ixf[:], ix[:, :, 0:2]))
                for k in range(2):
                    c.mark(dve.tensor_tensor(oh[:, k], iota8[:], ixf[:, :, k:k + 1].to_broadcast([TILE, 3, E]), ALU.is_equal))
                c.sync()
                c.link(dve.tensor_tensor(ohs[:], oh[:, 0], oh[:, 1], ALU.add))
                c.link(dve.tensor_tensor(ohs[:], ohs[:], valid[:], ALU.mult))
                dve.sem_inc(oh_ready, 1)
                dve.wait_ge(ed_ready, b + 1)
                c.link(dve.tensor_scalar(ed1[:], ed[:], 1.0, None, ALU.add))
                c.link(dve.reciprocal(wa[:], ed1[:]))
                c.mark(dve.tensor_copy(w1_all[:, bass.ds(3 * b, 3)], wa[:]))
                c.link(dve.tensor_tensor(w2_all[:, bass.ds(3 * b, 3)], ed[:], wa[:], ALU.mult))
                c.end()

            def slot_out(b):
                c = slot_c
                c.start(b)
                dve.wait_ge(pos_psum, b + 1)
                dve.wait_ge(ids_free, b + 1)
                pre_, tot = bank[7][0:TILE, 0:3 * E].rearrange("p (t e) -> p t e", t=3), bank[7][0:TILE, 3 * E:6 * E]
                for t in range(3):
                    c.mark(dve.tensor_tensor(pos[:, t, :], pre_[:, t, :], run[:], ALU.add))
                    c.link(dve.tensor_tensor(run[:], tot[:, E * t:E * t + E], run[:], ALU.add))
                dve.sem_inc(pos_used, 1)
                c.link(dve.tensor_tensor(posm[:], oh[:], pos[:].unsqueeze(1).to_broadcast([TILE, 2, 3, E]), ALU.mult))
                c.link(dve.tensor_reduce(slots[:].rearrange("p t k -> p k t"), posm[:], AX.X, ALU.add))
                dve.tensor_copy(slot_u[:], slots[:].rearrange("p t k -> p k t"))
                dve.tensor_copy(slot_all[:, bass.ds(3 * b, 3), :], slots[:])
                c.link(dve.tensor_scalar(id_u[:], idc[:], 0.0, None, ALU.add))
                dve.tensor_scalar(idc[:], idc[:], float(KEEP), None, ALU.add).then_inc(slots_ready, 1)
                c.end()

            def body(b, post, pre):
                for r in range(RT + LAG + 1):
                    if r < RT:
                        row_max(b, r)
                    if 0 <= r - 1 < RT:
                        row_recip(b, r - 1)
                    if r < RT:
                        row_bias(b, r)
                    if 0 <= r - 1 < RT:
                        row_scale(b, r - 1)
                    if post and r == 0:
                        oT_out(b - 1)
                        dve.wait_ge(oT_ready, b)
                    if r == 0:
                        vb_keep(b)
                    if 0 <= r - LAG - 1 < RT:
                        pT_out(b, r - LAG - 1)
                    if post and r == PROJ + 1:
                        hres_out(b - 1)
                    if post and r == PROJ + 3:
                        n2_out(b - 1)
                    if post and r == ROUTE + 1:
                        route_out(b - 1)
                    if post and r == POS + 1:
                        slot_out(b - 1)
                    if pre and r == HNT - 3:
                        hn_make(b + 1)
                    if pre and r == QQ + 1:
                        q_out(b + 1)
                    if pre and r == VV + 1:
                        v_out(b + 1)
                    if pre and r == VB + 1:
                        vb_out(b + 1)
                if pre:
                    k_out(b + 1)

            dve.wait_ge(bl_loaded, 16 * len(BL_PARTS))
            hn_make(0)
            q_out(0)
            v_out(0)
            vb_out(0)
            k_out(0)

            def edge():
                oT_out(B - 1)
                hres_out(B - 1)
                n2_out(B - 1)
                route_out(B - 1)
                slot_out(B - 1)

            batches(dve, body, edge)
            dve.wait_ge(slots_ready, B)
            dve.sem_inc(att_over, 1)
            dve.wait_ge(att_over, 4)
            dve.wait_ge(prep_ready, 3)

            tb_c = Chain(dve, dve_tab, 0)
            L = tb_c.link
            L(dve.tensor_tensor(cnt[:], run[:], base8[:], ALU.subtract))
            L(dve.tensor_scalar(cnti[:], cnt[:], 127.0, None, ALU.add))
            L(dve.tensor_scalar(cnti[:], cnti[:], 7, None, ALU.logical_shift_right))
            L(dve.tensor_copy(cntf[:], cnti[:]))
            L(dve.tensor_scalar(jump[:], cntf[:], -128.0, float(REGION), ALU.mult, ALU.add))
            L(dve.tensor_copy(upto[:, 0:1], cntf[:, 0:1]))
            for e in range(1, E):
                L(dve.tensor_tensor(upto[:, e:e + 1], upto[:, e - 1:e], cntf[:, e:e + 1], ALU.add))
            for e in range(E):
                tb_c.mark(dve.tensor_scalar(ge[:, e, :], tix[:], upto[0:1, e:e + 1], None, ALU.is_ge))
            tb_c.sync()
            L(dve.tensor_copy(te[:], ge[:, 0, :]))
            for e in range(1, E - 1):
                L(dve.tensor_tensor(te[:], te[:], ge[:, e, :], ALU.add))
            L(dve.tensor_copy(tile_e[:], te[:]))
            L(dve.tensor_scalar(ta[:], tix[:], 128.0, None, ALU.mult))
            for e in range(E):
                L(dve.scalar_tensor_tensor(out=ta[:], in0=ge[:, e, :], scalar=jump[0:1, e:e + 1], in1=ta[:], op0=ALU.mult, op1=ALU.add))
            L(dve.tensor_copy(tile_at[:], ta[:]))
            flat = slot_all[:].rearrange("p a k -> p (a k)")
            for e in range(E - 1):
                tb_c.mark(dve.tensor_scalar(slot_ge[:, e, :], flat, float((e + 1) * REGION), None, ALU.is_ge))
            tb_c.sync()
            L(dve.tensor_scalar(jump[:], jump[:], -1.0, None, ALU.mult))
            for e in range(E - 1):
                L(dve.scalar_tensor_tensor(out=flat, in0=slot_ge[:, e, :], scalar=jump[:, e:e + 1], in1=flat, op0=ALU.mult, op1=ALU.add))
            dve.sem_inc(tab_ready, 1)

            def xT_out(i, s):
                dve.wait_ge(xgT_psum, i + 1)
                wait(dve, gu_psum, 2 * i - 2)
                dve.tensor_copy(xgT[:, s], bank[6][0:CH, 0:256].rearrange("p (j q) -> p j q", j=2)).then_inc(xgT_ready, 1)

            def mult(i, s, k):
                dve.wait_ge(silu_done, 2 * i + k + 1)
                wait(dve, hT_psum, i - 1)
                dve.tensor_tensor(hh[:, s, k * HF:(k + 1) * HF], sg[:, k * HF:(k + 1) * HF], bank[2 * k + 1][:, 0:HF], ALU.mult).then_inc(hh_ready, 1)

            def y_out(i, s, n):
                dve.wait_ge(y_psum, i + 1)
                dve.wait_ge(y_stored[s], 16 * n + 16)
                dve.tensor_copy(yo[:, s, :], bank[7][:, 0:C]).then_inc(y_ready, 1)

            def pair(n, first):
                for s in range(2):
                    i = 2 * n + s
                    xT_out(i + 1, 1 - s)
                    mult(i, s, 0)
                    if not (first and s == 0):
                        y_out(i - 1, 1 - s, n + s - 1)
                    mult(i, s, 1)

            xT_out(0, 0)
            pair(0, True)
            with dve.Fori(1, TILES // 2) as n:
                pair(n, False)
            y_out(TILES - 1, 1, TILES // 2 - 1)

            def comb(b, first=False):
                dve.tensor_copy(sl_cur[:], slot_all[:, bass.ds(3 * b, 3), :].rearrange("p t k -> p k t")).then_inc(slc_ready, 1)
                dve.wait_ge(hc_loaded, 48 * b + 48)
                for t in range(3):
                    n = SIZES[t]
                    dve.wait_ge(y_gathered[t], 32 * b + 32)
                    dve.scalar_tensor_tensor(out=oa[0:n, t, :], in0=y1[0:n, t, :], scalar=w1_all[0:n, bass.ds(3 * b + t, 1)], in1=hc[0:n, t, :],
                                             op0=ALU.mult, op1=ALU.add).then_inc(comb_step, 1)
                if not first:
                    dve.wait_ge(out_stored, 48 * b)
                for t in range(3):
                    n = SIZES[t]
                    dve.wait_ge(comb_step, 3 * b + t + 1)
                    dve.scalar_tensor_tensor(out=oc[0:n, t, :], in0=y2[0:n, t, :], scalar=w2_all[0:n, bass.ds(3 * b + t, 1)], in1=oa[0:n, t, :],
                                             op0=ALU.mult, op1=ALU.add).then_inc(comb_done, 1)
                dve.wait_ge(comb_done, 3 * b + 3)

            comb(0, True)
            with dve.Fori(1, B) as b:
                comb(b)


def kernel(x, L0_tok_gamma, L0_tok_beta, L0_tok_w, L0_tok_b, L0_attn_w_qkv, L0_attn_b_qkv, L0_attn_w_l,
           L0_attn_b_l, L0_attn_w_w, L0_attn_b_w, L0_attn_w_proj, L0_attn_b_proj, L0_ffn_router_w,
           L0_ffn_Wg, L0_ffn_Wu, L0_ffn_Wd):
    import numpy as np
    import concourse.bacc as bacc
    from concourse.bass_utils import run_bass_kernel_spmd

    def up(w):
        return np.ascontiguousarray(np.transpose(np.asarray(w).reshape(E * F, 2, CH), (2, 1, 0)))

    down = np.ascontiguousarray(np.transpose(np.asarray(L0_ffn_Wd).reshape(E, C, F // 128, 128), (3, 0, 2, 1))).reshape(128, -1)
    arrays = {
        "x": x, "gamma": L0_tok_gamma, "beta": L0_tok_beta, "tok_w": L0_tok_w, "tok_b": L0_tok_b,
        "w_qkv": L0_attn_w_qkv, "b_qkv": L0_attn_b_qkv, "w_l": L0_attn_w_l, "b_l": L0_attn_b_l,
        "w_w": L0_attn_w_w, "b_w": L0_attn_b_w, "w_proj": L0_attn_w_proj, "b_proj": L0_attn_b_proj,
        "router_wT": np.ascontiguousarray(np.asarray(L0_ffn_router_w).T),
        "WgT": up(L0_ffn_Wg), "WuT": up(L0_ffn_Wu), "WdT": down,
    }
    arrays = {name: np.ascontiguousarray(a) for name, a in arrays.items()}
    nc = bacc.Bacc("TRN2", target_bir_lowering=False, num_devices=1)
    ins = [nc.dram_tensor(name, a.shape, mybir.dt.from_np(a.dtype), kind="ExternalInput").ap() for name, a in arrays.items()]
    out = nc.dram_tensor("out", (T, C), F32, kind="ExternalOutput").ap()
    xs = nc.dram_tensor("xs", (B * N, XW), F32, kind="Internal").ap()
    ids = nc.dram_tensor("ids", (SLOTS, 1), U32, kind="Internal").ap()
    h_rows = nc.dram_tensor("h_rows", (T, C), F32, kind="Internal").ap()
    n_rows = nc.dram_tensor("n_rows", (T, C), F32, kind="Internal").ap()
    y_rows = nc.dram_tensor("y_rows", (TILES * 128, C), F32, kind="Internal").ap()
    build(nc, *ins, out, xs, ids, h_rows, n_rows, y_rows)
    r = run_bass_kernel_spmd(nc, [arrays], core_ids=[0])
    return r.results[0]["out"].reshape(B, KEEP, C)
```

```python
import concourse.bass as bass
from concourse import mybir
from contextlib import ExitStack

F32 = mybir.dt.float32
F32R = mybir.dt.float32r
U32 = mybir.dt.uint32
I32 = mybir.dt.int32
ALU = mybir.AluOpType
ACT = mybir.ActivationFunctionType
AX = mybir.AxisListType

B, N, C = 32, 375, 192
KEEP = int(N * 0.7)
H, D = 12, 16
E, F = 8, 768
EPS = 1e-5
SCALE = D ** -0.5

TPP = 3
NP = N // TPP
XW = C + 2
GROUPS = 4
BG = B // GROUPS

TILE = 88
SIZES = [TILE, TILE, KEEP - 2 * TILE]
CH = C // 2

ROWS = H * KEEP
RT = -(-ROWS // 128)
P_RING = 5
CA = 128
CB = C - CA
DUP = CA + 2 * CB

LAG_T, LAG_LO, LAG_AV, LAG_ACC = 3, 3, 4, 5


def rows_of(r):
    return min(128, ROWS - 128 * r)


def last_tile(h):
    return (KEEP * (h + 1) - 1) // 128


def last_head(r):
    return (128 * r + rows_of(r) - 1) // KEEP


def before(r, ring):
    if r >= ring:
        return r - ring + 1
    return max(q for q in range(RT) if q % ring == r % ring) + 1 - RT


HEAD_PARTS = [(h, 0, h * D) for h in range(CA // D)] + \
    [(h, 1, h * D - CA + twice) for h in range(CA // D, H) for twice in (0, CB)]
W_LOADS = 9 + 8 + 3 * len(HEAD_PARTS)

BL_PARTS = [(g, r, max(g * KEEP - 128 * r, 0), min((g + 1) * KEEP - 128 * r, 128))
            for g in range(H) for r in range(g * KEEP // 128, last_tile(g) + 1)]

T = B * KEEP
REGION = -(-T // 128) * 128
TILES = (2 * T + E * 127) // 128
TILES += TILES % 2
SLOTS = -(-(E * REGION + (TILES + 2) * 128) // 128 ** 2) * 128 ** 2
HF = F // 2
COLS = B * 3


def build(nc, x, gamma, beta, tok_w, tok_b, w_qkv, b_qkv, w_l, b_l, w_w, b_w, w_proj, b_proj,
          router_wT, WgT, WuT, WdT, out, xs, who, n_rows):
    outer = ExitStack()
    with outer:
        outer.enter_context(nc.allow_non_contiguous_dma(reason="biases and slot numbers"))

        def sem(name):
            return outer.enter_context(nc.semaphore(name))

        def alloc(ctx, name, shape, dt=F32):
            return ctx.enter_context(nc.sbuf_tensor(name, shape, dt))

        def sb(name, shape, dt=F32):
            return alloc(outer, name, shape, dt)

        bank = [outer.enter_context(nc.psum_tensor(f"bank{i}", [128, 512], F32)) for i in range(8)]

        ident = sb("ident", [128, 128])
        ones = sb("ones", [128, 128])
        upper = sb("upper", [TILE, TILE])
        iota8 = sb("iota8", [TILE, 3, E])
        valid = sb("valid", [TILE, 3, E])
        run = sb("run", [TILE, E])
        tile_e = sb("tile_e", [1, TILES + 2], I32)
        tile_at = sb("tile_at", [1, TILES + 2], I32)

        att = ExitStack()
        w_raw = alloc(att, "w_raw", [128, 2, 3 * C])
        wq = alloc(att, "wq", [128, 4, 2 * DUP + C], F32R)
        bqk = alloc(att, "bqk", [128, 4])
        bv = alloc(att, "bv", [TILE, C])
        wl = alloc(att, "wl", [128, 2, H])
        bl = alloc(att, "bl", [128, RT])
        ww = alloc(att, "ww", [128, 2, H])
        bw = alloc(att, "bw", [128, 2])
        wp = alloc(att, "wp", [128, 2, C])
        bp = alloc(att, "bp", [TILE, C])
        rw = alloc(att, "rw", [CH, 2, E])
        half = alloc(att, "half", [TILE, 3])
        nobody = alloc(att, "nobody", [128, SLOTS // 128, 2], U32)
        blank = alloc(att, "blank", [128, C])
        idc = alloc(att, "idc", [TILE, 3])

        sel = ExitStack()
        xe = alloc(sel, "xe", [NP, B * TPP * XW])
        xe4 = xe[:].rearrange("p (b t w) -> p b t w", b=B, t=TPP)
        gw = alloc(sel, "gw", [NP, C])
        gtmp = alloc(sel, "gtmp", [NP, 2, C])
        c0 = alloc(sel, "c0", [NP, 1])
        c1 = alloc(sel, "c1", [NP, 1])
        tb = alloc(sel, "tb", [NP, 1])
        stats = alloc(sel, "stats", [NP, TPP, 6])
        mv = alloc(sel, "mv", [NP, TPP, 2])
        junk = alloc(sel, "junk", [NP, 2 * TPP, N])
        dots = alloc(sel, "dots", [NP, TPP])
        score = alloc(sel, "score", [NP, B * TPP])
        var = alloc(sel, "var", [NP, B * TPP])
        r0 = alloc(sel, "r0", [NP, B * TPP])
        rr = alloc(sel, "rr", [NP, B * TPP])
        earlier = alloc(sel, "earlier", [NP, TPP, N])
        row0 = alloc(sel, "row0", [NP, B])
        sc_cur = alloc(sel, "sc_cur", [NP, 2, TPP])
        sc_wide = alloc(sel, "sc_wide", [NP, 2, TPP, NP])
        x_out = alloc(sel, "x_out", [NP, 2, TPP, XW])
        above = alloc(sel, "above", [NP, 2, TPP])
        equal = alloc(sel, "equal", [NP, 2, TPP])
        place = alloc(sel, "place", [NP, 2, TPP], U32)
        sel.close()

        x_in = alloc(att, "x_in", [TILE, 3, XW])
        hn = alloc(att, "hn", [TILE, 3, DUP])
        hnT = alloc(att, "hnT", [128, 3, KEEP], F32R)
        qs = alloc(att, "qs", [128, 2, KEEP])
        kT = alloc(att, "kT", [128, 2 * 4 * KEEP], F32R)
        v = alloc(att, "v", [TILE, 3, C])
        vb = alloc(att, "vb", [128, 2])
        qh = alloc(att, "qh", [128, 3, ROWS], F32R)
        vs = alloc(att, "vs", [TILE, 3, 2 * CA + 4 * CB], F32R)
        q_full = alloc(att, "q_full", [128, 2, KEEP])
        nmax = alloc(att, "nmax", [128, RT])
        nbias = alloc(att, "nbias", [128, RT])
        zsum = alloc(att, "zsum", [128, RT])
        rz = alloc(att, "rz", [128, RT])
        prob = alloc(att, "prob", [128, P_RING, 3 * TILE])
        p_hi = alloc(att, "p_hi", [TILE, 3, ROWS], F32R)
        p_lo = alloc(att, "p_lo", [TILE, 3, ROWS], F32R)
        oT = alloc(att, "oT", [128, 2, KEEP])
        x_res = alloc(att, "x_res", [TILE, 3, C])
        hres = alloc(att, "hres", [TILE, 3, C])
        n2 = alloc(att, "n2", [TILE, 3, C])
        n2T = alloc(att, "n2T", [CH, 2, KEEP])
        st2 = alloc(att, "st2", [TILE, 3, 6])
        mv2 = alloc(att, "mv2", [TILE, 3, 2])
        ve = alloc(att, "ve", [TILE, 3])
        ra = alloc(att, "ra", [TILE, 3])
        rb = alloc(att, "rb", [TILE, 3])
        lg = alloc(att, "lg", [TILE, 3, E])
        mx = alloc(att, "mx", [TILE, 3, 8])
        ix = alloc(att, "ix", [TILE, 3, 8], U32)
        ixf = alloc(att, "ixf", [TILE, 3, 2])
        oh = alloc(att, "oh", [TILE, 2, 3, E])
        ohs = alloc(att, "ohs", [TILE, 3, E])
        dl = alloc(att, "dl", [TILE, 3])
        ed = alloc(att, "ed", [TILE, 3])
        ed1 = alloc(att, "ed1", [TILE, 3])
        pos = alloc(att, "pos", [TILE, 3, E])
        posm = alloc(att, "posm", [TILE, 2, 3, E])
        slots = alloc(att, "slots", [TILE, 3, 2])
        slot_u = alloc(att, "slot_u", [TILE, 2, 3], U32)
        who_out = alloc(att, "who_out", [TILE, 2, 3, 2], U32)
        att.close()

        ffn = ExitStack()
        wg = alloc(ffn, "wg", [CH, 2 * E * F])
        wu = alloc(ffn, "wu", [CH, 2 * E * F])
        wd = alloc(ffn, "wd", [128, E * (F // 128) * C])
        who_all = alloc(ffn, "who_all", [128, TILES * 2], U32)
        from_row = alloc(ffn, "from_row", [128, 2], U32)
        to_row = alloc(ffn, "to_row", [128, 2], U32)
        xg = alloc(ffn, "xg", [128, 2, C])
        xgT = alloc(ffn, "xgT", [CH, 2, 2, 128])
        sg = alloc(ffn, "sg", [128, F])
        hh = alloc(ffn, "hh", [128, 2, F])
        hT = alloc(ffn, "hT", [128, F // 128, 128])
        yo = alloc(ffn, "yo", [128, 2, C])
        cnt = alloc(ffn, "cnt", [TILE, E])
        cnti = alloc(ffn, "cnti", [TILE, E], I32)
        cntf = alloc(ffn, "cntf", [TILE, E])
        jump = alloc(ffn, "jump", [TILE, E])
        upto = alloc(ffn, "upto", [TILE, E])
        tix = alloc(ffn, "tix", [1, TILES + 2])
        ge = alloc(ffn, "ge", [1, E, TILES + 2])
        te = alloc(ffn, "te", [1, TILES + 2])
        ta = alloc(ffn, "ta", [1, TILES + 2])
        base8 = alloc(ffn, "base8", [TILE, E])
        ffn.close()

        dve_passed, pool_passed = sem("dve_passed"), sem("pool_passed")
        pool_c = sem("pool_c")
        consts_ready = sem("consts_ready")
        x_loaded = [sem(f"x_loaded{g}") for g in range(GROUPS)]
        tokp_loaded = sem("tokp_loaded")
        dve_prep = sem("dve_prep")
        dve_stat = sem("dve_stat")
        var_ready, sqrt_ready, score_ready = sem("var_ready"), sem("sqrt_ready"), sem("score_ready")
        wide_ready, rows_ready, rows_used = sem("wide_ready"), sem("rows_ready"), sem("rows_used")
        xout_ready, place_ready = sem("xout_ready"), sem("place_ready")
        scattered = [sem(f"scattered{i}") for i in range(2)]
        dve_rank = sem("dve_rank")
        w_loaded, ww_loaded = sem("w_loaded"), sem("ww_loaded")
        bl_loaded = sem("bl_loaded")
        prep_ready = sem("prep_ready")
        x_in_loaded, x_in_used = sem("x_in_loaded"), sem("x_in_used")
        x_res_loaded, x_res_ready = sem("x_res_loaded"), sem("x_res_ready")
        hn_ready, hnT_psum, hnT_ready = sem("hn_ready"), sem("hnT_psum"), sem("hnT_ready")
        q_psum, qs_ready, k_psum, kT_ready = sem("q_psum"), sem("qs_ready"), sem("k_psum"), sem("kT_ready")
        v_psum, v_ready, vb_psum, vb_ready = sem("v_psum"), sem("v_ready"), sem("vb_psum"), sem("vb_ready")
        vhi_ready, vlo_ready = sem("vhi_ready"), sem("vlo_ready")
        qh_hi, qh_lo_a, qh_lo_b = sem("qh_hi"), sem("qh_lo_a"), sem("qh_lo_b")
        bq_ready, q_full_ready = sem("bq_ready"), sem("q_full_ready")
        w_hi_ready, w_lo_ready, hnT_hi, kT_hi = sem("w_hi_ready"), sem("w_lo_ready"), sem("hnT_hi"), sem("kT_hi")
        s_psum, max_done, bias_ready = sem("s_psum"), sem("max_done"), sem("bias_ready")
        exp_done, rz_ready, prob_ready = sem("exp_done"), sem("rz_ready"), sem("prob_ready")
        t_psum, p_hi_ready, p_lo_ready = sem("t_psum"), sem("p_hi_ready"), sem("p_lo_ready")
        u_psum, acc_done = sem("u_psum"), sem("acc_done")
        proj_psum, hres_ready, n2_ready = sem("proj_psum"), sem("hres_ready"), sem("n2_ready")
        ve_ready, pow_ready = sem("ve_ready"), sem("pow_ready")
        n2T_psum, n2T_ready, router_psum, lg_ready = sem("n2T_psum"), sem("n2T_ready"), sem("router_psum"), sem("lg_ready")
        oh_ready, pos_psum, pos_used = sem("oh_ready"), sem("pos_psum"), sem("pos_used")
        dl_ready, ed_ready = sem("dl_ready"), sem("ed_ready")
        slots_ready, ids_sent = sem("slots_ready"), sem("ids_sent")
        blank_ready = sem("blank_ready")
        ids_zeroed, ids_free = sem("ids_zeroed"), sem("ids_free")
        dve_post, dve_route, dve_slot = sem("dve_post"), sem("dve_route"), sem("dve_slot")
        h_stored, n_stored = sem("h_stored"), sem("n_stored")
        att_over = sem("att_over")
        fw_loaded = sem("fw_loaded")
        tab_ready = sem("tab_ready")
        dve_tab = sem("dve_tab")
        who_loaded = [sem(f"who_loaded{i}") for i in range(2)]
        index_ready = sem("index_ready")
        added = sem("added")
        xg_loaded = [sem(f"xg_loaded{i}") for i in range(2)]
        xgT_psum, xgT_ready = sem("xgT_psum"), sem("xgT_ready")
        gu_psum, silu_done, hh_ready = sem("gu_psum"), sem("silu_done"), sem("hh_ready")
        hT_psum, hT_ready, y_psum, y_ready = sem("hT_psum"), sem("hT_ready"), sem("y_psum"), sem("y_ready")
        block = outer.enter_context(nc.Block())

        class Chain:

            def __init__(self, eng, signal, per):
                self.eng, self.sem, self.per, self.n, self.base = eng, signal, per, 0, 0

            def start(self, n):
                self.base, self.n = n * self.per, 0

            def mark(self, ins):
                self.n += 1
                ins.then_inc(self.sem, 1)

            def sync(self, apart=None):
                if apart is not None:
                    wait_apart(self.eng, self.sem, self.base + self.n, apart)
                else:
                    self.eng.wait_ge(self.sem, self.base + self.n)

            def link(self, ins):
                self.mark(ins)
                self.sync()

            def end(self):
                assert self.n == self.per, (self.n, self.per)

        def wait_apart(eng, signal, value, passed):
            eng.wait_ge(signal, value)
            eng.sem_inc(passed, 1)

        def wait(eng, signal, value):
            if not isinstance(value, int) or value > 0:
                eng.wait_ge(signal, value)

        def batches(eng, body):
            body(0, False, True, True)
            with eng.Fori(1, B - 1) as b:
                body(b, True, True, True)
            body(B - 1, True, True, False)
            body(B, True, False, False)

        def w_blocks(j):
            pairs = []
            for i in range(2):
                pairs.append((lambda w, c=i * DUP: w[:, c:c + CA], w_raw[:, j, i * C:i * C + CA]))
                pairs.append((lambda w, c=i * DUP + CA: w[:, c:c + 2 * CB].rearrange("p (a q) -> p a q", a=2),
                              w_raw[:, j, i * C + CA:i * C + C].unsqueeze(1).to_broadcast([128, 2, CB])))
            pairs.append((lambda w: w[:, 2 * DUP:2 * DUP + C], w_raw[:, j, 2 * C:3 * C]))
            return pairs

        def tok_rows(b, t):
            return bass.ds(b * KEEP + TILE * t, SIZES[t])

        PROJ, N2T, ROUTE, POS = 7, 14, 16, 20
        HN, HNT, QQ, KK, VV, VB = 0, 1, 3, 5, 9, 11

        def lagging(b, r, lag, prev, this):
            if r >= lag:
                return [(b, r - lag)] if this else []
            return [(b - 1, r - lag + RT)] if prev else []

        def head_slot(g):
            return max(last_tile(g), QQ + 1) + 1

        def lagging_heads(b, r, lag, prev, this):
            return [(bb, h, j) for j in range(2) for bb, q in lagging(b, r, lag + j, prev, this)
                    for h in range(H) if last_tile(h) == q]

        @block.sync
        def _(sp):
            sp.sem_inc(h_stored, 32)
            sp.sem_inc(n_stored, 32)
            xv = x.rearrange("b (p t) c -> p b t c", t=TPP)
            for g in range(GROUPS):
                for b in range(g * BG, g * BG + BG):
                    sp.dma_start(xe4[:, b, :, 0:C], xv[:, b]).then_inc(x_loaded[g], 16)
            half_rows = w_proj[CA:C, :]
            for dst, src in ((w_raw[:, 0, :], w_qkv[0:CA, :]), (w_raw[0:CB, 1, :], w_qkv[CA:C, :]),
                             (w_raw[CB:CA, 1, :], w_qkv[CA:C, :]),
                             (wp[:, 0, :], w_proj[0:CA, :]), (wp[0:CB, 1, :], half_rows), (wp[CB:CA, 1, :], half_rows),
                             (rw[:], router_wT.rearrange("(j p) n -> p j n", p=CH)),
                             (bv[:], b_qkv[2 * C:3 * C].partition_broadcast(TILE)),
                             (bp[:], b_proj.partition_broadcast(TILE))):
                sp.dma_start(dst, src).then_inc(w_loaded, 16)
            for i in range(2):
                for p, j, c in ((0, 0, 0), (CB, 0, CB), (0, 1, CA), (CB, 1, CA)):
                    sp.dma_start(bqk[p:p + CB, 2 * i + j:2 * i + j + 1],
                                 b_qkv[i * C + c:i * C + c + CB].rearrange("(p o) -> p o", o=1)).then_inc(w_loaded, 16)
            for hd, j, p in HEAD_PARTS:
                sp.dma_start(wl[p:p + D, j, :], w_l[hd].partition_broadcast(D)).then_inc(w_loaded, 16)
                sp.dma_start(ww[p:p + D, j, :], w_w[:, hd].partition_broadcast(D)).then_inc(w_loaded, 16)
                sp.dma_start(bw[p:p + D, j:j + 1], b_w[hd:hd + 1].partition_broadcast(D)).then_inc(w_loaded, 16)
            for g, r, lo, hi in BL_PARTS:
                sp.dma_start(bl[lo:hi, r:r + 1], b_l[g:g + 1].partition_broadcast(hi - lo)).then_inc(bl_loaded, 16)
            sp.wait_ge(blank_ready, 1)
            sp.dma_start(who.rearrange("(p n) o -> p n o", p=128), nobody[:]).then_inc(ids_zeroed, 16)
            sp.dma_start(n_rows[T:T + 128, :], blank[:]).then_inc(ids_zeroed, 16)
            sp.dma_start(out[T:T + 128, :], blank[:]).then_inc(ids_zeroed, 16)

            def load_x(b):
                sp.dma_start(x_in[:, 0:2, :], xs[bass.ds(b * N, 2 * TILE), :].rearrange("(t p) w -> p t w", p=TILE)).then_inc(x_in_loaded, 16)
                sp.dma_start(x_in[0:SIZES[2], 2, :], xs[bass.ds(b * N + 2 * TILE, SIZES[2]), :]).then_inc(x_in_loaded, 16)

            def load_res(b):
                sp.dma_start(x_res[:, 0:2, :], xs[bass.ds(b * N, 2 * TILE), 0:C].rearrange("(t p) w -> p t w", p=TILE)).then_inc(x_res_loaded, 16)
                sp.dma_start(x_res[0:SIZES[2], 2, :], xs[bass.ds(b * N + 2 * TILE, SIZES[2]), 0:C]).then_inc(x_res_loaded, 16)

            def store(b):
                sp.wait_ge(hres_ready, b + 1)
                sp.dma_start(out[bass.ds(b * KEEP, 2 * TILE), :].rearrange("(t p) w -> p t w", p=TILE), hres[:, 0:2, :]).then_inc(h_stored, 16)
                sp.dma_start(out[tok_rows(b, 2), :], hres[0:SIZES[2], 2, :]).then_inc(h_stored, 16)
                sp.wait_ge(n2_ready, b + 1)
                sp.dma_start(n_rows[bass.ds(b * KEEP, 2 * TILE), :].rearrange("(t p) w -> p t w", p=TILE), n2[:, 0:2, :]).then_inc(n_stored, 16)
                sp.dma_start(n_rows[tok_rows(b, 2), :], n2[0:SIZES[2], 2, :]).then_inc(n_stored, 16)

            for s in range(2):
                sp.wait_ge(scattered[s], 16 * TPP * (B // 2))
            load_x(0)

            def body(b, prev, this, nxt):
                if nxt:
                    sp.wait_ge(x_in_used, b + 1)
                    load_x(b + 1)
                if prev:
                    store(b - 1)
                if this:
                    load_res(b)

            batches(sp, body)

            sp.wait_ge(att_over, 4)
            sp.wait_ge(n_stored, 32 * B + 32)
            sp.wait_ge(h_stored, 32 * B + 32)
            sp.dma_start(wg[:], WgT.rearrange("p k n -> p (k n)")).then_inc(fw_loaded, 16)
            sp.dma_start(wu[:], WuT.rearrange("p k n -> p (k n)")).then_inc(fw_loaded, 16)
            sp.dma_start(wd[:], WdT).then_inc(fw_loaded, 16)
            sp.wait_ge(tab_ready, 1)
            sp.wait_ge(ids_sent, 16 * 6 * B)

            def load_who(i, s, n):
                at = sp.value_load(tile_at[0:1, bass.ds(i, 1)], min_val=0, max_val=SLOTS - 128)
                if not isinstance(n, int):
                    sp.wait_ge(who_loaded[s], 16 * n)
                sp.dma_start(who_all[:, bass.ds(2 * i, 2)], who[bass.ds(at, 128), :]).then_inc(who_loaded[s], 16)

            for s in range(2):
                load_who(s, s, 0)
            with sp.Fori(1, TILES // 2) as n:
                for s in range(2):
                    load_who(2 * n + s, s, n)
            sp.wait_ge(added, 16 * TILES)

        @block.gpsimd
        def _(pool):
            ch = Chain(pool, pool_c, 0)
            ch.link(pool.memset(ident[:], 0.0))
            ch.link(pool.affine_select(out=ident[:], in_=ident[:], compare_op=ALU.not_equal, fill=1.0, base=0,
                                       pattern=[[-1, 128]], channel_multiplier=1))
            ch.link(pool.memset(ones[:], 1.0))
            ch.link(pool.affine_select(out=upper[:], in_=ones[0:TILE, 0:TILE], compare_op=ALU.is_gt, fill=0.0,
                                       base=0, pattern=[[1, TILE]], channel_multiplier=-1))
            ch.link(pool.iota(iota8[:], pattern=[[0, 3], [1, E]], base=0, channel_multiplier=0,
                              allow_small_or_imprecise_dtypes=True))
            ch.link(pool.memset(valid[:], 1.0))
            ch.link(pool.affine_select(out=valid[:], in_=valid[:], compare_op=ALU.is_gt, fill=0.0, base=KEEP,
                                       pattern=[[-TILE, 3], [0, E]], channel_multiplier=-1))
            ch.link(pool.iota(run[:], pattern=[[REGION, E]], base=0, channel_multiplier=0,
                              allow_small_or_imprecise_dtypes=True))
            ch.link(pool.memset(earlier[:], 1.0))
            for t in range(TPP):
                ch.link(pool.affine_select(out=earlier[:, t, :].rearrange("p (a q) -> p a q", a=TPP),
                                           in_=earlier[:, t, :].rearrange("p (a q) -> p a q", a=TPP),
                                           compare_op=ALU.is_gt, fill=0.0, base=t,
                                           pattern=[[-1, TPP], [-TPP, NP]], channel_multiplier=TPP))
            ch.link(pool.iota(row0[:], pattern=[[N, B]], base=0, channel_multiplier=0,
                              allow_small_or_imprecise_dtypes=True))
            pool.sem_inc(consts_ready, 1)
            ch.link(pool.memset(half[:], -0.5))
            ch.link(pool.iota(nobody[:, :, 0].rearrange("p (a q) -> p a q", q=128), pattern=[[0, SLOTS // 128 // 128], [1, 128]], base=T, channel_multiplier=0))
            ch.link(pool.memset(nobody[:, :, 1], 0))
            ch.link(pool.memset(blank[:], 0.0))
            ch.link(pool.iota(idc[:], pattern=[[TILE, 3]], base=0, channel_multiplier=1,
                              allow_small_or_imprecise_dtypes=True))
            pool.sem_inc(blank_ready, 1)
            for dst, src in ((gtmp[:, 0], gamma), (gtmp[:, 1], beta), (gw[:], tok_w), (tb[:], tok_b)):
                pool.dma_start(dst, src.partition_broadcast(NP)).then_inc(tokp_loaded, 16)

            with pool.Fori(0, B // 2) as i:
                for s in range(2):
                    pool.wait_ge(place_ready, 2 * i + s + 1)
                    wait_apart(pool, xout_ready, 2 * i + s + 1, pool_passed)
                    for t in range(TPP):
                        pool.indirect_dma_start(out=xs, out_offset=bass.IndirectOffsetOnAxis(ap=place[:, s, t:t + 1], axis=0),
                                                in_=x_out[:, s, t, :], in_offset=None).then_inc(scattered[s], 16)
            for s in range(2):
                pool.wait_ge(scattered[s], 16 * TPP * (B // 2))
            ch.link(pool.memset(hres[:], 0.0))
            ch.link(pool.memset(n2[:], 0.0))
            ch.link(pool.memset(lg[:], 0.0))
            ch.link(pool.memset(v[:], 0.0))
            ch.link(pool.memset(vb[:], 0.0))
            ch.link(pool.memset(vs[:].bitcast(F32), 0.0))
            ch.link(pool.memset(prob[:], 0.0))
            pool.sem_inc(prep_ready, 1)

            def v_lo(b):
                pool.wait_ge(vhi_ready, b + 1)
                pool.tensor_tensor(vs[:, :, CA:2 * CA], v[:, :, 0:CA], vs[:, :, 0:CA].bitcast(F32), ALU.subtract)
                pool.tensor_tensor(vs[:, :, 2 * CA + CB:2 * CA + 2 * CB], v[:, :, CA:C],
                                   vs[:, :, 2 * CA:2 * CA + CB].bitcast(F32), ALU.subtract).then_inc(vlo_ready, 1)
                pool.wait_ge(vlo_ready, b + 1)

            def q_lo(b, g):
                wait_apart(pool, qh_hi, b * H + g + 1, pool_passed)
                at = slice(g * KEEP, (g + 1) * KEEP)
                pool.tensor_scalar(q_full[CB:CA, g % 2, :], qs[CB:CA, 1, :], wl[CB:CA, 1, g:g + 1], None, ALU.mult).then_inc(q_full_ready, 1)
                pool.wait_ge(q_full_ready, b * H + g + 1)
                pool.tensor_tensor(qh[CB:CA, 2, at], q_full[CB:CA, g % 2, :], qh[CB:CA, 2, at].bitcast(F32), ALU.subtract).then_inc(qh_lo_b, 1)
                pool.wait_ge(qh_lo_b, b * H + g + 1)

            def residual(b):
                pool.wait_ge(x_res_loaded, 32 * b + 32)
                for t in range(3):
                    n = SIZES[t]
                    ins = pool.tensor_tensor(x_res[0:n, t, :], x_res[0:n, t, :], bp[0:n, :], ALU.add)
                ins.then_inc(x_res_ready, 1)
                pool.wait_ge(x_res_ready, b + 1)

            def inv_std(b):
                pool.wait_ge(ve_ready, b + 1)
                pool.tensor_tensor(ra[:], ve[:], half[:], ALU.pow).then_inc(pow_ready, 1)
                pool.wait_ge(pow_ready, b + 1)

            def send_ids(b):
                wait_apart(pool, slots_ready, b + 1, pool_passed)
                for t in range(3):
                    n = SIZES[t]
                    for k in range(2):
                        pool.indirect_dma_start(out=who, out_offset=bass.IndirectOffsetOnAxis(ap=slot_u[0:n, k, t:t + 1], axis=0),
                                                in_=who_out[0:n, k, t, :], in_offset=None).then_inc(ids_sent, 16)

            def body(b, prev, this, nxt):
                def next_q_lo(heads):
                    if nxt:
                        for g in heads:
                            q_lo(b + 1, g)

                if this and prev:
                    q_lo(b, H - 1)
                if this:
                    v_lo(b)
                next_q_lo(range(3))
                if prev:
                    inv_std(b - 1)
                next_q_lo(range(3, 7))
                if this:
                    residual(b)
                next_q_lo(range(7, 10))
                if prev:
                    send_ids(b - 1)
                    pool.wait_ge(ids_sent, 16 * 6 * b)
                    pool.sem_inc(ids_free, 1)
                next_q_lo(range(10, 11))

            pool.wait_ge(ids_zeroed, 48)
            pool.sem_inc(ids_free, 1)
            for g in range(H):
                q_lo(0, g)
            batches(pool, body)
            pool.wait_ge(ids_sent, 16 * 6 * B)
            pool.sem_inc(att_over, 1)
            pool.wait_ge(att_over, 4)

            ch.link(pool.iota(tix[:], pattern=[[1, TILES + 2]], base=0, channel_multiplier=0,
                              allow_small_or_imprecise_dtypes=True))
            ch.link(pool.iota(base8[:], pattern=[[REGION, E]], base=0, channel_multiplier=0,
                              allow_small_or_imprecise_dtypes=True))
            pool.sem_inc(prep_ready, 1)

            def gather(i, s, n):
                pool.wait_ge(who_loaded[s], 16 * n + 16)
                wait(pool, xgT_psum, i - 1)
                pool.tensor_copy(from_row[:, s:s + 1], who_all[:, bass.ds(2 * i, 1)]).then_inc(index_ready, 1)

            def gather_go(i, s, n):
                pool.indirect_dma_start(out=xg[:, s, :], out_offset=None, in_=n_rows,
                                        in_offset=bass.IndirectOffsetOnAxis(ap=from_row[:, s:s + 1], axis=0)).then_inc(xg_loaded[s], 16)

            def add(i, s, n):
                wait(pool, added, 16 * i)
                pool.tensor_copy(to_row[:, s:s + 1], who_all[:, bass.ds(2 * i, 1)]).then_inc(index_ready, 1)

            def add_go(i, s, n):
                pool.indirect_dma_start(out=out, out_offset=bass.IndirectOffsetOnAxis(ap=to_row[:, s:s + 1], axis=0),
                                        in_=yo[:, s, :], in_offset=None, compute_op=ALU.add).then_inc(added, 16)

            for s in range(2):
                gather(s, s, 0)
                wait_apart(pool, index_ready, s + 1, pool_passed)
                gather_go(s, s, 0)

            def pair(n):
                for s in range(2):
                    i = 2 * n + s
                    gather(i, s, n)
                    wait_apart(pool, index_ready, 2 * i - 1, pool_passed)
                    gather_go(i, s, n)
                    add(i - 2, s, n - 1)
                    pool.wait_ge(index_ready, 2 * i)
                    wait_apart(pool, y_ready, i - 1, pool_passed)
                    add_go(i - 2, s, n - 1)

            pair(1)
            with pool.Fori(2, TILES // 2) as n:
                pair(n)
            for i in range(TILES - 2, TILES):
                add(i, i % 2, i // 2)
                pool.wait_ge(index_ready, TILES + i + 1)
                wait_apart(pool, y_ready, i + 1, pool_passed)
                add_go(i, i % 2, i // 2)

        @block.scalar
        def _(act):
            act.wait_ge(var_ready, 1)
            nc.scalar.activation(r0[:], var[:], ACT.Sqrt).then_inc(sqrt_ready, 1)
            act.wait_ge(score_ready, 1)

            def spread(i, first=False):
                for s in range(2):
                    b = 2 * i + s
                    act.wait_ge(rows_ready, b + 1)
                    src = score[:, bass.ds(b * TPP, TPP)].unsqueeze(2).to_broadcast([NP, TPP, NP])
                    nc.scalar.activation(sc_wide[:, s], src, ACT.Copy).then_inc(wide_ready, 1)
                    if not first:
                        act.wait_ge(scattered[s], 16 * TPP * i)
                    nc.scalar.activation(x_out[:, s].rearrange("p t w -> p (t w)"), xe[:, bass.ds(b * TPP * XW, TPP * XW)],
                                         ACT.Copy).then_inc(xout_ready, 1)

            spread(0, True)
            with act.Fori(1, B // 2) as i:
                spread(i)
            act.wait_ge(prep_ready, 1)

            def hnT_out(b):
                act.wait_ge(hnT_psum, b + 1)
                for j in range(2):
                    ins = nc.scalar.activation(hnT[:, 2 * j, :], bank[6 + j][:, 0:KEEP], ACT.Copy)
                ins.then_inc(hnT_hi, 1)

            def q_out(b):
                act.wait_ge(q_psum, b + 1)
                wait(act, qh_lo_a, b * H)
                wait(act, qh_lo_b, b * H)
                for j in range(2):
                    ins = nc.scalar.activation(qs[:, j, :], bank[6 + j][:, 0:KEEP], ACT.Identity, bias=bqk[:, j:j + 1], scale=SCALE)
                ins.then_inc(qs_ready, 1)

            def k_out(b):
                act.wait_ge(k_psum, b + 1)
                for j in range(2):
                    ins = nc.scalar.activation(kT[:, bass.ds((b & 1) * 4 * KEEP + 2 * j * KEEP, KEEP)], bank[6 + j][:, 0:KEEP],
                                               ACT.Identity, bias=bqk[:, 2 + j:3 + j])
                ins.then_inc(kT_hi, 1)

            def row_scale(b, r):
                n = rows_of(r)
                act.wait_ge(rz_ready, b * RT + r + 1)
                nc.scalar.activation(prob[0:n, r % P_RING, 0:KEEP], prob[0:n, r % P_RING, 0:KEEP], ACT.Copy,
                                     scale=rz[0:n, r:r + 1]).then_inc(prob_ready, 1)

            def n2T_out(b):
                act.wait_ge(n2T_psum, b + 1)
                for j in range(2):
                    ins = nc.scalar.activation(n2T[:, j, :], bank[6 + j][0:CH, 0:KEEP], ACT.Copy)
                ins.then_inc(n2T_ready, 1)

            def q_head(b, g):
                for j in range(2):
                    ins = nc.scalar.activation(qh[:, 2 * j, g * KEEP:(g + 1) * KEEP], qs[:, j, :], ACT.Copy,
                                               scale=wl[:, j, g:g + 1])
                ins.then_inc(qh_hi, 1)

            def exp_out(b, r):
                n = rows_of(r)
                act.wait_ge(bias_ready, b * RT + r + 1)
                wait(act, t_psum, b * RT + before(r, P_RING))
                nc.scalar.activation(prob[0:n, r % P_RING, 0:KEEP], bank[r % 2][0:n, 0:KEEP], ACT.Exp,
                                     bias=nbias[0:n, r:r + 1], accum_out=zsum[0:n, r:r + 1]).then_inc(exp_done, 1)

            def p_hi_out(b, r):
                n = rows_of(r)
                act.wait_ge(t_psum, b * RT + r + 1)
                nc.scalar.activation(p_hi[:, :, 128 * r:128 * r + n],
                                     bank[2 + r % 2][0:TILE, 0:384].rearrange("p (t q) -> p t q", t=3)[:, :, 0:n],
                                     ACT.Copy).then_inc(p_hi_ready, 1)

            def v_hi(b):
                act.wait_ge(v_ready, b + 1)
                wait(act, u_psum, b * 2 * H)
                nc.scalar.activation(vs[:, :, 0:CA], v[:, :, 0:CA], ACT.Copy)
                nc.scalar.activation(vs[:, :, 2 * CA:2 * CA + CB], v[:, :, CA:C], ACT.Copy)
                nc.scalar.activation(vs[:, :, 2 * CA + 2 * CB:2 * CA + 3 * CB], v[:, :, CA:C], ACT.Copy).then_inc(vhi_ready, 1)

            def soft2(b):
                act.wait_ge(dl_ready, b + 1)
                nc.scalar.activation(ed[:], dl[:], ACT.Exp).then_inc(ed_ready, 1)

            def body(b, prev, this, nxt):
                for r in range(RT):
                    for bb, q in lagging(b, r, LAG_T, prev, this):
                        p_hi_out(bb, q)
                    if this:
                        exp_out(b, r)
                    for bb, q in lagging(b, r, 1, prev, this):
                        row_scale(bb, q)
                    if this and r == LAG_ACC:
                        v_hi(b)
                    if nxt and r == HNT:
                        hnT_out(b + 1)
                    if prev and r == N2T:
                        n2T_out(b - 1)
                    if prev and r == ROUTE + 2:
                        soft2(b - 1)
                    if nxt and r == QQ + 1:
                        q_out(b + 1)
                    if nxt and r == KK + 1:
                        k_out(b + 1)
                    for g in [g for g in range(H) if nxt and head_slot(g) == r]:
                        if g == 0:
                            act.wait_ge(qs_ready, b + 2)
                        act.wait_ge(s_psum, b * RT + last_tile(g) + 1)
                        q_head(b + 1, g)
                    if this and r == 0 and prev:
                        act.wait_ge(s_psum, b * RT)
                        q_head(b, H - 1)

            act.wait_ge(w_loaded, 16 * W_LOADS)
            act.wait_ge(bq_ready, 1)
            for j in range(2):
                for dst, src in w_blocks(j):
                    ins = nc.scalar.activation(dst(wq[:, 2 * j]), src, ACT.Copy)
            ins.then_inc(w_hi_ready, 1)
            hnT_out(0)
            q_out(0)
            k_out(0)
            act.wait_ge(qs_ready, 1)
            for g in range(H):
                q_head(0, g)

            batches(act, body)
            act.wait_ge(n2T_ready, B)
            act.sem_inc(att_over, 1)
            act.wait_ge(att_over, 4)

            def gate(i, k):
                act.wait_ge(gu_psum, 2 * i + k + 1)
                wait(act, hh_ready, 2 * i + k - 1)
                nc.scalar.activation(sg[:, k * HF:(k + 1) * HF], bank[2 * k][:, 0:HF], ACT.Silu).then_inc(silu_done, 1)

            def hT_out(i):
                act.wait_ge(hT_psum, i + 1)
                wait(act, y_psum, i)
                for k in range(2):
                    ins = nc.scalar.activation(hT[:, 3 * k:3 * k + 3, :], bank[4 + k][:, 0:384].rearrange("p (a q) -> p a q", a=3),
                                               ACT.Copy)
                ins.then_inc(hT_ready, 1)

            def pair(n, first):
                for s in range(2):
                    i = 2 * n + s
                    gate(i, 0)
                    if not (first and s == 0):
                        hT_out(i - 1)
                    gate(i, 1)

            pair(0, True)
            with act.Fori(1, TILES // 2) as n:
                pair(n, False)
            hT_out(TILES - 1)

        @block.tensor
        def _(pe):
            pe.sem_inc(rows_ready, 2)
            pe.wait_ge(consts_ready, 1)
            with pe.Fori(0, B // 2) as i:
                for s in range(2):
                    b = 2 * i + s
                    pe.wait_ge(wide_ready, b + 1)
                    pe.wait_ge(rows_used, b + 1)
                    for t in range(TPP):
                        ins = pe.transpose(bank[s][0:NP, t * NP:(t + 1) * NP], sc_wide[:, s, t, :], ident[0:NP, 0:NP])
                    ins.then_inc(rows_ready, 1)

            def hnT_in(b):
                pe.wait_ge(hn_ready, b + 1)
                wait(pe, pos_used, b - 1)
                for j in range(2):
                    for t in range(3):
                        n = SIZES[t]
                        ins = pe.transpose(bank[6 + j][:, TILE * t:TILE * t + n], hn[0:n, t, j * CA:(j + 1) * CA], ident[0:n, 0:n])
                ins.then_inc(hnT_psum, 1)

            HN_PRODUCTS = ((CA, 0, 0), (CA, 0, 1), (CA, 1, 0), (CA, 2, 2), (CB, 3, 2))

            def qk_in(b, which, signal):
                for c in range(2):
                    at = which * DUP + c * CA
                    for n, (rows, w, x) in enumerate(HN_PRODUCTS):
                        ins = pe.matmul(bank[6 + c][:, 0:KEEP], wq[0:rows, w, at:at + CA], hnT[0:rows, x, :],
                                        start=(n == 0), stop=(n == len(HN_PRODUCTS) - 1))
                ins.then_inc(signal, 1)

            def v_in(b):
                for t in range(3):
                    n = SIZES[t]
                    dst = bank[6 + t // 2][0:n, (t % 2) * C:(t % 2) * C + C]
                    for i, (rows, w, x) in enumerate(HN_PRODUCTS):
                        ins = pe.matmul(dst, hnT[0:rows, x, TILE * t:TILE * t + n], wq[0:rows, w, 2 * DUP:2 * DUP + C],
                                        start=(i == 0), stop=(i == len(HN_PRODUCTS) - 1))
                ins.then_inc(v_psum, 1)

            def vb_in(b):
                pe.wait_ge(v_ready, b + 1)
                for j, (c, m) in enumerate(((0, CA), (CA, CB))):
                    for t in range(3):
                        ins = pe.matmul(bank[6][0:m, j:j + 1], v[:, t, c:c + m], ones[0:TILE, 0:1], start=(t == 0), stop=(t == 2))
                ins.then_inc(vb_psum, 1)

            def scores(b, r):
                n = rows_of(r)
                if r == 0:
                    pe.wait_ge(kT_ready, b + 1)
                pe.wait_ge(qh_lo_a, b * H + last_head(r) + 1)
                pe.wait_ge(qh_lo_b, b * H + last_head(r) + 1)
                wait(pe, exp_done, b * RT + before(r, 2))
                products = ((CA, 0, 0), (CA, 1, 0), (CA, 0, 1), (CA, 2, 2), (CB, 2, 3))
                for i, (rows, q, k) in enumerate(products):
                    ins = pe.matmul(bank[r % 2][0:n, 0:KEEP], qh[0:rows, q, 128 * r:128 * r + n],
                                    kT[0:rows, bass.ds((b & 1) * 4 * KEEP + k * KEEP, KEEP)], start=(i == 0), stop=(i == len(products) - 1))
                ins.then_inc(s_psum, 1)

            def turn(b, r):
                n = rows_of(r)
                pe.wait_ge(prob_ready, b * RT + r + 1)
                wait(pe, p_lo_ready, b * RT + before(r, 2))
                for t in range(3):
                    ins = pe.transpose(bank[2 + r % 2][0:TILE, 128 * t:128 * t + n], prob[0:n, r % P_RING, TILE * t:TILE * t + TILE], ident[0:n, 0:n])
                ins.then_inc(t_psum, 1)

            def av(b, h, j):
                if h == 0 and j == 0:
                    pe.wait_ge(vlo_ready, b + 1)
                pe.wait_ge(p_lo_ready, b * RT + last_tile(h) + 1)
                at = slice(h * KEEP, (h + 1) * KEEP)
                hi_a, lo_a, hl_b, h0_b = (slice(c, c + CA) for c in range(0, 4 * CA, CA))
                products = (((hi_a, p_hi), (hi_a, p_lo), (lo_a, p_hi)), ((hl_b, p_hi), (h0_b, p_lo)))[j]
                wait(pe, acc_done, 2 * (b * H + h) + j - 1)
                for n, (part, p) in enumerate(products):
                    for t in range(3):
                        ins = pe.matmul(bank[4 + j][:, 0:KEEP], vs[:, t, part], p[:, t, at],
                                        start=(n == 0 and t == 0), stop=(n == len(products) - 1 and t == 2))
                ins.then_inc(u_psum, 1)

            def proj(b):
                pe.wait_ge(acc_done, 2 * H * (b + 1))
                for t in range(3):
                    n = SIZES[t]
                    dst = bank[6 + t // 2][0:n, (t % 2) * C:(t % 2) * C + C]
                    for k in range(2):
                        ins = pe.matmul(dst, oT[:, k, TILE * t:TILE * t + n], wp[:, k, :], start=(k == 0), stop=(k == 1))
                ins.then_inc(proj_psum, 1)

            def n2T_in(b):
                pe.wait_ge(n2_ready, b + 1)
                for j in range(2):
                    for t in range(3):
                        n = SIZES[t]
                        ins = pe.transpose(bank[6 + j][0:CH, TILE * t:TILE * t + n], n2[0:n, t, j * CH:(j + 1) * CH], ident[0:n, 0:n])
                ins.then_inc(n2T_psum, 1)

            def route_in(b):
                pe.wait_ge(n2T_ready, b + 1)
                for t in range(3):
                    n = SIZES[t]
                    for k in range(2):
                        ins = pe.matmul(bank[6][0:n, E * t:E * t + E], n2T[:, k, TILE * t:TILE * t + n], rw[:, k, :], start=(k == 0), stop=(k == 1))
                ins.then_inc(router_psum, 1)

            def pos_in(b):
                pe.wait_ge(oh_ready, b + 1)
                pe.matmul(bank[7][0:TILE, 0:3 * E], upper[:], ohs[:].rearrange("p t e -> p (t e)"), start=True, stop=True)
                pe.matmul(bank[7][0:TILE, 3 * E:6 * E], ones[0:TILE, 0:TILE], ohs[:].rearrange("p t e -> p (t e)"), start=True, stop=True).then_inc(pos_psum, 1)

            def body(b, prev, this, nxt):
                for r in range(RT):
                    if this:
                        scores(b, r)
                    for bb, q in lagging(b, r, LAG_T, prev, this):
                        turn(bb, q)
                    for bb, h, j in lagging_heads(b, r, LAG_AV, prev, this):
                        av(bb, h, j)
                    if nxt and r == HNT:
                        hnT_in(b + 1)
                    if nxt and r == QQ:
                        pe.wait_ge(hnT_ready, b + 2)
                        qk_in(b + 1, 0, q_psum)
                    if nxt and r == KK:
                        pe.wait_ge(qs_ready, b + 2)
                        qk_in(b + 1, 1, k_psum)
                    if prev and r == PROJ:
                        if nxt:
                            pe.wait_ge(kT_ready, b + 2)
                        proj(b - 1)
                    if nxt and r == VV:
                        if prev:
                            pe.wait_ge(hres_ready, b)
                        else:
                            pe.wait_ge(kT_ready, b + 2)
                        v_in(b + 1)
                    if nxt and r == VB:
                        vb_in(b + 1)
                    if prev and r == N2T:
                        if nxt:
                            pe.wait_ge(vb_ready, b + 2)
                        n2T_in(b - 1)
                    if prev and r == ROUTE:
                        route_in(b - 1)
                    if prev and r == POS:
                        pos_in(b - 1)

            pe.wait_ge(prep_ready, 1)
            pe.wait_ge(w_loaded, 16 * W_LOADS)
            hnT_in(0)
            pe.wait_ge(w_lo_ready, 1)
            pe.wait_ge(hnT_ready, 1)
            qk_in(0, 0, q_psum)
            pe.wait_ge(qs_ready, 1)
            qk_in(0, 1, k_psum)
            pe.wait_ge(kT_ready, 1)
            v_in(0)
            vb_in(0)
            pe.wait_ge(vb_ready, 1)

            batches(pe, body)
            pe.wait_ge(pos_psum, B)
            pe.sem_inc(att_over, 1)
            pe.wait_ge(att_over, 4)
            pe.wait_ge(tab_ready, 1)
            pe.wait_ge(fw_loaded, 48)

            def x_turn(i, s, n):
                pe.wait_ge(xg_loaded[s], 16 * n + 16)
                wait(pe, xgT_ready, i)
                for j in range(2):
                    ins = pe.transpose(bank[6][0:CH, 128 * j:128 * j + 128], xg[:, s, j * CH:(j + 1) * CH], ident[:])
                ins.then_inc(xgT_psum, 1)

            def gate_up(i, s, k, at):
                pe.wait_ge(xgT_ready, i + 1)
                wait(pe, hh_ready, 2 * i + k - 1)
                for c, w in enumerate((wg, wu)):
                    for kk in range(2):
                        ins = pe.matmul(bank[2 * k + c][:, 0:HF], xgT[:, s, kk, :],
                                        w[:, bass.ds(at * F + kk * E * F + k * HF, HF)], start=(kk == 0), stop=(kk == 1))
                ins.then_inc(gu_psum, 1)

            def h_turn(i, s):
                pe.wait_ge(hh_ready, 2 * i + 2)
                wait(pe, hT_ready, i)
                for c in range(F // 128):
                    ins = pe.transpose(bank[4 + c // 3][:, 128 * (c % 3):128 * (c % 3) + 128], hh[:, s, 128 * c:128 * c + 128], ident[:])
                ins.then_inc(hT_psum, 1)

            def down(i, at):
                pe.wait_ge(hT_ready, i + 1)
                wait(pe, y_ready, i)
                for c in range(F // 128):
                    ins = pe.matmul(bank[7][:, 0:C], hT[:, c, :], wd[:, bass.ds(at * (F // 128 * C) + c * C, C)],
                                    start=(c == 0), stop=(c == F // 128 - 1))
                ins.then_inc(y_psum, 1)

            def expert(i):
                return pe.value_load(tile_e[0:1, bass.ds(i, 1)], min_val=0, max_val=E - 1)

            def pair(n, first, last):
                for s in range(2):
                    i = 2 * n + s
                    gate_up(i, s, 0, expert(i))
                    if not (first and s == 0):
                        h_turn(i - 1, 1 - s)
                    gate_up(i, s, 1, expert(i))
                    if not (last and s == 1):
                        x_turn(i + 1, 1 - s, n + s)
                    if not (first and s == 0):
                        down(i - 1, expert(i - 1))

            x_turn(0, 0, 0)
            pair(0, True, False)
            with pe.Fori(1, TILES // 2 - 1) as n:
                pair(n, False, False)
            pair(TILES // 2 - 1, False, True)
            h_turn(TILES - 1, 1)
            down(TILES - 1, expert(TILES - 1))

        @block.vector
        def _(dve):
            dve.sem_inc(pos_used, 1)
            dve.sem_inc(rows_used, 2)
            ch = Chain(dve, dve_prep, 0)
            dve.wait_ge(tokp_loaded, 64)
            ch.link(dve.scalar_tensor_tensor(out=junk[:, 0, 0:C], in0=gtmp[:, 1], scalar=1.0, in1=gw[:], op0=ALU.mult, op1=ALU.mult, accum_out=c1[:]))
            ch.link(dve.tensor_tensor(c0[:], c1[:], tb[:], ALU.add))
            ch.link(dve.tensor_tensor(gw[:], gtmp[:, 0], gw[:], ALU.mult))
            st = Chain(dve, dve_stat, 4 * TPP + 1)

            def stat(b, g):
                st.start(b)
                for t in range(TPP):
                    st.mark(dve.bn_stats(stats[:, t, :], xe[:, bass.ds((b * TPP + t) * XW, C)]))
                st.sync(dve_passed)
                for t in range(TPP):
                    st.mark(dve.bn_aggr(mv[:, t, :], stats[:, t, :]))
                st.sync()
                for t in range(TPP):
                    st.mark(dve.scalar_tensor_tensor(out=junk[:, t, 0:C], in0=xe[:, bass.ds((b * TPP + t) * XW, C)], scalar=mv[:, t, 0:1],
                                                     in1=gw[:], op0=ALU.subtract, op1=ALU.mult, accum_out=dots[:, t:t + 1]))
                for t in range(TPP):
                    st.mark(dve.tensor_copy(xe[:, bass.ds((b * TPP + t) * XW + C, 2)], mv[:, t, :]))
                st.sync()
                st.link(dve.tensor_copy(score[:, bass.ds(b * TPP, TPP)], dots[:]))
                st.end()

            for g in range(GROUPS):
                dve.wait_ge(x_loaded[g], 16 * BG)
                with dve.Fori(g * BG, g * BG + BG) as b:
                    stat(b, g)
            rstd = xe4[:, :, :, C + 1:C + 2].rearrange("p b t o -> p (b t o)")
            ch.link(dve.tensor_scalar(var[:], rstd, EPS, None, ALU.add))
            dve.sem_inc(var_ready, 1)
            dve.wait_ge(sqrt_ready, 1)
            ch.link(dve.reciprocal(rr[:], r0[:]))
            ch.link(dve.tensor_tensor(r0[:], rr[:], rr[:], ALU.mult))
            ch.link(dve.tensor_tensor(r0[:], r0[:], var[:], ALU.mult))
            ch.link(dve.tensor_scalar(r0[:], r0[:], -0.5, 0.5, ALU.mult, ALU.add))
            ch.link(dve.tensor_tensor(r0[:], r0[:], rr[:], ALU.mult))
            ch.link(dve.tensor_tensor(rr[:], r0[:], rr[:], ALU.add))
            ch.link(dve.tensor_copy(rstd, rr[:]))
            ch.link(dve.tensor_tensor(score[:], score[:], rr[:], ALU.mult))
            ch.link(dve.tensor_scalar(score[:], score[:], c0[:, 0:1], None, ALU.add))
            dve.sem_inc(score_ready, 1)
            dve.wait_ge(consts_ready, 1)

            rk = Chain(dve, dve_rank, 2 + 2 * TPP)
            with dve.Fori(0, B // 2) as i:
                for s in range(2):
                    b = 2 * i + s
                    rk.start(b)
                    rk.link(dve.tensor_copy(sc_cur[:, s], score[:, bass.ds(b * TPP, TPP)]))
                    dve.wait_ge(rows_ready, b + 3)
                    for t in range(TPP):
                        rk.mark(dve.tensor_scalar(junk[:, t, :], bank[s][0:NP, 0:N], sc_cur[:, s, t:t + 1], 0.0, ALU.is_gt, ALU.add,
                                                  accum_out=above[:, s, t:t + 1]))
                        rk.link(dve.scalar_tensor_tensor(out=junk[:, TPP + t, :], in0=bank[s][0:NP, 0:N], scalar=sc_cur[:, s, t:t + 1],
                                                         in1=earlier[:, t, :], op0=ALU.is_equal, op1=ALU.mult,
                                                         accum_out=equal[:, s, t:t + 1]))
                    dve.sem_inc(rows_used, 1)
                    dve.wait_ge(xout_ready, b + 1)
                    rk.link(dve.scalar_tensor_tensor(out=place[:, s], in0=above[:, s], scalar=row0[:, bass.ds(b, 1)], in1=equal[:, s],
                                                     op0=ALU.add, op1=ALU.add))
                    dve.sem_inc(place_ready, 1)
                    rk.end()

            dve.wait_ge(prep_ready, 1)
            dve.wait_ge(w_loaded, 16 * W_LOADS)

            def hn_make(b):
                dve.wait_ge(x_in_loaded, 32 * b + 32)
                wait(dve, hnT_psum, b)
                for t in range(3):
                    n = SIZES[t]
                    mean, rstd = x_in[0:n, t, C:C + 1], x_in[0:n, t, C + 1:C + 2]
                    dve.tensor_scalar(hn[0:n, t, 0:CA], x_in[0:n, t, 0:CA], mean, rstd, ALU.subtract, ALU.mult)
                    ins = dve.tensor_scalar(hn[0:n, t, CA:DUP].rearrange("p (a q) -> p a q", a=2),
                                            x_in[0:n, t, CA:C].unsqueeze(1).to_broadcast([n, 2, CB]), mean, rstd, ALU.subtract, ALU.mult)
                ins.then_inc(hn_ready, 1)
                dve.wait_ge(hn_ready, b + 1)
                dve.sem_inc(x_in_used, 1)

            def hnT_lo(b):
                dve.wait_ge(hnT_hi, b + 1)
                dve.tensor_tensor(hnT[:, 1, :], bank[6][:, 0:KEEP], hnT[:, 0, :].bitcast(F32), ALU.subtract)
                dve.tensor_tensor(hnT[CB:CA, 2, :], bank[7][CB:CA, 0:KEEP], hnT[CB:CA, 2, :].bitcast(F32), ALU.subtract).then_inc(hnT_ready, 1)

            def q_lo(b, g):
                dve.wait_ge(qh_hi, b * H + g + 1)
                at = slice(g * KEEP, (g + 1) * KEEP)
                dve.scalar_tensor_tensor(out=qh[:, 1, at], in0=qs[:, 0, :], scalar=wl[:, 0, g:g + 1],
                                         in1=qh[:, 0, at].bitcast(F32), op0=ALU.mult, op1=ALU.subtract).then_inc(qh_lo_a, 1)

            def k_lo(b):
                dve.wait_ge(kT_hi, b + 1)
                for j, n in enumerate((CA, CB)):
                    at = (b & 1) * 4 * KEEP + 2 * j * KEEP
                    ins = dve.scalar_tensor_tensor(out=kT[0:n, bass.ds(at + KEEP, KEEP)], in0=bank[6 + j][0:n, 0:KEEP],
                                                   scalar=bqk[0:n, 2 + j:3 + j], in1=kT[0:n, bass.ds(at, KEEP)].bitcast(F32),
                                                   op0=ALU.add, op1=ALU.subtract)
                ins.then_inc(kT_ready, 1)

            def v_out(b):
                dve.wait_ge(v_psum, b + 1)
                wait(dve, vlo_ready, b)
                for t in range(3):
                    n = SIZES[t]
                    ins = dve.tensor_tensor(v[0:n, t, :], bank[6 + t // 2][0:n, (t % 2) * C:(t % 2) * C + C], bv[0:n, :], ALU.add)
                ins.then_inc(v_ready, 1)

            def vb_out(b):
                dve.wait_ge(vb_psum, b + 1)
                wait(dve, acc_done, 2 * ((b - 1) * H + 1))
                dve.tensor_tensor(vb[:, 0:1], bank[6][:, 0:1], bw[:, 0:1], ALU.mult)
                dve.tensor_tensor(vb[0:CB, 1:2], bank[6][0:CB, 1:2], bw[0:CB, 1:2], ALU.mult).then_inc(vb_ready, 1)

            def row_max(b, r):
                n = rows_of(r)
                dve.wait_ge(s_psum, b * RT + r + 1)
                dve.tensor_reduce(nmax[0:n, r:r + 1], bank[r % 2][0:n, 0:KEEP], AX.X, ALU.max, negate=True).then_inc(max_done, 1)

            def row_bias(b, r):
                n = rows_of(r)
                dve.wait_ge(max_done, b * RT + r + 1)
                dve.tensor_scalar(nbias[0:n, r:r + 1], nmax[0:n, r:r + 1], bl[0:n, r:r + 1], bl[0:n, r:r + 1],
                                  ALU.subtract, ALU.add).then_inc(bias_ready, 1)

            def row_recip(b, r):
                n = rows_of(r)
                dve.wait_ge(exp_done, b * RT + r + 1)
                dve.reciprocal(rz[0:n, r:r + 1], zsum[0:n, r:r + 1]).then_inc(rz_ready, 1)

            def p_lo_out(b, r):
                n = rows_of(r)
                at = slice(128 * r, 128 * r + n)
                dve.wait_ge(p_hi_ready, b * RT + r + 1)
                dve.tensor_tensor(p_lo[:, :, at], bank[2 + r % 2][0:TILE, 0:384].rearrange("p (t q) -> p t q", t=3)[:, :, 0:n],
                                  p_hi[:, :, at].bitcast(F32), ALU.subtract).then_inc(p_lo_ready, 1)

            def accumulate(b, h, j):
                if h == 0 and j == 0:
                    wait(dve, proj_psum, b)
                    dve.wait_ge(vb_ready, b + 1)
                dve.wait_ge(u_psum, 2 * (b * H + h) + j + 1)
                if h == 0:
                    ins = dve.tensor_scalar(oT[:, j, :], bank[4 + j][:, 0:KEEP], ww[:, j, h:h + 1], vb[:, j:j + 1], ALU.mult, ALU.add)
                else:
                    dve.wait_ge(acc_done, 2 * (b * H + h) + j - 1)
                    ins = dve.scalar_tensor_tensor(out=oT[:, j, :], in0=bank[4 + j][:, 0:KEEP], scalar=ww[:, j, h:h + 1],
                                                   in1=oT[:, j, :], op0=ALU.mult, op1=ALU.add)
                ins.then_inc(acc_done, 1)

            post_c = Chain(dve, dve_post, 14)
            route_c = Chain(dve, dve_route, 16)
            slot_c = Chain(dve, dve_slot, 9)

            def hres_out(b):
                c = post_c
                c.start(b)
                dve.wait_ge(proj_psum, b + 1)
                dve.wait_ge(x_res_ready, b + 1)
                dve.wait_ge(h_stored, 32 * b + 32)
                for t in range(3):
                    n = SIZES[t]
                    ins = dve.tensor_tensor(hres[0:n, t, :], bank[6 + t // 2][0:n, (t % 2) * C:(t % 2) * C + C], x_res[0:n, t, :], ALU.add)
                ins.then_inc(hres_ready, 1)
                dve.wait_ge(hres_ready, b + 1)
                for t in range(3):
                    c.mark(dve.bn_stats(st2[:, t, :], hres[:, t, :]))
                c.sync(dve_passed)
                for t in range(3):
                    c.mark(dve.bn_aggr(mv2[:, t, :], st2[:, t, :]))
                c.sync()
                c.link(dve.tensor_scalar(ve[:], mv2[:, :, 1], EPS, None, ALU.add))
                dve.sem_inc(ve_ready, 1)

            def n2_out(b):
                c = post_c
                dve.wait_ge(pow_ready, b + 1)
                c.link(dve.tensor_tensor(rb[:], ra[:], ra[:], ALU.mult))
                c.link(dve.tensor_tensor(rb[:], rb[:], ve[:], ALU.mult))
                c.link(dve.tensor_scalar(rb[:], rb[:], -0.5, 0.5, ALU.mult, ALU.add))
                c.link(dve.tensor_tensor(rb[:], rb[:], ra[:], ALU.mult))
                c.link(dve.tensor_tensor(rb[:], rb[:], ra[:], ALU.add))

            def n2_write(b):
                c = post_c
                dve.wait_ge(n_stored, 32 * b + 32)
                for t in range(2):
                    c.mark(dve.tensor_scalar(n2[:, t, :], hres[:, t, :], mv2[:, t, 0:1], rb[:, t:t + 1], ALU.subtract, ALU.mult))
                dve.tensor_scalar(n2[:, 2, :], hres[:, 2, :], mv2[:, 2, 0:1], rb[:, 2:3], ALU.subtract, ALU.mult).then_inc(n2_ready, 1)
                c.end()

            def route_out(b):
                c = route_c
                c.start(b)
                dve.wait_ge(router_psum, b + 1)
                dve.tensor_copy(lg[:, 0:2, :], bank[6][0:TILE, 0:2 * E].rearrange("p (t e) -> p t e", t=2))
                c.mark(dve.tensor_copy(lg[0:SIZES[2], 2, :], bank[6][0:SIZES[2], 2 * E:3 * E]))
                c.sync(dve_passed)
                for t in range(3):
                    c.mark(dve.max(mx[:, t, :], lg[:, t, :]))

            def route_b(b):
                c = route_c
                c.sync(dve_passed)
                for t in range(3):
                    c.mark(dve.max_index(ix[:, t, :], mx[:, t, :], lg[:, t, :]))
                c.link(dve.tensor_tensor(dl[:], mx[:, :, 1], mx[:, :, 0], ALU.subtract))
                dve.sem_inc(dl_ready, 1)
                c.link(dve.tensor_copy(ixf[:], ix[:, :, 0:2]))
                for k in range(2):
                    c.mark(dve.tensor_tensor(oh[:, k], iota8[:], ixf[:, :, k:k + 1].to_broadcast([TILE, 3, E]), ALU.is_equal))

            def route_d(b):
                c = route_c
                c.sync()
                c.link(dve.tensor_tensor(ohs[:], oh[:, 0], oh[:, 1], ALU.add))
                c.link(dve.tensor_tensor(ohs[:], ohs[:], valid[:], ALU.mult))
                dve.sem_inc(oh_ready, 1)
                dve.wait_ge(ed_ready, b + 1)
                c.link(dve.tensor_scalar(ed1[:], ed[:], 1.0, None, ALU.add))
                dve.wait_ge(ids_free, b + 1)
                weights = who_out[:].bitcast(F32)
                c.link(dve.reciprocal(weights[:, 0, :, 1], ed1[:]))
                c.link(dve.tensor_tensor(weights[:, 1, :, 1], ed[:], weights[:, 0, :, 1], ALU.mult))
                c.end()

            def slot_out(b):
                c = slot_c
                c.start(b)
                dve.wait_ge(pos_psum, b + 1)
                pre_, tot = bank[7][0:TILE, 0:3 * E].rearrange("p (t e) -> p t e", t=3), bank[7][0:TILE, 3 * E:6 * E]
                for t in range(3):
                    c.mark(dve.tensor_tensor(pos[:, t, :], pre_[:, t, :], run[:], ALU.add))
                    c.link(dve.tensor_tensor(run[:], tot[:, E * t:E * t + E], run[:], ALU.add))
                dve.sem_inc(pos_used, 1)
                c.link(dve.tensor_tensor(posm[:], oh[:], pos[:].unsqueeze(1).to_broadcast([TILE, 2, 3, E]), ALU.mult))
                c.link(dve.tensor_reduce(slots[:].rearrange("p t k -> p k t"), posm[:], AX.X, ALU.add))
                dve.tensor_copy(slot_u[:], slots[:].rearrange("p t k -> p k t"))
                c.link(dve.tensor_copy(who_out[:, :, :, 0], idc[:].unsqueeze(1).to_broadcast([TILE, 2, 3])))
                dve.tensor_scalar(idc[:], idc[:], float(KEEP), None, ALU.add).then_inc(slots_ready, 1)
                c.end()

            def body(b, prev, this, nxt):
                for r in range(RT):
                    if this:
                        row_max(b, r)
                    for bb, q in lagging(b, r, 1, prev, this):
                        row_recip(bb, q)
                    if this:
                        row_bias(b, r)
                    for bb, q in lagging(b, r, LAG_LO, prev, this):
                        p_lo_out(bb, q)
                    for bb, h, j in lagging_heads(b, r, LAG_ACC, prev, this):
                        accumulate(bb, h, j)
                    if nxt and r == HN:
                        hn_make(b + 1)
                    if nxt and r == HNT:
                        hnT_lo(b + 1)
                    if nxt and r == KK + 1:
                        k_lo(b + 1)
                    for g in range(H):
                        if head_slot(g) + 1 == r and nxt:
                            q_lo(b + 1, g)
                        if head_slot(g) + 1 == RT + r and this and prev:
                            q_lo(b, g)
                    if prev and r == PROJ + 1:
                        hres_out(b - 1)
                    if prev and r == PROJ + 3:
                        n2_out(b - 1)
                    if prev and r == PROJ + 4:
                        n2_write(b - 1)
                    if nxt and r == VV + 1:
                        v_out(b + 1)
                    if nxt and r == VB + 1:
                        vb_out(b + 1)
                    if prev and r == ROUTE + 1:
                        route_out(b - 1)
                    if prev and r == ROUTE + 2:
                        route_b(b - 1)
                    if prev and r == ROUTE + 3:
                        route_d(b - 1)
                    if prev and r == POS + 1:
                        slot_out(b - 1)

            dve.wait_ge(bl_loaded, 16 * len(BL_PARTS))
            dve.tensor_scalar(bqk[:, 0:2], bqk[:, 0:2], SCALE, None, ALU.mult).then_inc(bq_ready, 1)
            hn_make(0)
            dve.wait_ge(w_hi_ready, 1)
            for j in range(2):
                for dst, src in w_blocks(j):
                    ins = dve.tensor_tensor(dst(wq[:, 2 * j + 1]), src, dst(wq[:, 2 * j]).bitcast(F32), ALU.subtract)
            ins.then_inc(w_lo_ready, 1)
            hnT_lo(0)
            k_lo(0)
            for g in range(H):
                q_lo(0, g)
            v_out(0)
            vb_out(0)

            batches(dve, body)
            dve.wait_ge(slots_ready, B)
            dve.sem_inc(att_over, 1)
            dve.wait_ge(att_over, 4)
            dve.wait_ge(prep_ready, 2)

            tb_c = Chain(dve, dve_tab, 0)
            L = tb_c.link
            L(dve.tensor_tensor(cnt[:], run[:], base8[:], ALU.subtract))
            L(dve.tensor_scalar(cnti[:], cnt[:], 127.0, None, ALU.add))
            L(dve.tensor_scalar(cnti[:], cnti[:], 7, None, ALU.logical_shift_right))
            L(dve.tensor_copy(cntf[:], cnti[:]))
            L(dve.tensor_scalar(jump[:], cntf[:], -128.0, float(REGION), ALU.mult, ALU.add))
            L(dve.tensor_copy(upto[:, 0:1], cntf[:, 0:1]))
            for e in range(1, E):
                L(dve.tensor_tensor(upto[:, e:e + 1], upto[:, e - 1:e], cntf[:, e:e + 1], ALU.add))
            for e in range(E):
                tb_c.mark(dve.tensor_scalar(ge[:, e, :], tix[:], upto[0:1, e:e + 1], None, ALU.is_ge))
            tb_c.sync()
            L(dve.tensor_copy(te[:], ge[:, 0, :]))
            for e in range(1, E - 1):
                L(dve.tensor_tensor(te[:], te[:], ge[:, e, :], ALU.add))
            L(dve.tensor_copy(tile_e[:], te[:]))
            L(dve.tensor_scalar(ta[:], tix[:], 128.0, None, ALU.mult))
            for e in range(E):
                L(dve.scalar_tensor_tensor(out=ta[:], in0=ge[:, e, :], scalar=jump[0:1, e:e + 1], in1=ta[:], op0=ALU.mult, op1=ALU.add))
            L(dve.tensor_copy(tile_at[:], ta[:]))
            dve.sem_inc(tab_ready, 1)

            def xT_out(i, s):
                dve.wait_ge(xgT_psum, i + 1)
                wait(dve, gu_psum, 2 * i - 2)
                dve.tensor_copy(xgT[:, s], bank[6][0:CH, 0:256].rearrange("p (j q) -> p j q", j=2)).then_inc(xgT_ready, 1)

            def mult(i, s, k):
                dve.wait_ge(silu_done, 2 * i + k + 1)
                wait(dve, hT_psum, i - 1)
                dve.tensor_tensor(hh[:, s, k * HF:(k + 1) * HF], sg[:, k * HF:(k + 1) * HF], bank[2 * k + 1][:, 0:HF], ALU.mult).then_inc(hh_ready, 1)

            def y_out(i, s, n):
                dve.wait_ge(y_psum, i + 1)
                dve.wait_ge(who_loaded[s], 16 * n + 16)
                wait(dve, added, 16 * i - 16)
                dve.tensor_scalar(yo[:, s, :], bank[7][:, 0:C], who_all[:, bass.ds(2 * i + 1, 1)].bitcast(F32), None, ALU.mult).then_inc(y_ready, 1)

            def pair(n, first, last):
                for s in range(2):
                    i = 2 * n + s
                    mult(i, s, 0)
                    mult(i, s, 1)
                    if not (last and s == 1):
                        xT_out(i + 1, 1 - s)
                    if not (first and s == 0):
                        y_out(i - 1, 1 - s, n + s - 1)

            xT_out(0, 0)
            pair(0, True, False)
            pair(1, False, False)
            with dve.Fori(2, TILES // 2 - 1) as n:
                pair(n, False, False)
            pair(TILES // 2 - 1, False, True)
            y_out(TILES - 1, 1, TILES // 2 - 1)


def kernel(x, L0_tok_gamma, L0_tok_beta, L0_tok_w, L0_tok_b, L0_attn_w_qkv, L0_attn_b_qkv, L0_attn_w_l,
           L0_attn_b_l, L0_attn_w_w, L0_attn_b_w, L0_attn_w_proj, L0_attn_b_proj, L0_ffn_router_w,
           L0_ffn_Wg, L0_ffn_Wu, L0_ffn_Wd):
    import numpy as np
    import concourse.bacc as bacc
    from concourse.bass_utils import run_bass_kernel_spmd

    def up(w):
        return np.ascontiguousarray(np.transpose(np.asarray(w).reshape(E * F, 2, CH), (2, 1, 0)))

    down = np.ascontiguousarray(np.transpose(np.asarray(L0_ffn_Wd).reshape(E, C, F // 128, 128), (3, 0, 2, 1))).reshape(128, -1)
    arrays = {
        "x": x, "gamma": L0_tok_gamma, "beta": L0_tok_beta, "tok_w": L0_tok_w, "tok_b": L0_tok_b,
        "w_qkv": L0_attn_w_qkv, "b_qkv": L0_attn_b_qkv, "w_l": L0_attn_w_l, "b_l": L0_attn_b_l,
        "w_w": L0_attn_w_w, "b_w": L0_attn_b_w, "w_proj": L0_attn_w_proj, "b_proj": L0_attn_b_proj,
        "router_wT": np.ascontiguousarray(np.asarray(L0_ffn_router_w).T),
        "WgT": up(L0_ffn_Wg), "WuT": up(L0_ffn_Wu), "WdT": down,
    }
    arrays = {name: np.ascontiguousarray(a) for name, a in arrays.items()}
    nc = bacc.Bacc("TRN2", target_bir_lowering=False, num_devices=1)
    ins = [nc.dram_tensor(name, a.shape, mybir.dt.from_np(a.dtype), kind="ExternalInput").ap() for name, a in arrays.items()]
    out = nc.dram_tensor("out", (T + 128, C), F32, kind="ExternalOutput").ap()
    xs = nc.dram_tensor("xs", (B * N, XW), F32, kind="Internal").ap()
    who = nc.dram_tensor("who", (SLOTS, 2), U32, kind="Internal").ap()
    n_rows = nc.dram_tensor("n_rows", (T + 128, C), F32, kind="Internal").ap()
    build(nc, *ins, out, xs, who, n_rows)
    r = run_bass_kernel_spmd(nc, [arrays], core_ids=[0])
    return r.results[0]["out"][:T].reshape(B, KEEP, C)
```

```python
import concourse.bass as bass
from concourse import mybir
from contextlib import ExitStack

F32 = mybir.dt.float32
F32R = mybir.dt.float32r
U32 = mybir.dt.uint32
I32 = mybir.dt.int32
ALU = mybir.AluOpType
ACT = mybir.ActivationFunctionType
AX = mybir.AxisListType

B, N, C = 32, 375, 192
KEEP = int(N * 0.7)
H, D = 12, 16
E, F = 8, 768
EPS = 1e-5
SCALE = D ** -0.5

TPP = 3
NP = N // TPP
XW = C + 2
GROUPS = 8
BG = B // GROUPS
STAT = BG * TPP
X_RING = 4

TILE = 88
SIZES = [TILE, TILE, KEEP - 2 * TILE]
CH = C // 2

ROWS = H * KEEP
RT = -(-ROWS // 128)
P_RING = 5
CA = 128
CB = C - CA
DUP = CA + 2 * CB

LAG_T, LAG_LO, LAG_AV, LAG_ACC = 3, 3, 4, 5


def rows_of(r):
    return min(128, ROWS - 128 * r)


def last_tile(h):
    return (KEEP * (h + 1) - 1) // 128


def last_head(r):
    return (128 * r + rows_of(r) - 1) // KEEP


def before(r, ring):
    if r >= ring:
        return r - ring + 1
    return max(q for q in range(RT) if q % ring == r % ring) + 1 - RT


HEAD_PARTS = [(h, 0, h * D) for h in range(CA // D)] + \
    [(h, 1, h * D - CA + twice) for h in range(CA // D, H) for twice in (0, CB)]
W_LOADS = 9 + 8 + 3 * len(HEAD_PARTS)

BL_PARTS = [(g, r, max(g * KEEP - 128 * r, 0), min((g + 1) * KEEP - 128 * r, 128))
            for g in range(H) for r in range(g * KEEP // 128, last_tile(g) + 1)]

T = B * KEEP
REGION = -(-T // 128) * 128
TILES = (2 * T + E * 127) // 128
TILES += TILES % 2
SLOTS = -(-(E * REGION + (TILES + 2) * 128) // 128 ** 2) * 128 ** 2
HF = F // 2


def build(nc, x, gamma, beta, tok_w, tok_b, w_qkv, b_qkv, w_l, b_l, w_w, b_w, w_proj, b_proj,
          router_wT, WgT, WuT, WdT, out, xs, who, n_rows):
    outer = ExitStack()
    with outer:
        outer.enter_context(nc.allow_non_contiguous_dma(reason="biases and slot numbers"))

        def sem(name):
            return outer.enter_context(nc.semaphore(name))

        def alloc(ctx, name, shape, dt=F32):
            return ctx.enter_context(nc.sbuf_tensor(name, shape, dt))

        def sb(name, shape, dt=F32):
            return alloc(outer, name, shape, dt)

        bank = [outer.enter_context(nc.psum_tensor(f"bank{i}", [128, 512], F32)) for i in range(8)]

        ident = sb("ident", [128, 128])
        ones = sb("ones", [128, 128])
        upper = sb("upper", [TILE, TILE])
        iota8 = sb("iota8", [TILE, 3, E])
        valid = sb("valid", [TILE, 3, E])
        run = sb("run", [TILE, E])
        pair_e = sb("pair_e", [1, TILES // 2 + 1], I32)
        tile_at = sb("tile_at", [1, TILES + 2], I32)

        att = ExitStack()
        w_raw = alloc(att, "w_raw", [128, 2, 3 * C])
        wq = alloc(att, "wq", [128, 4, 2 * DUP + C], F32R)
        bqk = alloc(att, "bqk", [128, 4])
        bv = alloc(att, "bv", [TILE, C])
        wl = alloc(att, "wl", [128, 2, H])
        bl = alloc(att, "bl", [128, RT])
        ww = alloc(att, "ww", [128, 2, H])
        bw = alloc(att, "bw", [128, 2])
        wp = alloc(att, "wp", [128, 2, C])
        bp = alloc(att, "bp", [TILE, C])
        rw = alloc(att, "rw", [CH, 2, E])
        half = alloc(att, "half", [TILE, 3])
        nobody = alloc(att, "nobody", [128, SLOTS // 128, 2], U32)
        blank = alloc(att, "blank", [128, DUP])
        idc = alloc(att, "idc", [TILE, 3])

        sel = ExitStack()
        xe = alloc(sel, "xe", [NP, B * TPP * XW])
        xe4 = xe[:].rearrange("p (b t w) -> p b t w", b=B, t=TPP)
        gw = alloc(sel, "gw", [NP, C])
        gtmp = alloc(sel, "gtmp", [NP, 2, C])
        c0 = alloc(sel, "c0", [NP, 1])
        c1 = alloc(sel, "c1", [NP, 1])
        tb = alloc(sel, "tb", [NP, 1])
        stats = alloc(sel, "stats", [NP, STAT, 6])
        mv = alloc(sel, "mv", [NP, STAT, 2])
        junk = alloc(sel, "junk", [NP, STAT, N])
        dots = alloc(sel, "dots", [NP, STAT])
        score = alloc(sel, "score", [NP, B * TPP])
        var = alloc(sel, "var", [NP, B * TPP])
        r0 = alloc(sel, "r0", [NP, B * TPP])
        rr = alloc(sel, "rr", [NP, B * TPP])
        earlier = alloc(sel, "earlier", [NP, TPP, N])
        row0 = alloc(sel, "row0", [NP, B])
        sc_wide = alloc(sel, "sc_wide", [NP, 2, TPP, NP])
        x_out = alloc(sel, "x_out", [NP, X_RING, TPP, XW])
        above = alloc(sel, "above", [NP, X_RING, TPP])
        equal = alloc(sel, "equal", [NP, X_RING, TPP])
        place = alloc(sel, "place", [NP, X_RING, TPP], U32)
        sel.close()

        x_in = alloc(att, "x_in", [TILE, 3, XW])
        hn = alloc(att, "hn", [TILE, 3, DUP])
        hnT = alloc(att, "hnT", [128, 3, KEEP], F32R)
        qs = alloc(att, "qs", [128, 2, KEEP])
        kT = alloc(att, "kT", [128, 2 * 4 * KEEP], F32R)
        v = alloc(att, "v", [TILE, 3, C])
        vb = alloc(att, "vb", [128, 2])
        qh = alloc(att, "qh", [128, 3, ROWS], F32R)
        vs = alloc(att, "vs", [TILE, 3, 2 * CA + 4 * CB], F32R)
        q_full = alloc(att, "q_full", [128, 2, KEEP])
        nmax = alloc(att, "nmax", [128, RT])
        nbias = alloc(att, "nbias", [128, RT])
        zsum = alloc(att, "zsum", [128, RT])
        rz = alloc(att, "rz", [128, RT])
        prob = alloc(att, "prob", [128, P_RING, 3 * TILE])
        p_hi = alloc(att, "p_hi", [TILE, 3, ROWS], F32R)
        p_lo = alloc(att, "p_lo", [TILE, 3, ROWS], F32R)
        oT = alloc(att, "oT", [128, 2, KEEP])
        x_res = alloc(att, "x_res", [TILE, 3, C])
        hres = alloc(att, "hres", [TILE, 3, C])
        n2 = alloc(att, "n2", [TILE, 3, C])
        n2T = alloc(att, "n2T", [CH, 2, KEEP])
        st2 = alloc(att, "st2", [TILE, 3, 6])
        mv2 = alloc(att, "mv2", [TILE, 3, 2])
        ve = alloc(att, "ve", [TILE, 3])
        ra = alloc(att, "ra", [TILE, 3])
        rb = alloc(att, "rb", [TILE, 3])
        lg = alloc(att, "lg", [TILE, 3, E])
        mx = alloc(att, "mx", [TILE, 3, 8])
        ix = alloc(att, "ix", [TILE, 3, 8], U32)
        ixf = alloc(att, "ixf", [TILE, 3, 2])
        oh = alloc(att, "oh", [TILE, 2, 3, E])
        ohs = alloc(att, "ohs", [TILE, 3, E])
        dl = alloc(att, "dl", [TILE, 3])
        ed = alloc(att, "ed", [TILE, 3])
        ed1 = alloc(att, "ed1", [TILE, 3])
        pos = alloc(att, "pos", [TILE, 3, E])
        posm = alloc(att, "posm", [TILE, 2, 3, E])
        slots = alloc(att, "slots", [TILE, 3, 2])
        slot_u = alloc(att, "slot_u", [TILE, 2, 3], U32)
        who_out = alloc(att, "who_out", [TILE, 2, 3, 2], U32)
        att.close()

        ffn = ExitStack()
        wg = alloc(ffn, "wg", [128, 3 * E * F], F32R)
        wu = alloc(ffn, "wu", [128, 3 * E * F], F32R)
        wd = alloc(ffn, "wd", [128, E * (F // 128) * C])
        who_all = alloc(ffn, "who_all", [128, TILES * 2], U32)
        from_row = alloc(ffn, "from_row", [128, 2], U32)
        to_row = alloc(ffn, "to_row", [128, 2], U32)
        xg = alloc(ffn, "xg", [128, 2, DUP])
        x_hi = alloc(ffn, "x_hi", [128, 2, 2, 128], F32R)
        x_lo = alloc(ffn, "x_lo", [128, 2, 2, 128], F32R)
        stage = alloc(ffn, "stage", [128, 2, 2, F])
        sg = stage[:, 0, 0, :]
        hh = stage[:, 1]
        hT = stage[:, 0, 1, :].rearrange("p (a q) -> p a q", q=128)
        yo = alloc(ffn, "yo", [128, 2, C])
        cnt = alloc(ffn, "cnt", [TILE, E])
        cnti = alloc(ffn, "cnti", [TILE, E], I32)
        cntf = alloc(ffn, "cntf", [TILE, E])
        jump = alloc(ffn, "jump", [TILE, E])
        upto = alloc(ffn, "upto", [TILE, E])
        tix = alloc(ffn, "tix", [1, TILES + 2])
        ge = alloc(ffn, "ge", [1, TILES + 2])
        te = alloc(ffn, "te", [1, TILES + 2])
        ta = alloc(ffn, "ta", [1, TILES + 2])
        trio = alloc(ffn, "trio", [1, TILES // 2 + 1])
        base8 = alloc(ffn, "base8", [TILE, E])
        ffn.close()

        dve_passed, pool_passed = sem("dve_passed"), sem("pool_passed")
        pool_c = sem("pool_c")
        consts_ready = sem("consts_ready")
        x_loaded = [sem(f"x_loaded{g}") for g in range(GROUPS)]
        tokp_loaded = sem("tokp_loaded")
        dve_prep = sem("dve_prep")
        dve_stat = sem("dve_stat")
        var_ready, sqrt_ready, score_ready = sem("var_ready"), sem("sqrt_ready"), sem("score_ready")
        wide_ready, rows_ready, rows_used = sem("wide_ready"), sem("rows_ready"), sem("rows_used")
        xout_ready, place_ready = sem("xout_ready"), sem("place_ready")
        scattered = [sem(f"scattered{i}") for i in range(X_RING)]
        w_loaded = sem("w_loaded")
        bl_loaded = sem("bl_loaded")
        prep_ready = sem("prep_ready")
        x_in_loaded, x_in_used = sem("x_in_loaded"), sem("x_in_used")
        x_res_loaded, x_res_ready = sem("x_res_loaded"), sem("x_res_ready")
        hn_ready, hnT_psum, hnT_ready = sem("hn_ready"), sem("hnT_psum"), sem("hnT_ready")
        q_psum, qs_ready, k_psum, kT_ready = sem("q_psum"), sem("qs_ready"), sem("k_psum"), sem("kT_ready")
        v_psum, v_ready, vb_psum, vb_ready = sem("v_psum"), sem("v_ready"), sem("vb_psum"), sem("vb_ready")
        vhi_ready, vlo_ready = sem("vhi_ready"), sem("vlo_ready")
        qh_hi, qh_lo_a, qh_lo_b = sem("qh_hi"), sem("qh_lo_a"), sem("qh_lo_b")
        bq_ready, q_full_ready = sem("bq_ready"), sem("q_full_ready")
        w_hi_ready, w_lo_ready, hnT_hi, kT_hi = sem("w_hi_ready"), sem("w_lo_ready"), sem("hnT_hi"), sem("kT_hi")
        s_psum, max_done, bias_ready = sem("s_psum"), sem("max_done"), sem("bias_ready")
        exp_done, rz_ready, prob_ready = sem("exp_done"), sem("rz_ready"), sem("prob_ready")
        t_psum, p_hi_ready, p_lo_ready = sem("t_psum"), sem("p_hi_ready"), sem("p_lo_ready")
        u_psum, acc_done = sem("u_psum"), sem("acc_done")
        proj_psum, hres_ready, n2_ready = sem("proj_psum"), sem("hres_ready"), sem("n2_ready")
        ve_ready, pow_ready = sem("ve_ready"), sem("pow_ready")
        n2T_psum, n2T_ready, router_psum = sem("n2T_psum"), sem("n2T_ready"), sem("router_psum")
        oh_ready, pos_psum, pos_used = sem("oh_ready"), sem("pos_psum"), sem("pos_used")
        dl_ready, ed_ready = sem("dl_ready"), sem("ed_ready")
        slots_ready, ids_sent = sem("slots_ready"), sem("ids_sent")
        blank_ready = sem("blank_ready")
        ids_zeroed, ids_free = sem("ids_zeroed"), sem("ids_free")
        dve_post, dve_route, dve_slot = sem("dve_post"), sem("dve_route"), sem("dve_slot")
        h_stored, n_stored = sem("h_stored"), sem("n_stored")
        att_over = sem("att_over")
        wd_loaded = sem("wd_loaded")
        stage_loaded = [sem("gate_loaded"), sem("up_loaded")]
        stage_hi, split_done = sem("stage_hi"), [sem("gate_split"), sem("up_split")]
        x_hi_ready = sem("x_hi_ready")
        tab_ready = sem("tab_ready")
        dve_tab = sem("dve_tab")
        who_loaded = [sem(f"who_loaded{i}") for i in range(2)]
        index_ready = sem("index_ready")
        added = sem("added")
        xg_loaded = [sem(f"xg_loaded{i}") for i in range(2)]
        xgT_psum, x_lo_ready = sem("xgT_psum"), sem("x_lo_ready")
        gu_psum, silu_done, hh_ready = sem("gu_psum"), sem("silu_done"), sem("hh_ready")
        hT_psum, hT_ready, y_psum, y_ready = sem("hT_psum"), sem("hT_ready"), sem("y_psum"), sem("y_ready")
        block = outer.enter_context(nc.Block())

        class Chain:

            def __init__(self, eng, signal, per):
                self.eng, self.sem, self.per, self.n, self.base = eng, signal, per, 0, 0

            def start(self, n):
                self.base, self.n = n * self.per, 0

            def mark(self, ins):
                self.n += 1
                ins.then_inc(self.sem, 1)

            def sync(self, apart=None):
                if apart is not None:
                    wait_apart(self.eng, self.sem, self.base + self.n, apart)
                else:
                    self.eng.wait_ge(self.sem, self.base + self.n)

            def link(self, ins):
                self.mark(ins)
                self.sync()

            def end(self):
                assert self.n == self.per, (self.n, self.per)

        def wait_apart(eng, signal, value, passed):
            eng.wait_ge(signal, value)
            eng.sem_inc(passed, 1)

        def wait(eng, signal, value):
            if not isinstance(value, int) or value > 0:
                eng.wait_ge(signal, value)

        def batches(eng, body):
            body(0, False, True, True)
            with eng.Fori(1, B - 1) as b:
                body(b, True, True, True)
            body(B - 1, True, True, False)
            body(B, True, False, False)

        def w_blocks(j):
            pairs = []
            for i in range(2):
                pairs.append((lambda w, c=i * DUP: w[:, c:c + CA], w_raw[:, j, i * C:i * C + CA]))
                pairs.append((lambda w, c=i * DUP + CA: w[:, c:c + 2 * CB].rearrange("p (a q) -> p a q", a=2),
                              w_raw[:, j, i * C + CA:i * C + C].unsqueeze(1).to_broadcast([128, 2, CB])))
            pairs.append((lambda w: w[:, 2 * DUP:2 * DUP + C], w_raw[:, j, 2 * C:3 * C]))
            return pairs

        def tok_rows(b, t):
            return bass.ds(b * KEEP + TILE * t, SIZES[t])

        PROJ, N2T, ROUTE, POS = 7, 14, 16, 21
        HN, HNT, QQ, KK, VV, VB = 0, 1, 3, 5, 9, 12

        def lagging(b, r, lag, prev, this):
            if r >= lag:
                return [(b, r - lag)] if this else []
            return [(b - 1, r - lag + RT)] if prev else []

        def head_slot(g):
            return max(last_tile(g) + 1, QQ + 4 + g)

        def lagging_heads(b, r, lag, prev, this):
            return [(bb, h, j) for j in range(2) for bb, q in lagging(b, r, lag + j, prev, this)
                    for h in range(H) if last_tile(h) == q]

        @block.sync
        def _(sp):
            sp.sem_inc(h_stored, 32)
            sp.sem_inc(n_stored, 64)
            xv = x.rearrange("b (p t) c -> p b t c", t=TPP)
            for g in range(GROUPS):
                for b in range(g * BG, g * BG + BG):
                    sp.dma_start(xe4[:, b, :, 0:C], xv[:, b]).then_inc(x_loaded[g], 16)
            half_rows = w_proj[CA:C, :]
            for dst, src in ((w_raw[:, 0, :], w_qkv[0:CA, :]), (w_raw[0:CB, 1, :], w_qkv[CA:C, :]),
                             (w_raw[CB:CA, 1, :], w_qkv[CA:C, :]),
                             (wp[:, 0, :], w_proj[0:CA, :]), (wp[0:CB, 1, :], half_rows), (wp[CB:CA, 1, :], half_rows),
                             (rw[:], router_wT.rearrange("(j p) n -> p j n", p=CH)),
                             (bv[:], b_qkv[2 * C:3 * C].partition_broadcast(TILE)),
                             (bp[:], b_proj.partition_broadcast(TILE))):
                sp.dma_start(dst, src).then_inc(w_loaded, 16)
            for i in range(2):
                for p, j, c in ((0, 0, 0), (CB, 0, CB), (0, 1, CA), (CB, 1, CA)):
                    sp.dma_start(bqk[p:p + CB, 2 * i + j:2 * i + j + 1],
                                 b_qkv[i * C + c:i * C + c + CB].rearrange("(p o) -> p o", o=1)).then_inc(w_loaded, 16)
            for hd, j, p in HEAD_PARTS:
                sp.dma_start(wl[p:p + D, j, :], w_l[hd].partition_broadcast(D)).then_inc(w_loaded, 16)
                sp.dma_start(ww[p:p + D, j, :], w_w[:, hd].partition_broadcast(D)).then_inc(w_loaded, 16)
                sp.dma_start(bw[p:p + D, j:j + 1], b_w[hd:hd + 1].partition_broadcast(D)).then_inc(w_loaded, 16)
            for g, r, lo, hi in BL_PARTS:
                sp.dma_start(bl[lo:hi, r:r + 1], b_l[g:g + 1].partition_broadcast(hi - lo)).then_inc(bl_loaded, 16)
            sp.wait_ge(blank_ready, 1)
            sp.dma_start(who.rearrange("(p n) o -> p n o", p=128), nobody[:]).then_inc(ids_zeroed, 16)
            sp.dma_start(n_rows[T:T + 128, :], blank[:]).then_inc(ids_zeroed, 16)
            sp.dma_start(out[T:T + 128, :], blank[:, 0:C]).then_inc(ids_zeroed, 16)

            def load_x(b):
                sp.dma_start(x_in[:, 0:2, :], xs[bass.ds(b * N, 2 * TILE), :].rearrange("(t p) w -> p t w", p=TILE)).then_inc(x_in_loaded, 16)
                sp.dma_start(x_in[0:SIZES[2], 2, :], xs[bass.ds(b * N + 2 * TILE, SIZES[2]), :]).then_inc(x_in_loaded, 16)

            def load_res(b):
                sp.dma_start(x_res[:, 0:2, :], xs[bass.ds(b * N, 2 * TILE), 0:C].rearrange("(t p) w -> p t w", p=TILE)).then_inc(x_res_loaded, 16)
                sp.dma_start(x_res[0:SIZES[2], 2, :], xs[bass.ds(b * N + 2 * TILE, SIZES[2]), 0:C]).then_inc(x_res_loaded, 16)

            def store(b):
                sp.wait_ge(hres_ready, b + 1)
                sp.dma_start(out[bass.ds(b * KEEP, 2 * TILE), :].rearrange("(t p) w -> p t w", p=TILE), hres[:, 0:2, :]).then_inc(h_stored, 16)
                sp.dma_start(out[tok_rows(b, 2), :], hres[0:SIZES[2], 2, :]).then_inc(h_stored, 16)
                sp.wait_ge(n2_ready, b + 1)
                for c, src in ((slice(0, C), slice(0, C)), (slice(C, DUP), slice(CA, C))):
                    sp.dma_start(n_rows[bass.ds(b * KEEP, 2 * TILE), c].rearrange("(t p) w -> p t w", p=TILE), n2[:, 0:2, src]).then_inc(n_stored, 16)
                    sp.dma_start(n_rows[tok_rows(b, 2), c], n2[0:SIZES[2], 2, src]).then_inc(n_stored, 16)

            for s in range(X_RING):
                sp.wait_ge(scattered[s], 16 * TPP * (B // X_RING))
            load_x(0)

            def body(b, prev, this, nxt):
                if nxt:
                    sp.wait_ge(x_in_used, b + 1)
                    load_x(b + 1)
                if prev:
                    store(b - 1)
                if this:
                    load_res(b)

            batches(sp, body)

            sp.wait_ge(att_over, 4)
            sp.wait_ge(n_stored, 64 * B + 64)
            sp.wait_ge(h_stored, 32 * B + 32)

            def load_expert(e, k):
                for dst, c, rows in ((stage[:, k, 0, :], 0, CA), (stage[0:CB, k, 1, :], CA, CB), (stage[CB:CA, k, 1, :], CA, CB)):
                    sp.dma_start(dst, (WgT, WuT)[k][c:c + rows, bass.ds(e * F, F)]).then_inc(stage_loaded[k], 16)

            for k in range(2):
                load_expert(0, k)
            sp.dma_start(wd[:], WdT).then_inc(wd_loaded, 16)
            with sp.Fori(1, E) as e:
                for k in range(2):
                    sp.wait_ge(split_done[k], e)
                    load_expert(e, k)
            sp.wait_ge(tab_ready, 1)
            sp.wait_ge(ids_sent, 16 * 6 * B)

            def load_who(i, s, n):
                at = sp.value_load(tile_at[0:1, bass.ds(i, 1)], min_val=0, max_val=SLOTS - 128)
                if not isinstance(n, int):
                    sp.wait_ge(who_loaded[s], 16 * n)
                sp.dma_start(who_all[:, bass.ds(2 * i, 2)], who[bass.ds(at, 128), :]).then_inc(who_loaded[s], 16)

            for s in range(2):
                load_who(s, s, 0)
            with sp.Fori(1, TILES // 2) as n:
                for s in range(2):
                    load_who(2 * n + s, s, n)
            sp.wait_ge(added, 16 * TILES)

        @block.gpsimd
        def _(pool):
            for dst, src in ((gtmp[:, 0], gamma), (gtmp[:, 1], beta), (gw[:], tok_w), (tb[:], tok_b)):
                pool.dma_start(dst, src.partition_broadcast(NP)).then_inc(tokp_loaded, 16)
            ch = Chain(pool, pool_c, 0)
            ch.link(pool.memset(ident[:], 0.0))
            ch.link(pool.affine_select(out=ident[:], in_=ident[:], compare_op=ALU.not_equal, fill=1.0, base=0,
                                       pattern=[[-1, 128]], channel_multiplier=1))
            ch.link(pool.memset(ones[:], 1.0))
            ch.link(pool.affine_select(out=upper[:], in_=ones[0:TILE, 0:TILE], compare_op=ALU.is_gt, fill=0.0,
                                       base=0, pattern=[[1, TILE]], channel_multiplier=-1))
            ch.link(pool.iota(iota8[:], pattern=[[0, 3], [1, E]], base=0, channel_multiplier=0,
                              allow_small_or_imprecise_dtypes=True))
            ch.link(pool.memset(valid[:], 1.0))
            ch.link(pool.affine_select(out=valid[:], in_=valid[:], compare_op=ALU.is_gt, fill=0.0, base=KEEP,
                                       pattern=[[-TILE, 3], [0, E]], channel_multiplier=-1))
            ch.link(pool.iota(run[:], pattern=[[REGION, E]], base=0, channel_multiplier=0,
                              allow_small_or_imprecise_dtypes=True))
            ch.link(pool.memset(earlier[:], 1.0))
            for t in range(TPP):
                ch.link(pool.affine_select(out=earlier[:, t, :].rearrange("p (a q) -> p a q", a=TPP),
                                           in_=earlier[:, t, :].rearrange("p (a q) -> p a q", a=TPP),
                                           compare_op=ALU.is_gt, fill=0.0, base=t,
                                           pattern=[[-1, TPP], [-TPP, NP]], channel_multiplier=TPP))
            ch.link(pool.iota(row0[:], pattern=[[N, B]], base=0, channel_multiplier=0,
                              allow_small_or_imprecise_dtypes=True))
            pool.sem_inc(consts_ready, 1)
            ch.link(pool.memset(half[:], -0.5))
            ch.link(pool.iota(nobody[:, :, 0].rearrange("p (a q) -> p a q", q=128), pattern=[[0, SLOTS // 128 // 128], [1, 128]], base=T, channel_multiplier=0))
            ch.link(pool.memset(nobody[:, :, 1], 0))
            ch.link(pool.memset(blank[:], 0.0))
            ch.link(pool.iota(idc[:], pattern=[[TILE, 3]], base=0, channel_multiplier=1,
                              allow_small_or_imprecise_dtypes=True))
            pool.sem_inc(blank_ready, 1)

            with pool.Fori(0, B // X_RING) as i:
                for s in range(X_RING):
                    pool.wait_ge(place_ready, X_RING * i + s + 1)
                    wait_apart(pool, xout_ready, X_RING * i + s + 1, pool_passed)
                    for t in range(TPP):
                        pool.indirect_dma_start(out=xs, out_offset=bass.IndirectOffsetOnAxis(ap=place[:, s, t:t + 1], axis=0),
                                                in_=x_out[:, s, t, :], in_offset=None).then_inc(scattered[s], 16)
            for s in range(X_RING):
                pool.wait_ge(scattered[s], 16 * TPP * (B // X_RING))
            ch.link(pool.memset(hres[:], 0.0))
            ch.link(pool.memset(n2[:], 0.0))
            ch.link(pool.memset(lg[:], 0.0))
            ch.link(pool.memset(v[:], 0.0))
            ch.link(pool.memset(vb[:], 0.0))
            ch.link(pool.memset(vs[:].bitcast(F32), 0.0))
            ch.link(pool.memset(prob[:], 0.0))
            pool.sem_inc(prep_ready, 1)

            def v_lo(b):
                pool.wait_ge(vhi_ready, 2 * b + 1)
                pool.tensor_tensor(vs[:, :, CA:2 * CA], v[:, :, 0:CA], vs[:, :, 0:CA].bitcast(F32), ALU.subtract).then_inc(vlo_ready, 1)
                pool.wait_ge(vhi_ready, 2 * b + 2)
                pool.tensor_tensor(vs[:, :, 2 * CA + CB:2 * CA + 2 * CB], v[:, :, CA:C],
                                   vs[:, :, 2 * CA:2 * CA + CB].bitcast(F32), ALU.subtract).then_inc(vlo_ready, 1)
                pool.wait_ge(vlo_ready, 2 * b + 2)

            def q_lo(b, g):
                wait_apart(pool, qh_hi, b * H + g + 1, pool_passed)
                at = slice(g * KEEP, (g + 1) * KEEP)
                pool.tensor_scalar(q_full[CB:CA, g % 2, :], qs[CB:CA, 1, :], wl[CB:CA, 1, g:g + 1], None, ALU.mult).then_inc(q_full_ready, 1)
                pool.wait_ge(q_full_ready, b * H + g + 1)
                pool.tensor_tensor(qh[CB:CA, 2, at], q_full[CB:CA, g % 2, :], qh[CB:CA, 2, at].bitcast(F32), ALU.subtract).then_inc(qh_lo_b, 1)
                pool.wait_ge(qh_lo_b, b * H + g + 1)

            def residual(b):
                pool.wait_ge(x_res_loaded, 32 * b + 32)
                for t in range(3):
                    n = SIZES[t]
                    ins = pool.tensor_tensor(x_res[0:n, t, :], x_res[0:n, t, :], bp[0:n, :], ALU.add)
                ins.then_inc(x_res_ready, 1)
                pool.wait_ge(x_res_ready, b + 1)

            def inv_std(b):
                pool.wait_ge(ve_ready, b + 1)
                pool.tensor_tensor(ra[:], ve[:], half[:], ALU.pow).then_inc(pow_ready, 1)
                pool.wait_ge(pow_ready, b + 1)

            def send_ids(b):
                wait_apart(pool, slots_ready, b + 1, pool_passed)
                for t in range(3):
                    n = SIZES[t]
                    for k in range(2):
                        pool.indirect_dma_start(out=who, out_offset=bass.IndirectOffsetOnAxis(ap=slot_u[0:n, k, t:t + 1], axis=0),
                                                in_=who_out[0:n, k, t, :], in_offset=None).then_inc(ids_sent, 16)

            def body(b, prev, this, nxt):
                def next_q_lo(heads):
                    if nxt:
                        for g in heads:
                            q_lo(b + 1, g)

                if this and prev:
                    q_lo(b, H - 1)
                if this:
                    v_lo(b)
                next_q_lo(range(3))
                if prev:
                    inv_std(b - 1)
                next_q_lo(range(3, 7))
                if this:
                    residual(b)
                next_q_lo(range(7, 10))
                next_q_lo(range(10, 11))
                if prev:
                    send_ids(b - 1)
                    pool.wait_ge(ids_sent, 16 * 6 * b)
                    pool.sem_inc(ids_free, 1)

            pool.wait_ge(ids_zeroed, 48)
            pool.sem_inc(ids_free, 1)
            for g in range(H):
                q_lo(0, g)
            batches(pool, body)
            pool.wait_ge(ids_sent, 16 * 6 * B)
            pool.sem_inc(att_over, 1)
            pool.wait_ge(att_over, 4)

            ch.link(pool.iota(tix[:], pattern=[[1, TILES + 2]], base=0, channel_multiplier=0,
                              allow_small_or_imprecise_dtypes=True))
            ch.link(pool.iota(base8[:], pattern=[[REGION, E]], base=0, channel_multiplier=0,
                              allow_small_or_imprecise_dtypes=True))
            pool.sem_inc(prep_ready, 1)

            def gather(i, s, n):
                pool.wait_ge(who_loaded[s], 16 * n + 16)
                wait(pool, xgT_psum, i - 1)
                pool.tensor_copy(from_row[:, s:s + 1], who_all[:, bass.ds(2 * i, 1)]).then_inc(index_ready, 1)

            def gather_go(i, s, n):
                pool.indirect_dma_start(out=xg[:, s, :], out_offset=None, in_=n_rows,
                                        in_offset=bass.IndirectOffsetOnAxis(ap=from_row[:, s:s + 1], axis=0)).then_inc(xg_loaded[s], 16)

            def add(i, s):
                wait(pool, added, 16 * i)
                pool.tensor_copy(to_row[:, s:s + 1], who_all[:, bass.ds(2 * i, 1)]).then_inc(index_ready, 1)

            def add_go(i, s):
                pool.indirect_dma_start(out=out, out_offset=bass.IndirectOffsetOnAxis(ap=to_row[:, s:s + 1], axis=0),
                                        in_=yo[:, s, :], in_offset=None, compute_op=ALU.add).then_inc(added, 16)

            def step(i, s, n):
                gather(i, s, n)
                wait_apart(pool, index_ready, 2 * i - 2, pool_passed)
                gather_go(i, s, n)
                add(i - 3, 1 - s)
                pool.wait_ge(index_ready, 2 * i - 1)
                wait_apart(pool, y_ready, i - 2, pool_passed)
                add_go(i - 3, 1 - s)

            for i in range(3):
                gather(i, i % 2, i // 2)
                wait_apart(pool, index_ready, i + 1, pool_passed)
                gather_go(i, i % 2, i // 2)
            step(3, 1, 1)
            with pool.Fori(2, TILES // 2) as n:
                for s in range(2):
                    step(2 * n + s, s, n)
            for i in range(TILES - 3, TILES):
                add(i, i % 2)
                pool.wait_ge(index_ready, TILES + i + 1)
                wait_apart(pool, y_ready, i + 1, pool_passed)
                add_go(i, i % 2)

        @block.scalar
        def _(act):
            act.wait_ge(var_ready, 1)
            nc.scalar.activation(r0[:], var[:], ACT.Sqrt).then_inc(sqrt_ready, 1)
            act.wait_ge(score_ready, 1)

            def spread(i, first=False):
                for s in range(X_RING):
                    b = X_RING * i + s
                    act.wait_ge(rows_ready, b + 1)
                    src = score[:, bass.ds(b * TPP, TPP)].unsqueeze(2).to_broadcast([NP, TPP, NP])
                    nc.scalar.activation(sc_wide[:, s % 2], src, ACT.Copy).then_inc(wide_ready, 1)
                    if not first:
                        act.wait_ge(scattered[s], 16 * TPP * i)
                    nc.scalar.activation(x_out[:, s].rearrange("p t w -> p (t w)"), xe[:, bass.ds(b * TPP * XW, TPP * XW)],
                                         ACT.Copy).then_inc(xout_ready, 1)

            spread(0, True)
            with act.Fori(1, B // X_RING) as i:
                spread(i)
            act.wait_ge(prep_ready, 1)

            def hnT_out(b):
                act.wait_ge(hnT_psum, b + 1)
                for j in range(2):
                    ins = nc.scalar.activation(hnT[:, 2 * j, :], bank[6 + j][:, 0:KEEP], ACT.Copy)
                ins.then_inc(hnT_hi, 1)

            def q_out(b):
                act.wait_ge(q_psum, b + 1)
                wait(act, qh_lo_a, b * H)
                wait(act, qh_lo_b, b * H)
                for j in range(2):
                    ins = nc.scalar.activation(qs[:, j, :], bank[6 + j][:, 0:KEEP], ACT.Identity, bias=bqk[:, j:j + 1], scale=SCALE)
                ins.then_inc(qs_ready, 1)

            def k_out(b):
                act.wait_ge(k_psum, b + 1)
                for j in range(2):
                    ins = nc.scalar.activation(kT[:, bass.ds((b & 1) * 4 * KEEP + 2 * j * KEEP, KEEP)], bank[6 + j][:, 0:KEEP],
                                               ACT.Identity, bias=bqk[:, 2 + j:3 + j])
                ins.then_inc(kT_hi, 1)

            def row_scale(b, r):
                n = rows_of(r)
                act.wait_ge(rz_ready, b * RT + r + 1)
                nc.scalar.activation(prob[0:n, r % P_RING, 0:KEEP], prob[0:n, r % P_RING, 0:KEEP], ACT.Copy,
                                     scale=rz[0:n, r:r + 1]).then_inc(prob_ready, 1)

            def n2T_out(b):
                act.wait_ge(n2T_psum, b + 1)
                for j in range(2):
                    ins = nc.scalar.activation(n2T[:, j, :], bank[6 + j][0:CH, 0:KEEP], ACT.Copy)
                ins.then_inc(n2T_ready, 1)

            def q_head(b, g):
                for j in range(2):
                    ins = nc.scalar.activation(qh[:, 2 * j, g * KEEP:(g + 1) * KEEP], qs[:, j, :], ACT.Copy,
                                               scale=wl[:, j, g:g + 1])
                ins.then_inc(qh_hi, 1)

            def exp_out(b, r):
                n = rows_of(r)
                act.wait_ge(bias_ready, b * RT + r + 1)
                wait(act, t_psum, b * RT + before(r, P_RING))
                nc.scalar.activation(prob[0:n, r % P_RING, 0:KEEP], bank[r % 2][0:n, 0:KEEP], ACT.Exp,
                                     bias=nbias[0:n, r:r + 1], accum_out=zsum[0:n, r:r + 1]).then_inc(exp_done, 1)

            def p_hi_out(b, r):
                n = rows_of(r)
                act.wait_ge(t_psum, b * RT + r + 1)
                nc.scalar.activation(p_hi[:, :, 128 * r:128 * r + n],
                                     bank[2 + r % 2][0:TILE, 0:384].rearrange("p (t q) -> p t q", t=3)[:, :, 0:n],
                                     ACT.Copy).then_inc(p_hi_ready, 1)

            def v_hi_a(b):
                act.wait_ge(v_ready, b + 1)
                wait(act, u_psum, b * 2 * H - 1)
                nc.scalar.activation(vs[:, :, 0:CA], v[:, :, 0:CA], ACT.Copy).then_inc(vhi_ready, 1)

            def v_hi_b(b):
                wait(act, u_psum, b * 2 * H)
                nc.scalar.activation(vs[:, :, 2 * CA:2 * CA + CB], v[:, :, CA:C], ACT.Copy)
                nc.scalar.activation(vs[:, :, 2 * CA + 2 * CB:2 * CA + 3 * CB], v[:, :, CA:C], ACT.Copy).then_inc(vhi_ready, 1)

            def soft2(b):
                act.wait_ge(dl_ready, b + 1)
                nc.scalar.activation(ed[:], dl[:], ACT.Exp).then_inc(ed_ready, 1)

            def body(b, prev, this, nxt):
                for r in range(RT):
                    if nxt and r == HNT + 1:
                        hnT_out(b + 1)
                    if nxt and r == QQ + 1:
                        q_out(b + 1)
                    if nxt and r == KK + 1:
                        k_out(b + 1)
                    if prev and r == N2T + 1:
                        n2T_out(b - 1)
                    if prev and r == ROUTE + 4:
                        soft2(b - 1)
                    for bb, q in lagging(b, r, LAG_T, prev, this):
                        p_hi_out(bb, q)
                    if this:
                        exp_out(b, r)
                    for bb, q in lagging(b, r, 1, prev, this):
                        row_scale(bb, q)
                    if this and r == LAG_AV:
                        v_hi_a(b)
                    if this and r == LAG_AV + 1:
                        v_hi_b(b)
                    for g in [g for g in range(H) if nxt and head_slot(g) == r]:
                        if g == 0:
                            act.wait_ge(qs_ready, b + 2)
                        act.wait_ge(s_psum, b * RT + last_tile(g) + 1)
                        q_head(b + 1, g)
                    if this and r == 0 and prev:
                        act.wait_ge(s_psum, b * RT)
                        q_head(b, H - 1)

            act.wait_ge(w_loaded, 16 * W_LOADS)
            act.wait_ge(bq_ready, 1)
            for j in range(2):
                for dst, src in w_blocks(j):
                    ins = nc.scalar.activation(dst(wq[:, 2 * j]), src, ACT.Copy)
            ins.then_inc(w_hi_ready, 1)
            hnT_out(0)
            q_out(0)
            k_out(0)
            act.wait_ge(qs_ready, 1)
            for g in range(H):
                q_head(0, g)

            batches(act, body)
            act.wait_ge(n2T_ready, B)
            act.sem_inc(att_over, 1)
            act.wait_ge(att_over, 4)

            with act.Fori(0, E) as e:
                for k, w in enumerate((wg, wu)):
                    act.wait_ge(stage_loaded[k], 48 * e + 48)
                    for j in range(2):
                        ins = nc.scalar.activation(w[:, bass.ds(e * F + 2 * j * E * F, F)], stage[:, k, j, :], ACT.Copy)
                    ins.then_inc(stage_hi, 1)

            def x_hi_out(i, s):
                act.wait_ge(xgT_psum, i + 1)
                wait(act, gu_psum, 2 * i - 2)
                nc.scalar.activation(x_hi[:, s], bank[6][:, 0:256].rearrange("p (j q) -> p j q", j=2), ACT.Copy).then_inc(x_hi_ready, 1)

            def gate(i, k):
                act.wait_ge(gu_psum, 2 * i + k + 1)
                wait(act, hh_ready, 2 * i + k - 1)
                nc.scalar.activation(sg[:, k * HF:(k + 1) * HF], bank[2 * k][:, 0:HF], ACT.Silu).then_inc(silu_done, 1)

            def hT_out(i):
                act.wait_ge(hT_psum, i + 1)
                wait(act, y_psum, i)
                for k in range(2):
                    ins = nc.scalar.activation(hT[:, 3 * k:3 * k + 3, :], bank[4 + k][:, 0:384].rearrange("p (a q) -> p a q", a=3),
                                               ACT.Copy)
                ins.then_inc(hT_ready, 1)

            def pair(n, first, last):
                for s in range(2):
                    i = 2 * n + s
                    gate(i, 0)
                    if not (first and s == 0):
                        hT_out(i - 1)
                    gate(i, 1)
                    if not (last and s == 1):
                        x_hi_out(i + 1, 1 - s)

            x_hi_out(0, 0)
            pair(0, True, False)
            with act.Fori(1, TILES // 2 - 1) as n:
                pair(n, False, False)
            pair(TILES // 2 - 1, False, True)
            hT_out(TILES - 1)

        @block.tensor
        def _(pe):
            pe.sem_inc(rows_ready, 2)
            pe.wait_ge(consts_ready, 1)
            with pe.Fori(0, B // 2) as i:
                for s in range(2):
                    b = 2 * i + s
                    pe.wait_ge(wide_ready, b + 1)
                    pe.wait_ge(rows_used, b + 1)
                    for t in range(TPP):
                        ins = pe.transpose(bank[s][0:NP, t * NP:(t + 1) * NP], sc_wide[:, s, t, :], ident[0:NP, 0:NP])
                    ins.then_inc(rows_ready, 1)

            def hnT_in(b):
                pe.wait_ge(hn_ready, b + 1)
                wait(pe, pos_used, b - 1)
                for j in range(2):
                    for t in range(3):
                        n = SIZES[t]
                        ins = pe.transpose(bank[6 + j][:, TILE * t:TILE * t + n], hn[0:n, t, j * CA:(j + 1) * CA], ident[0:n, 0:n])
                ins.then_inc(hnT_psum, 1)

            HN_PRODUCTS = ((CA, 0, 0), (CA, 0, 1), (CA, 1, 0), (CA, 2, 2), (CB, 3, 2))

            def qk_in(b, which, signal):
                for c in range(2):
                    at = which * DUP + c * CA
                    for n, (rows, w, x) in enumerate(HN_PRODUCTS):
                        ins = pe.matmul(bank[6 + c][:, 0:KEEP], wq[0:rows, w, at:at + CA], hnT[0:rows, x, :],
                                        start=(n == 0), stop=(n == len(HN_PRODUCTS) - 1))
                ins.then_inc(signal, 1)

            def v_in(b):
                for t in range(3):
                    n = SIZES[t]
                    dst = bank[6 + t // 2][0:n, (t % 2) * C:(t % 2) * C + C]
                    for i, (rows, w, x) in enumerate(HN_PRODUCTS):
                        ins = pe.matmul(dst, hnT[0:rows, x, TILE * t:TILE * t + n], wq[0:rows, w, 2 * DUP:2 * DUP + C],
                                        start=(i == 0), stop=(i == len(HN_PRODUCTS) - 1))
                ins.then_inc(v_psum, 1)

            def vb_in(b):
                pe.wait_ge(v_ready, b + 1)
                for j, (c, m) in enumerate(((0, CA), (CA, CB))):
                    for t in range(3):
                        ins = pe.matmul(bank[6][0:m, j:j + 1], v[:, t, c:c + m], ones[0:TILE, 0:1], start=(t == 0), stop=(t == 2))
                ins.then_inc(vb_psum, 1)

            def scores(b, r):
                n = rows_of(r)
                if r == 0:
                    pe.wait_ge(kT_ready, b + 1)
                pe.wait_ge(qh_lo_a, b * H + last_head(r) + 1)
                pe.wait_ge(qh_lo_b, b * H + last_head(r) + 1)
                wait(pe, exp_done, b * RT + before(r, 2))
                products = ((CA, 0, 0), (CA, 1, 0), (CA, 0, 1), (CA, 2, 2), (CB, 2, 3))
                for i, (rows, q, k) in enumerate(products):
                    ins = pe.matmul(bank[r % 2][0:n, 0:KEEP], qh[0:rows, q, 128 * r:128 * r + n],
                                    kT[0:rows, bass.ds((b & 1) * 4 * KEEP + k * KEEP, KEEP)], start=(i == 0), stop=(i == len(products) - 1))
                ins.then_inc(s_psum, 1)

            def turn(b, r):
                n = rows_of(r)
                pe.wait_ge(prob_ready, b * RT + r + 1)
                wait(pe, p_lo_ready, b * RT + before(r, 2))
                for t in range(3):
                    ins = pe.transpose(bank[2 + r % 2][0:TILE, 128 * t:128 * t + n], prob[0:n, r % P_RING, TILE * t:TILE * t + TILE], ident[0:n, 0:n])
                ins.then_inc(t_psum, 1)

            def av(b, h, j):
                if h == 0:
                    pe.wait_ge(vlo_ready, 2 * b + j + 1)
                pe.wait_ge(p_lo_ready, b * RT + last_tile(h) + 1)
                at = slice(h * KEEP, (h + 1) * KEEP)
                hi_a, lo_a, hl_b, h0_b = (slice(c, c + CA) for c in range(0, 4 * CA, CA))
                products = (((hi_a, p_hi), (hi_a, p_lo), (lo_a, p_hi)), ((hl_b, p_hi), (h0_b, p_lo)))[j]
                wait(pe, acc_done, 2 * (b * H + h) + j - 1)
                for n, (part, p) in enumerate(products):
                    for t in range(3):
                        ins = pe.matmul(bank[4 + j][:, 0:KEEP], vs[:, t, part], p[:, t, at],
                                        start=(n == 0 and t == 0), stop=(n == len(products) - 1 and t == 2))
                ins.then_inc(u_psum, 1)

            def proj(b):
                pe.wait_ge(acc_done, 2 * H * (b + 1))
                for t in range(3):
                    n = SIZES[t]
                    dst = bank[6 + t // 2][0:n, (t % 2) * C:(t % 2) * C + C]
                    for k in range(2):
                        ins = pe.matmul(dst, oT[:, k, TILE * t:TILE * t + n], wp[:, k, :], start=(k == 0), stop=(k == 1))
                ins.then_inc(proj_psum, 1)

            def n2T_in(b):
                pe.wait_ge(n2_ready, b + 1)
                for j in range(2):
                    for t in range(3):
                        n = SIZES[t]
                        ins = pe.transpose(bank[6 + j][0:CH, TILE * t:TILE * t + n], n2[0:n, t, j * CH:(j + 1) * CH], ident[0:n, 0:n])
                ins.then_inc(n2T_psum, 1)

            def route_in(b):
                pe.wait_ge(n2T_ready, b + 1)
                for t in range(3):
                    n = SIZES[t]
                    for k in range(2):
                        ins = pe.matmul(bank[6][0:n, E * t:E * t + E], n2T[:, k, TILE * t:TILE * t + n], rw[:, k, :], start=(k == 0), stop=(k == 1))
                ins.then_inc(router_psum, 1)

            def pos_in(b):
                pe.wait_ge(oh_ready, b + 1)
                pe.matmul(bank[7][0:TILE, 0:3 * E], upper[:], ohs[:].rearrange("p t e -> p (t e)"), start=True, stop=True)
                pe.matmul(bank[7][0:TILE, 3 * E:6 * E], ones[0:TILE, 0:TILE], ohs[:].rearrange("p t e -> p (t e)"), start=True, stop=True).then_inc(pos_psum, 1)

            def body(b, prev, this, nxt):
                for r in range(RT):
                    if this:
                        scores(b, r)
                    for bb, q in lagging(b, r, LAG_T, prev, this):
                        turn(bb, q)
                    for bb, h, j in lagging_heads(b, r, LAG_AV, prev, this):
                        av(bb, h, j)
                    if nxt and r == HNT:
                        hnT_in(b + 1)
                    if nxt and r == QQ:
                        pe.wait_ge(hnT_ready, b + 2)
                        qk_in(b + 1, 0, q_psum)
                    if nxt and r == KK:
                        pe.wait_ge(qs_ready, b + 2)
                        qk_in(b + 1, 1, k_psum)
                    if prev and r == PROJ:
                        if nxt:
                            pe.wait_ge(kT_ready, b + 2)
                        proj(b - 1)
                    if nxt and r == VV:
                        if prev:
                            pe.wait_ge(hres_ready, b)
                        else:
                            pe.wait_ge(kT_ready, b + 2)
                        v_in(b + 1)
                    if nxt and r == VB:
                        vb_in(b + 1)
                    if prev and r == N2T:
                        if nxt:
                            pe.wait_ge(vb_ready, b + 2)
                        n2T_in(b - 1)
                    if prev and r == ROUTE:
                        route_in(b - 1)
                    if prev and r == POS:
                        pos_in(b - 1)

            pe.wait_ge(prep_ready, 1)
            pe.wait_ge(w_loaded, 16 * W_LOADS)
            hnT_in(0)
            pe.wait_ge(w_lo_ready, 1)
            pe.wait_ge(hnT_ready, 1)
            qk_in(0, 0, q_psum)
            pe.wait_ge(qs_ready, 1)
            qk_in(0, 1, k_psum)
            pe.wait_ge(kT_ready, 1)
            v_in(0)
            vb_in(0)
            pe.wait_ge(vb_ready, 1)

            batches(pe, body)
            pe.wait_ge(pos_psum, B)
            pe.sem_inc(att_over, 1)
            pe.wait_ge(att_over, 4)
            pe.wait_ge(tab_ready, 1)
            for k in range(2):
                pe.wait_ge(split_done[k], E)
            pe.wait_ge(wd_loaded, 16)

            def x_turn(i, s, n):
                pe.wait_ge(xg_loaded[s], 16 * n + 16)
                wait(pe, x_lo_ready, i)
                for j in range(2):
                    ins = pe.transpose(bank[6][:, 128 * j:128 * j + 128], xg[:, s, j * CA:(j + 1) * CA], ident[:])
                ins.then_inc(xgT_psum, 1)

            def gate_up(i, s, k, at):
                pe.wait_ge(x_lo_ready, i + 1)
                wait(pe, hh_ready, 2 * i + k - 1)
                products = ((CA, x_hi[:, s, 0], 0), (CA, x_lo[:, s, 0], 0), (CA, x_hi[:, s, 0], 1),
                            (CA, x_hi[:, s, 1], 2), (CB, x_lo[0:CB, s, 1], 2))
                for c, w in enumerate((wg, wu)):
                    for n, (rows, xT, tile) in enumerate(products):
                        ins = pe.matmul(bank[2 * k + c][:, 0:HF], xT, w[0:rows, bass.ds(at * F + tile * E * F + k * HF, HF)],
                                        start=(n == 0), stop=(n == len(products) - 1))
                ins.then_inc(gu_psum, 1)

            def h_turn(i, s):
                pe.wait_ge(hh_ready, 2 * i + 2)
                wait(pe, hT_ready, i)
                for c in range(F // 128):
                    ins = pe.transpose(bank[4 + c // 3][:, 128 * (c % 3):128 * (c % 3) + 128], hh[:, s, 128 * c:128 * c + 128], ident[:])
                ins.then_inc(hT_psum, 1)

            def down(i, at):
                pe.wait_ge(hT_ready, i + 1)
                wait(pe, y_ready, i)
                for c in range(F // 128):
                    ins = pe.matmul(bank[7][:, 0:C], hT[:, c, :], wd[:, bass.ds(at * (F // 128 * C) + c * C, C)],
                                    start=(c == 0), stop=(c == F // 128 - 1))
                ins.then_inc(y_psum, 1)

            def experts(n):
                three = pe.value_load(pair_e[0:1, bass.ds(n, 1)], min_val=0, max_val=E ** 3 - 1)
                return {-1: three & 7, 0: (three >> 3) & 7, 1: (three >> 6) & 7}

            def pair(n, first, last):
                at = experts(n)
                for s in range(2):
                    i = 2 * n + s
                    gate_up(i, s, 0, at[s])
                    if not (first and s == 0):
                        h_turn(i - 1, 1 - s)
                    gate_up(i, s, 1, at[s])
                    if not (last and s == 1):
                        x_turn(i + 1, 1 - s, n + s)
                    if not (first and s == 0):
                        down(i - 1, at[s - 1])

            x_turn(0, 0, 0)
            pair(0, True, False)
            with pe.Fori(1, TILES // 2 - 1) as n:
                pair(n, False, False)
            pair(TILES // 2 - 1, False, True)
            h_turn(TILES - 1, 1)
            down(TILES - 1, experts(TILES // 2)[-1])

        @block.vector
        def _(dve):
            dve.sem_inc(pos_used, 1)
            dve.sem_inc(rows_used, 2)
            ch = Chain(dve, dve_prep, 0)
            dve.wait_ge(tokp_loaded, 64)
            ch.link(dve.scalar_tensor_tensor(out=junk[:, 0, 0:C], in0=gtmp[:, 1], scalar=1.0, in1=gw[:], op0=ALU.mult, op1=ALU.mult, accum_out=c1[:]))
            ch.link(dve.tensor_tensor(c0[:], c1[:], tb[:], ALU.add))
            ch.link(dve.tensor_tensor(gw[:], gtmp[:, 0], gw[:], ALU.mult))
            st = Chain(dve, dve_stat, 3 * STAT + 2)

            def stat(i):
                st.start(i)
                for t in range(STAT):
                    st.mark(dve.bn_stats(stats[:, t, :], xe[:, bass.ds((i * STAT + t) * XW, C)]))
                st.sync(dve_passed)
                for t in range(STAT):
                    st.mark(dve.bn_aggr(mv[:, t, :], stats[:, t, :]))
                st.sync()
                for t in range(STAT):
                    st.mark(dve.scalar_tensor_tensor(out=junk[:, t, 0:C], in0=xe[:, bass.ds((i * STAT + t) * XW, C)], scalar=mv[:, t, 0:1],
                                                     in1=gw[:], op0=ALU.subtract, op1=ALU.mult, accum_out=dots[:, t:t + 1]))
                behind = xe[:, bass.ds(i * STAT * XW, STAT * XW)].rearrange("p (t w) -> p t w", w=XW)[:, :, C:XW]
                st.mark(dve.tensor_copy(behind, mv[:]))
                st.sync()
                st.link(dve.tensor_copy(score[:, bass.ds(i * STAT, STAT)], dots[:]))
                st.end()

            for g in range(GROUPS):
                dve.wait_ge(x_loaded[g], 16 * BG)
                stat(g)
            rstd = xe4[:, :, :, C + 1:C + 2].rearrange("p b t o -> p (b t o)")
            ch.link(dve.tensor_scalar(var[:], rstd, EPS, None, ALU.add))
            dve.sem_inc(var_ready, 1)
            dve.wait_ge(sqrt_ready, 1)
            ch.link(dve.reciprocal(rr[:], r0[:]))
            ch.link(dve.tensor_tensor(r0[:], rr[:], rr[:], ALU.mult))
            ch.link(dve.tensor_tensor(r0[:], r0[:], var[:], ALU.mult))
            ch.link(dve.tensor_scalar(r0[:], r0[:], -0.5, 0.5, ALU.mult, ALU.add))
            ch.link(dve.tensor_tensor(r0[:], r0[:], rr[:], ALU.mult))
            ch.link(dve.tensor_tensor(rr[:], r0[:], rr[:], ALU.add))
            ch.link(dve.tensor_copy(rstd, rr[:]))
            ch.link(dve.tensor_tensor(score[:], score[:], rr[:], ALU.mult))
            ch.link(dve.tensor_scalar(score[:], score[:], c0[:, 0:1], None, ALU.add))
            dve.sem_inc(score_ready, 1)
            dve.wait_ge(consts_ready, 1)

            def count(b, s):
                dve.wait_ge(rows_ready, b + 3)
                for t in range(TPP):
                    own, slot = score[:, bass.ds(b * TPP + t, 1)], t + 2 * (s % 2) * TPP
                    dve.tensor_scalar(junk[:, slot, :], bank[s % 2][0:NP, 0:N], own, 0.0, ALU.is_gt, ALU.add,
                                      accum_out=above[:, s, t:t + 1])
                    ins = dve.scalar_tensor_tensor(out=junk[:, TPP + slot, :], in0=bank[s % 2][0:NP, 0:N], scalar=own,
                                                   in1=earlier[:, t, :], op0=ALU.is_equal, op1=ALU.mult,
                                                   accum_out=equal[:, s, t:t + 1])
                ins.then_inc(rows_used, 1)

            def find_place(b, s):
                wait_apart(dve, rows_used, b + 3, dve_passed)
                dve.wait_ge(xout_ready, b + 1)
                dve.scalar_tensor_tensor(out=place[:, s], in0=above[:, s], scalar=row0[:, bass.ds(b, 1)], in1=equal[:, s],
                                         op0=ALU.add, op1=ALU.add).then_inc(place_ready, 1)

            def rank(i, first=False):
                for s in range(X_RING):
                    b = X_RING * i + s
                    count(b, s)
                    if not (first and s == 0):
                        find_place(b - 1, (s - 1) % X_RING)

            rank(0, True)
            with dve.Fori(1, B // X_RING) as i:
                rank(i)
            find_place(B - 1, X_RING - 1)

            dve.wait_ge(prep_ready, 1)
            dve.wait_ge(w_loaded, 16 * W_LOADS)

            def hn_make(b):
                dve.wait_ge(x_in_loaded, 32 * b + 32)
                wait(dve, hnT_psum, b)
                for t in range(3):
                    n = SIZES[t]
                    mean, rstd = x_in[0:n, t, C:C + 1], x_in[0:n, t, C + 1:C + 2]
                    dve.tensor_scalar(hn[0:n, t, 0:CA], x_in[0:n, t, 0:CA], mean, rstd, ALU.subtract, ALU.mult)
                    ins = dve.tensor_scalar(hn[0:n, t, CA:DUP].rearrange("p (a q) -> p a q", a=2),
                                            x_in[0:n, t, CA:C].unsqueeze(1).to_broadcast([n, 2, CB]), mean, rstd, ALU.subtract, ALU.mult)
                ins.then_inc(hn_ready, 1)
                dve.wait_ge(hn_ready, b + 1)
                dve.sem_inc(x_in_used, 1)

            def hnT_lo(b):
                dve.wait_ge(hnT_hi, b + 1)
                dve.tensor_tensor(hnT[:, 1, :], bank[6][:, 0:KEEP], hnT[:, 0, :].bitcast(F32), ALU.subtract)
                dve.tensor_tensor(hnT[CB:CA, 2, :], bank[7][CB:CA, 0:KEEP], hnT[CB:CA, 2, :].bitcast(F32), ALU.subtract).then_inc(hnT_ready, 1)

            def q_lo(b, g):
                dve.wait_ge(qh_hi, b * H + g + 1)
                at = slice(g * KEEP, (g + 1) * KEEP)
                dve.scalar_tensor_tensor(out=qh[:, 1, at], in0=qs[:, 0, :], scalar=wl[:, 0, g:g + 1],
                                         in1=qh[:, 0, at].bitcast(F32), op0=ALU.mult, op1=ALU.subtract).then_inc(qh_lo_a, 1)

            def k_lo(b):
                dve.wait_ge(kT_hi, b + 1)
                for j, n in enumerate((CA, CB)):
                    at = (b & 1) * 4 * KEEP + 2 * j * KEEP
                    ins = dve.scalar_tensor_tensor(out=kT[0:n, bass.ds(at + KEEP, KEEP)], in0=bank[6 + j][0:n, 0:KEEP],
                                                   scalar=bqk[0:n, 2 + j:3 + j], in1=kT[0:n, bass.ds(at, KEEP)].bitcast(F32),
                                                   op0=ALU.add, op1=ALU.subtract)
                ins.then_inc(kT_ready, 1)

            def v_out(b):
                dve.wait_ge(v_psum, b + 1)
                wait(dve, vlo_ready, 2 * b)
                for t in range(3):
                    n = SIZES[t]
                    ins = dve.tensor_tensor(v[0:n, t, :], bank[6 + t // 2][0:n, (t % 2) * C:(t % 2) * C + C], bv[0:n, :], ALU.add)
                ins.then_inc(v_ready, 1)

            def vb_out(b):
                dve.wait_ge(vb_psum, b + 1)
                wait(dve, acc_done, 2 * ((b - 1) * H + 1))
                dve.tensor_tensor(vb[:, 0:1], bank[6][:, 0:1], bw[:, 0:1], ALU.mult)
                dve.tensor_tensor(vb[0:CB, 1:2], bank[6][0:CB, 1:2], bw[0:CB, 1:2], ALU.mult).then_inc(vb_ready, 1)

            def row_max(b, r):
                n = rows_of(r)
                dve.wait_ge(s_psum, b * RT + r + 1)
                dve.tensor_reduce(nmax[0:n, r:r + 1], bank[r % 2][0:n, 0:KEEP], AX.X, ALU.max, negate=True).then_inc(max_done, 1)

            def row_bias(b, r):
                n = rows_of(r)
                dve.wait_ge(max_done, b * RT + r + 1)
                dve.scalar_tensor_tensor(out=nbias[0:n, r:r + 1], in0=nmax[0:n, r:r + 1], scalar=bl[0:n, r:r + 1],
                                         in1=bl[0:n, r:r + 1], op0=ALU.subtract, op1=ALU.add).then_inc(bias_ready, 1)

            def row_recip(b, r):
                n = rows_of(r)
                dve.wait_ge(exp_done, b * RT + r + 1)
                dve.reciprocal(rz[0:n, r:r + 1], zsum[0:n, r:r + 1]).then_inc(rz_ready, 1)

            def p_lo_out(b, r):
                n = rows_of(r)
                at = slice(128 * r, 128 * r + n)
                dve.wait_ge(p_hi_ready, b * RT + r + 1)
                dve.tensor_tensor(p_lo[:, :, at], bank[2 + r % 2][0:TILE, 0:384].rearrange("p (t q) -> p t q", t=3)[:, :, 0:n],
                                  p_hi[:, :, at].bitcast(F32), ALU.subtract).then_inc(p_lo_ready, 1)

            def accumulate(b, h, j):
                if h == 0 and j == 0:
                    wait(dve, proj_psum, b)
                    dve.wait_ge(vb_ready, b + 1)
                dve.wait_ge(u_psum, 2 * (b * H + h) + j + 1)
                if h == 0:
                    ins = dve.tensor_scalar(oT[:, j, :], bank[4 + j][:, 0:KEEP], ww[:, j, h:h + 1], vb[:, j:j + 1], ALU.mult, ALU.add)
                else:
                    dve.wait_ge(acc_done, 2 * (b * H + h) + j - 1)
                    ins = dve.scalar_tensor_tensor(out=oT[:, j, :], in0=bank[4 + j][:, 0:KEEP], scalar=ww[:, j, h:h + 1],
                                                   in1=oT[:, j, :], op0=ALU.mult, op1=ALU.add)
                ins.then_inc(acc_done, 1)

            post_c = Chain(dve, dve_post, 14)
            route_c = Chain(dve, dve_route, 16)
            slot_c = Chain(dve, dve_slot, 9)

            def hres_out(b):
                c = post_c
                c.start(b)
                dve.wait_ge(proj_psum, b + 1)
                dve.wait_ge(x_res_ready, b + 1)
                dve.wait_ge(h_stored, 32 * b + 32)
                for t in range(3):
                    n = SIZES[t]
                    ins = dve.tensor_tensor(hres[0:n, t, :], bank[6 + t // 2][0:n, (t % 2) * C:(t % 2) * C + C], x_res[0:n, t, :], ALU.add)
                ins.then_inc(hres_ready, 1)

            def norm_out(b):
                c = post_c
                dve.wait_ge(hres_ready, b + 1)
                for t in range(3):
                    c.mark(dve.bn_stats(st2[:, t, :], hres[:, t, :]))
                c.sync(dve_passed)
                for t in range(3):
                    c.mark(dve.bn_aggr(mv2[:, t, :], st2[:, t, :]))
                c.sync()
                c.link(dve.tensor_scalar(ve[:], mv2[:, :, 1], EPS, None, ALU.add))
                dve.sem_inc(ve_ready, 1)

            def n2_out(b):
                c = post_c
                dve.wait_ge(pow_ready, b + 1)
                c.link(dve.tensor_tensor(rb[:], ra[:], ra[:], ALU.mult))
                c.link(dve.tensor_tensor(rb[:], rb[:], ve[:], ALU.mult))
                c.link(dve.tensor_scalar(rb[:], rb[:], -0.5, 0.5, ALU.mult, ALU.add))
                c.link(dve.tensor_tensor(rb[:], rb[:], ra[:], ALU.mult))
                c.link(dve.tensor_tensor(rb[:], rb[:], ra[:], ALU.add))

            def n2_write(b):
                c = post_c
                dve.wait_ge(n_stored, 64 * b + 64)
                for t in range(2):
                    c.mark(dve.tensor_scalar(n2[:, t, :], hres[:, t, :], mv2[:, t, 0:1], rb[:, t:t + 1], ALU.subtract, ALU.mult))
                dve.tensor_scalar(n2[:, 2, :], hres[:, 2, :], mv2[:, 2, 0:1], rb[:, 2:3], ALU.subtract, ALU.mult).then_inc(n2_ready, 1)
                c.end()

            def route_out(b):
                c = route_c
                c.start(b)
                dve.wait_ge(router_psum, b + 1)
                dve.tensor_copy(lg[:, 0:2, :], bank[6][0:TILE, 0:2 * E].rearrange("p (t e) -> p t e", t=2))
                c.mark(dve.tensor_copy(lg[0:SIZES[2], 2, :], bank[6][0:SIZES[2], 2 * E:3 * E]))
                c.sync(dve_passed)
                for t in range(3):
                    c.mark(dve.max(mx[:, t, :], lg[:, t, :]))

            def route_rank(b):
                c = route_c
                c.sync(dve_passed)
                for t in range(3):
                    c.mark(dve.max_index(ix[:, t, :], mx[:, t, :], lg[:, t, :]))
                c.link(dve.tensor_tensor(dl[:], mx[:, :, 1], mx[:, :, 0], ALU.subtract))
                dve.sem_inc(dl_ready, 1)
                c.mark(dve.tensor_copy(ixf[:], ix[:, :, 0:2]))

            def route_hot(b):
                c = route_c
                c.sync()
                for k in range(2):
                    c.mark(dve.tensor_tensor(oh[:, k], iota8[:], ixf[:, :, k:k + 1].to_broadcast([TILE, 3, E]), ALU.is_equal))
                c.sync()
                c.link(dve.tensor_tensor(ohs[:], oh[:, 0], oh[:, 1], ALU.add))
                c.link(dve.tensor_tensor(ohs[:], ohs[:], valid[:], ALU.mult))
                dve.sem_inc(oh_ready, 1)

            def route_weights(b):
                c = route_c
                dve.wait_ge(ed_ready, b + 1)
                c.link(dve.tensor_scalar(ed1[:], ed[:], 1.0, None, ALU.add))
                dve.wait_ge(ids_free, b + 1)
                weights = who_out[:].bitcast(F32)
                c.link(dve.reciprocal(weights[:, 0, :, 1], ed1[:]))
                c.link(dve.tensor_tensor(weights[:, 1, :, 1], ed[:], weights[:, 0, :, 1], ALU.mult))
                c.end()

            def slot_out(b):
                c = slot_c
                c.start(b)
                dve.wait_ge(pos_psum, b + 1)
                pre_, tot = bank[7][0:TILE, 0:3 * E].rearrange("p (t e) -> p t e", t=3), bank[7][0:TILE, 3 * E:6 * E]
                for t in range(3):
                    c.mark(dve.tensor_tensor(pos[:, t, :], pre_[:, t, :], run[:], ALU.add))
                    c.link(dve.tensor_tensor(run[:], tot[:, E * t:E * t + E], run[:], ALU.add))
                dve.sem_inc(pos_used, 1)

            def slot_pick(b):
                c = slot_c
                c.link(dve.tensor_tensor(posm[:], oh[:], pos[:].unsqueeze(1).to_broadcast([TILE, 2, 3, E]), ALU.mult))
                c.link(dve.tensor_reduce(slots[:].rearrange("p t k -> p k t"), posm[:], AX.X, ALU.add))
                dve.tensor_copy(slot_u[:], slots[:].rearrange("p t k -> p k t"))
                c.link(dve.tensor_copy(who_out[:, :, :, 0], idc[:].unsqueeze(1).to_broadcast([TILE, 2, 3])))
                dve.tensor_scalar(idc[:], idc[:], float(KEEP), None, ALU.add).then_inc(slots_ready, 1)
                c.end()

            def body(b, prev, this, nxt):
                for r in range(RT):
                    if this:
                        row_max(b, r)
                    for bb, q in lagging(b, r, 1, prev, this):
                        row_recip(bb, q)
                    if this:
                        row_bias(b, r)
                    for bb, q in lagging(b, r, LAG_LO, prev, this):
                        p_lo_out(bb, q)
                    for bb, h, j in lagging_heads(b, r, LAG_ACC, prev, this):
                        accumulate(bb, h, j)
                    if nxt and r == HN:
                        hn_make(b + 1)
                    if nxt and r == HNT + 1:
                        hnT_lo(b + 1)
                    if nxt and r == KK + 1:
                        k_lo(b + 1)
                    for g in range(H):
                        if head_slot(g) + 1 == r and nxt:
                            q_lo(b + 1, g)
                        if head_slot(g) + 1 == RT + r and this and prev:
                            q_lo(b, g)
                    if prev and r == PROJ + 1:
                        hres_out(b - 1)
                    if prev and r == PROJ + 2:
                        norm_out(b - 1)
                    if prev and r == PROJ + 4:
                        n2_out(b - 1)
                    if prev and r == PROJ + 5:
                        n2_write(b - 1)
                    if nxt and r == VV + 1:
                        v_out(b + 1)
                    if nxt and r == VB + 1:
                        vb_out(b + 1)
                    if prev and r == ROUTE + 1:
                        route_out(b - 1)
                    if prev and r == ROUTE + 2:
                        route_rank(b - 1)
                    if prev and r == ROUTE + 4:
                        route_hot(b - 1)
                    if prev and r == ROUTE + 5:
                        route_weights(b - 1)
                    if prev and r == POS + 1:
                        slot_out(b - 1)
                    if prev and r == POS + 2:
                        slot_pick(b - 1)

            dve.wait_ge(bl_loaded, 16 * len(BL_PARTS))
            dve.tensor_scalar(bqk[:, 0:2], bqk[:, 0:2], SCALE, None, ALU.mult).then_inc(bq_ready, 1)
            hn_make(0)
            dve.wait_ge(w_hi_ready, 1)
            for j in range(2):
                for dst, src in w_blocks(j):
                    ins = dve.tensor_tensor(dst(wq[:, 2 * j + 1]), src, dst(wq[:, 2 * j]).bitcast(F32), ALU.subtract)
            ins.then_inc(w_lo_ready, 1)
            hnT_lo(0)
            k_lo(0)
            v_out(0)
            vb_out(0)
            for g in range(H):
                q_lo(0, g)

            batches(dve, body)
            dve.wait_ge(slots_ready, B)
            dve.sem_inc(att_over, 1)
            dve.wait_ge(att_over, 4)
            dve.wait_ge(prep_ready, 2)

            tb_c = Chain(dve, dve_tab, 0)
            L = tb_c.link
            L(dve.tensor_tensor(cnt[:], run[:], base8[:], ALU.subtract))
            L(dve.tensor_scalar(cnti[:], cnt[:], 127.0, None, ALU.add))
            L(dve.tensor_scalar(cnti[:], cnti[:], 7, None, ALU.logical_shift_right))
            L(dve.tensor_copy(cntf[:], cnti[:]))
            L(dve.tensor_scalar(jump[:], cntf[:], -128.0, float(REGION), ALU.mult, ALU.add))
            L(dve.tensor_copy(upto[:, 0:1], cntf[:, 0:1]))
            for e in range(1, E):
                L(dve.tensor_tensor(upto[:, e:e + 1], upto[:, e - 1:e], cntf[:, e:e + 1], ALU.add))
            L(dve.tensor_scalar(te[:], tix[:], upto[0:1, 0:1], None, ALU.is_ge))
            for e in range(1, E - 1):
                L(dve.scalar_tensor_tensor(out=te[:], in0=tix[:], scalar=upto[0:1, e:e + 1], in1=te[:], op0=ALU.is_ge, op1=ALU.add))
            te2 = te[:].rearrange("p (n s) -> p n s", s=2)
            L(dve.scalar_tensor_tensor(out=trio[:], in0=te2[:, :, 1], scalar=8.0, in1=te2[:, :, 0], op0=ALU.mult, op1=ALU.add))
            L(dve.tensor_scalar(trio[:], trio[:], 8.0, None, ALU.mult))
            L(dve.tensor_tensor(trio[:, 1:], trio[:, 1:], te2[:, 0:TILES // 2, 1], ALU.add))
            L(dve.tensor_copy(pair_e[:], trio[:]))
            L(dve.tensor_scalar(ta[:], tix[:], 128.0, None, ALU.mult))
            for e in range(E):
                L(dve.tensor_scalar(ge[:], tix[:], upto[0:1, e:e + 1], None, ALU.is_ge))
                L(dve.scalar_tensor_tensor(out=ta[:], in0=ge[:], scalar=jump[0:1, e:e + 1], in1=ta[:], op0=ALU.mult, op1=ALU.add))
            L(dve.tensor_copy(tile_at[:], ta[:]))
            dve.sem_inc(tab_ready, 1)

            with dve.Fori(0, E) as e:
                for k, w in enumerate((wg, wu)):
                    dve.wait_ge(stage_hi, 2 * e + k + 1)
                    dve.tensor_tensor(w[:, bass.ds(e * F + E * F, F)], stage[:, k, 0, :], w[:, bass.ds(e * F, F)].bitcast(F32), ALU.subtract)
                    last = w[CB:CA, bass.ds(e * F + 2 * E * F, F)]
                    dve.tensor_tensor(last, stage[CB:CA, k, 1, :], last.bitcast(F32), ALU.subtract).then_inc(split_done[k], 1)

            def x_lo_out(i, s):
                dve.wait_ge(x_hi_ready, i + 1)
                dve.tensor_tensor(x_lo[:, s], bank[6][:, 0:256].rearrange("p (j q) -> p j q", j=2), x_hi[:, s].bitcast(F32),
                                  ALU.subtract).then_inc(x_lo_ready, 1)

            def mult(i, s, k):
                dve.wait_ge(silu_done, 2 * i + k + 1)
                wait(dve, hT_psum, i - 1)
                dve.tensor_tensor(hh[:, s, k * HF:(k + 1) * HF], sg[:, k * HF:(k + 1) * HF], bank[2 * k + 1][:, 0:HF], ALU.mult).then_inc(hh_ready, 1)

            def y_out(i, s, n):
                dve.wait_ge(y_psum, i + 1)
                dve.wait_ge(who_loaded[s], 16 * n + 16)
                wait(dve, added, 16 * i - 16)
                dve.tensor_scalar(yo[:, s, :], bank[7][:, 0:C], who_all[:, bass.ds(2 * i + 1, 1)].bitcast(F32), None, ALU.mult).then_inc(y_ready, 1)

            def pair(n, first, last):
                for s in range(2):
                    i = 2 * n + s
                    mult(i, s, 0)
                    mult(i, s, 1)
                    if not (last and s == 1):
                        x_lo_out(i + 1, 1 - s)
                    if not (first and s == 0):
                        y_out(i - 1, 1 - s, n + s - 1)

            x_lo_out(0, 0)
            pair(0, True, False)
            pair(1, False, False)
            with dve.Fori(2, TILES // 2 - 1) as n:
                pair(n, False, False)
            pair(TILES // 2 - 1, False, True)
            y_out(TILES - 1, 1, TILES // 2 - 1)


def kernel(x, L0_tok_gamma, L0_tok_beta, L0_tok_w, L0_tok_b, L0_attn_w_qkv, L0_attn_b_qkv, L0_attn_w_l,
           L0_attn_b_l, L0_attn_w_w, L0_attn_b_w, L0_attn_w_proj, L0_attn_b_proj, L0_ffn_router_w,
           L0_ffn_Wg, L0_ffn_Wu, L0_ffn_Wd):
    import numpy as np
    import concourse.bacc as bacc
    from concourse.bass_utils import run_bass_kernel_spmd

    def up(w):
        return np.ascontiguousarray(np.asarray(w).reshape(E * F, C).T)

    down = np.ascontiguousarray(np.transpose(np.asarray(L0_ffn_Wd).reshape(E, C, F // 128, 128), (3, 0, 2, 1))).reshape(128, -1)
    arrays = {
        "x": x, "gamma": L0_tok_gamma, "beta": L0_tok_beta, "tok_w": L0_tok_w, "tok_b": L0_tok_b,
        "w_qkv": L0_attn_w_qkv, "b_qkv": L0_attn_b_qkv, "w_l": L0_attn_w_l, "b_l": L0_attn_b_l,
        "w_w": L0_attn_w_w, "b_w": L0_attn_b_w, "w_proj": L0_attn_w_proj, "b_proj": L0_attn_b_proj,
        "router_wT": np.ascontiguousarray(np.asarray(L0_ffn_router_w).T),
        "WgT": up(L0_ffn_Wg), "WuT": up(L0_ffn_Wu), "WdT": down,
    }
    arrays = {name: np.ascontiguousarray(a) for name, a in arrays.items()}
    nc = bacc.Bacc("TRN2", target_bir_lowering=False, num_devices=1)
    ins = [nc.dram_tensor(name, a.shape, mybir.dt.from_np(a.dtype), kind="ExternalInput").ap() for name, a in arrays.items()]
    out = nc.dram_tensor("out", (T + 128, C), F32, kind="ExternalOutput").ap()
    xs = nc.dram_tensor("xs", (B * N, XW), F32, kind="Internal").ap()
    who = nc.dram_tensor("who", (SLOTS, 2), U32, kind="Internal").ap()
    n_rows = nc.dram_tensor("n_rows", (T + 128, DUP), F32, kind="Internal").ap()
    build(nc, *ins, out, xs, who, n_rows)
    r = run_bass_kernel_spmd(nc, [arrays], core_ids=[0])
    return r.results[0]["out"][:T].reshape(B, KEEP, C)
```
